# Optimizing a Trainium2 kernel written in Bass

```python
import numpy as np
import jax
import jax.numpy as jnp

def _softmax(x, axis=-1):
    return jax.nn.softmax(x, axis=axis)

def _gelu(x):
    return jax.nn.gelu(x, approximate=True)

def _silu(x):
    return jax.nn.silu(x)

def _sigmoid(x):
    return jax.nn.sigmoid(x)

def _layernorm(x, axis=-1, eps=1e-05):
    m = jnp.mean(x, axis=axis, keepdims=True)
    v = jnp.var(x, axis=axis, keepdims=True)
    return (x - m) / jnp.sqrt(v + eps)

def _scatter_add(tgt, idx, src, axis=0):
    return tgt.at[idx].add(src)

def _segment_sum(src, seg, n):
    return jax.ops.segment_sum(src, seg, n)
kernel_name = 'mk_hybrid_d2_jaxref_r8_c81c25'

def setup_inputs(seed: int=0):
    np.random.seed(seed)
    _w = jnp.asarray

    def _L0_attn_a_setup():
        import jax, jax.numpy as jnp
        import numpy as np
        H, D, CR, SEL_K = (8, 64, 32, 16)
        ROPE_DIM, THETA, WINDOW, GROUPS = (32, 10000.0, 64, 2)
        INTER, HID, QC = (64, 128, 32)
        NEG = -1e+30

        def _rope_cache(t):
            half = ROPE_DIM // 2
            inv = 1.0 / THETA ** (jnp.arange(half, dtype=jnp.float32) * 2.0 / ROPE_DIM)
            ang = jnp.arange(t, dtype=jnp.float32)[:, None] * inv[None, :]
            return (jnp.cos(ang), jnp.sin(ang))

        def _apply_partial_rope(x, cos, sin):
            half = ROPE_DIM // 2
            x1, x2, rest = (x[..., :half], x[..., half:ROPE_DIM], x[..., ROPE_DIM:])
            return jnp.concatenate([x1 * cos - x2 * sin, x1 * sin + x2 * cos, rest], -1)

        def _rmsnorm(x, g, eps=1e-06):
            return x * jax.lax.rsqrt(jnp.mean(x * x, -1, keepdims=True) + eps) * g
        key = jax.random.key(seed)
        ks = jax.random.split(key, 9)
        f = lambda k, shp, s: jax.random.normal(k, shp, jnp.float32) * s
        return {'h': f(ks[0], (1, 256, HID), 1.0), 'w_qc': f(ks[1], (HID, QC), QC ** (-0.5)), 'w_qup': f(ks[2], (QC, H * D), (H * D) ** (-0.5)), 'w_k': f(ks[3], (HID, D), HID ** (-0.5)), 'w_v': f(ks[4], (HID, D), HID ** (-0.5)), 'g_qnorm': jnp.ones((D,), jnp.float32), 'g_knorm': jnp.ones((D,), jnp.float32), 'w_gate': f(ks[5], (D, 3), 0.05), 'b_gate': jnp.zeros((3,), jnp.float32), 'sink_logit': f(ks[6], (H,), 0.1), 'w_out_group': f(ks[7], (GROUPS, H // GROUPS * D, INTER), 0.05), 'w_out': f(ks[8], (GROUPS * INTER, HID), 0.03)}
    _L0_attn_a_in = _L0_attn_a_setup()

    def _L0_attn_b_setup():
        import jax, jax.numpy as jnp
        import numpy as np
        B, L, D, H, F = (2, 128, 128, 16, 512)
        DH = D // H
        EPS = 1e-06

        def _layernorm(x, g, b, eps=1e-05):
            m = jnp.mean(x, axis=-1, keepdims=True)
            v = jnp.mean((x - m) ** 2, axis=-1, keepdims=True)
            return (x - m) / jnp.sqrt(v + eps) * g + b

        def _decoder_layer(inputs, Wq, bq, Wk, bk, Wv, bv, Wo, bo, ln1_g, ln1_b, W1, b1, W2, b2, ln2_g, ln2_b):
            Bn, Ln, Dn = inputs.shape

            def heads(W, b):
                return (inputs @ W + b).reshape(Bn, Ln, H, DH).transpose(0, 2, 1, 3)
            q = jax.nn.sigmoid(heads(Wq, bq))
            k = jax.nn.sigmoid(heads(Wk, bk))
            v = heads(Wv, bv)
            normal = (jnp.arange(Ln, dtype=jnp.float32) + 1.0)[None, None, :]
            sink_in = normal / jnp.einsum('bhld,bhld->bhl', q + EPS, jnp.cumsum(k, axis=2) + EPS)
            src_out = normal / jnp.einsum('bhld,bhld->bhl', k + EPS, jnp.cumsum(q, axis=2) + EPS)
            cons_sink = jnp.einsum('bhld,bhld->bhl', q + EPS, jnp.cumsum(k * src_out[..., None], axis=2) + EPS) / normal
            cons_src = jnp.einsum('bhld,bhld->bhl', k + EPS, jnp.cumsum(q * sink_in[..., None], axis=2) + EPS) / normal
            cons_src = jnp.clip(cons_src, -1.0, 1.0)
            sink_alloc = jax.nn.sigmoid(cons_sink)
            cons_src = jnp.exp(cons_src)
            src_comp = cons_src / jnp.cumsum(cons_src, axis=-1) * normal
            qs = q * (sink_in / normal)[..., None]
            vs = v * src_comp[..., None]
            kv = jnp.cumsum(jnp.einsum('bhld,bhlm->bhldm', k, vs), axis=2)
            x = jnp.einsum('bhld,bhldm->bhlm', qs, kv) * sink_alloc[..., None]
            x = x.transpose(0, 2, 1, 3).reshape(Bn, Ln, Dn)
            attn = x @ Wo + bo
            h = _layernorm(inputs + attn, ln1_g, ln1_b)
            ffn = jax.nn.gelu(h @ W1 + b1, approximate=False) @ W2 + b2
            return _layernorm(h + ffn, ln2_g, ln2_b)
        key = jax.random.key(seed)
        ks = jax.random.split(key, 12)

        def w(k, shape):
            return jax.random.normal(k, shape, dtype=jnp.float32) * 0.02
        return {'inputs': jax.random.normal(ks[0], (B, L, D), dtype=jnp.float32), 'attn_mask': jnp.zeros((L, L), dtype=jnp.bool_), 'Wq': w(ks[1], (D, D)), 'bq': jnp.zeros((D,), jnp.float32), 'Wk': w(ks[2], (D, D)), 'bk': jnp.zeros((D,), jnp.float32), 'Wv': w(ks[3], (D, D)), 'bv': jnp.zeros((D,), jnp.float32), 'Wo': w(ks[4], (D, D)), 'bo': jnp.zeros((D,), jnp.float32), 'ln1_g': jnp.ones((D,), jnp.float32), 'ln1_b': jnp.zeros((D,), jnp.float32), 'W1': w(ks[5], (D, F)), 'b1': jnp.zeros((F,), jnp.float32), 'W2': w(ks[6], (F, D)), 'b2': jnp.zeros((D,), jnp.float32), 'ln2_g': jnp.ones((D,), jnp.float32), 'ln2_b': jnp.zeros((D,), jnp.float32)}
    _L0_attn_b_in = _L0_attn_b_setup()

    def _L0_ffn_setup():
        import jax, jax.numpy as jnp
        import numpy as np
        TOP_K = 2
        CAPACITY_FACTOR = 1.25

        def _moe_forward(x, gate_w, wi_gate, wi_up, wo):
            B, S, D = x.shape
            E = wi_gate.shape[0]
            N = B * S
            capacity = max(int(N / E * CAPACITY_FACTOR), 1)
            x_flat = x.reshape(N, D)
            router_logits = x_flat @ gate_w.T
            router_probs = jax.nn.softmax(router_logits, axis=-1)
            top_k_probs, top_k_idx = jax.lax.top_k(router_probs, TOP_K)
            top_k_probs = top_k_probs / jnp.sum(top_k_probs, axis=-1, keepdims=True)
            out = jnp.zeros_like(x_flat)
            experts = jnp.arange(E, dtype=jnp.int32)
            for k in range(TOP_K):
                eid = top_k_idx[:, k]
                ew = top_k_probs[:, k]
                onehot = (eid[:, None] == experts[None, :]).astype(jnp.int32)
                pos_all = jnp.cumsum(onehot, axis=0) - 1
                pos = jnp.take_along_axis(pos_all, eid[:, None].astype(jnp.int32), axis=1)[:, 0]
                valid = pos < capacity
                pos_c = jnp.where(valid, pos, 0)
                disp = jnp.zeros((E, capacity, D), x_flat.dtype).at[eid, pos_c].add(jnp.where(valid[:, None], x_flat, 0.0))
                gate = jax.nn.silu(jnp.einsum('ecd,efd->ecf', disp, wi_gate))
                up = jnp.einsum('ecd,efd->ecf', disp, wi_up)
                expert_out = jnp.einsum('ecf,edf->ecd', gate * up, wo)
                tok_out = expert_out[eid, pos_c]
                out = out + jnp.where(valid[:, None], ew[:, None] * tok_out, 0.0)
            return out.reshape(B, S, D)
        key = jax.random.key(seed)
        k1, k2, k3, k4, k5 = jax.random.split(key, 5)
        B, S, D, F, E = (4, 256, 128, 512, 8)
        return {'x': jax.random.normal(k1, (B, S, D), dtype=jnp.float32), 'gate_w': jax.random.normal(k2, (E, D), dtype=jnp.float32) * 0.02, 'wi_gate': jax.random.normal(k3, (E, F, D), dtype=jnp.float32) * 0.02, 'wi_up': jax.random.normal(k4, (E, F, D), dtype=jnp.float32) * 0.02, 'wo': jax.random.normal(k5, (E, D, F), dtype=jnp.float32) * 0.02}
    _L0_ffn_in = _L0_ffn_setup()

    def _L1_attn_a_setup():
        import jax, jax.numpy as jnp
        import numpy as np
        from jax import lax
        SHIFT = 1
        GAMMA = 0.25

        def q_shift_1d(x, shift=SHIFT, gamma=GAMMA):
            B, T, C = x.shape
            c1 = int(C * gamma)
            c2 = int(C * gamma * 2)
            fwd = jnp.pad(x[:, :T - shift, :c1], ((0, 0), (shift, 0), (0, 0)))
            bwd = jnp.pad(x[:, shift:, c1:c2], ((0, 0), (0, shift), (0, 0)))
            return jnp.concatenate([fwd, bwd, x[:, :, c2:]], axis=-1)

        def wkv_scan(w, u, k, v):
            B, T, C = k.shape
            ew = jnp.exp(w)

            def step(carry, kv):
                a, b = carry
                kt, vt = kv
                eku = jnp.exp(u + kt)
                out = (a + eku * vt) / (b + eku)
                ek = jnp.exp(kt)
                return ((a * ew + ek * vt, b * ew + ek), out)
            k_t = jnp.moveaxis(k, 1, 0)
            v_t = jnp.moveaxis(v, 1, 0)
            init = (jnp.zeros((B, C), k.dtype), jnp.zeros((B, C), k.dtype))
            _, ys = lax.scan(step, init, (k_t, v_t))
            return jnp.moveaxis(ys, 0, 1)
        key = jax.random.key(seed)
        ks = jax.random.split(key, 10)
        B, T, C = (8, 512, 128)
        s = 1.0 / np.sqrt(C)
        return {'x': jax.random.normal(ks[0], (B, T, C), jnp.float32), 'Wk': jax.random.normal(ks[1], (C, C), jnp.float32) * s, 'Wv': jax.random.normal(ks[2], (C, C), jnp.float32) * s, 'Wr': jax.random.normal(ks[3], (C, C), jnp.float32) * s, 'Wo': jax.random.normal(ks[4], (C, C), jnp.float32) * s, 'spatial_decay': jax.random.normal(ks[5], (C,), jnp.float32), 'spatial_first': jax.random.normal(ks[6], (C,), jnp.float32), 'mix_k': jax.random.uniform(ks[7], (C,), jnp.float32), 'mix_v': jax.random.uniform(ks[8], (C,), jnp.float32), 'mix_r': jax.random.uniform(ks[9], (C,), jnp.float32)}
    _L1_attn_a_in = _L1_attn_a_setup()

    def _L1_attn_b_setup():
        import jax, jax.numpy as jnp
        import numpy as np
        NUM_HEADS = 16
        HIDDEN = 128
        HEAD_DIM = HIDDEN // NUM_HEADS
        GROUP_SIZE = 32

        def _attention(q, k, v, head_dim):
            scores = jnp.einsum('bghqd,bghkd->bghqk', q, k) / head_dim ** 0.5
            w = jax.nn.softmax(scores, axis=-1)
            return jnp.einsum('bghqk,bghkd->bghqd', w, v)
        key = jax.random.key(seed)
        k1, k2, k3 = jax.random.split(key, 3)
        hidden_states = jax.random.normal(k1, (2, 1024, HIDDEN), dtype=jnp.float32)
        w_qkv = jax.random.normal(k2, (3 * HIDDEN, HIDDEN), dtype=jnp.float32) * 0.02
        b_qkv = jax.random.normal(k3, (3 * HIDDEN,), dtype=jnp.float32) * 0.02
        return {'hidden_states': hidden_states, 'w_qkv': w_qkv, 'b_qkv': b_qkv}
    _L1_attn_b_in = _L1_attn_b_setup()

    def _L1_ffn_setup():
        import jax, jax.numpy as jnp
        import numpy as np
        B, S, D, H, F = (4, 512, 128, 16, 512)
        CAP = 0.125
        ROPE_BASE = 10000.0

        def rmsnorm(x, g):
            return x * jax.lax.rsqrt(jnp.mean(x * x, -1, keepdims=True) + 1e-06) * g

        def rope(t, pos):
            hd = t.shape[-1]
            inv = 1.0 / ROPE_BASE ** (jnp.arange(0, hd, 2, dtype=jnp.float32) / hd)
            f = pos[:, None, :, None].astype(jnp.float32) * inv
            emb = jnp.concatenate([f, f], axis=-1)
            cos, sin = (jnp.cos(emb), jnp.sin(emb))
            rot = jnp.concatenate([-t[..., hd // 2:], t[..., :hd // 2]], axis=-1)
            return t * cos + rot * sin
        key = jax.random.key(seed)
        ks = jax.random.split(key, 9)
        scale = 0.02
        x = jax.random.normal(ks[0], (B, S, D), jnp.float32)
        causal = jnp.where(jnp.tril(jnp.ones((S, S), bool)), 0.0, -1000000000.0).astype(jnp.float32)
        attention_mask = jnp.broadcast_to(causal[None, None], (B, 1, S, S))
        position_ids = jnp.broadcast_to(jnp.arange(S, dtype=jnp.int32), (B, S))
        return {'x': x, 'attention_mask': attention_mask, 'position_ids': position_ids, 'router_w': jax.random.normal(ks[1], (D, 1), jnp.float32) * scale, 'router_b': jnp.zeros((1,), jnp.float32), 'wq': jax.random.normal(ks[2], (D, D), jnp.float32) * scale, 'wk': jax.random.normal(ks[3], (D, D), jnp.float32) * scale, 'wv': jax.random.normal(ks[4], (D, D), jnp.float32) * scale, 'wo': jax.random.normal(ks[5], (D, D), jnp.float32) * scale, 'w1': jax.random.normal(ks[6], (D, F), jnp.float32) * scale, 'w2': jax.random.normal(ks[7], (F, D), jnp.float32) * scale, 'ln1': jnp.ones((D,), jnp.float32), 'ln2': jnp.ones((D,), jnp.float32)}
    _L1_ffn_in = _L1_ffn_setup()
    _d = {'L0_attn_a_h': _L0_attn_a_in['h'], 'L0_attn_a_w_qc': _L0_attn_a_in['w_qc'], 'L0_attn_a_w_qup': _L0_attn_a_in['w_qup'], 'L0_attn_a_w_k': _L0_attn_a_in['w_k'], 'L0_attn_a_w_v': _L0_attn_a_in['w_v'], 'L0_attn_a_g_qnorm': _L0_attn_a_in['g_qnorm'], 'L0_attn_a_g_knorm': _L0_attn_a_in['g_knorm'], 'L0_attn_a_w_gate': _L0_attn_a_in['w_gate'], 'L0_attn_a_b_gate': _L0_attn_a_in['b_gate'], 'L0_attn_a_sink_logit': _L0_attn_a_in['sink_logit'], 'L0_attn_a_w_out_group': _L0_attn_a_in['w_out_group'], 'L0_attn_a_w_out': _L0_attn_a_in['w_out'], 'L0_attn_b_attn_mask': _L0_attn_b_in['attn_mask'], 'L0_attn_b_Wq': _L0_attn_b_in['Wq'], 'L0_attn_b_bq': _L0_attn_b_in['bq'], 'L0_attn_b_Wk': _L0_attn_b_in['Wk'], 'L0_attn_b_bk': _L0_attn_b_in['bk'], 'L0_attn_b_Wv': _L0_attn_b_in['Wv'], 'L0_attn_b_bv': _L0_attn_b_in['bv'], 'L0_attn_b_Wo': _L0_attn_b_in['Wo'], 'L0_attn_b_bo': _L0_attn_b_in['bo'], 'L0_attn_b_ln1_g': _L0_attn_b_in['ln1_g'], 'L0_attn_b_ln1_b': _L0_attn_b_in['ln1_b'], 'L0_attn_b_W1': _L0_attn_b_in['W1'], 'L0_attn_b_b1': _L0_attn_b_in['b1'], 'L0_attn_b_W2': _L0_attn_b_in['W2'], 'L0_attn_b_b2': _L0_attn_b_in['b2'], 'L0_attn_b_ln2_g': _L0_attn_b_in['ln2_g'], 'L0_attn_b_ln2_b': _L0_attn_b_in['ln2_b'], 'L0_ffn_gate_w': _L0_ffn_in['gate_w'], 'L0_ffn_wi_gate': _L0_ffn_in['wi_gate'], 'L0_ffn_wi_up': _L0_ffn_in['wi_up'], 'L0_ffn_wo': _L0_ffn_in['wo'], 'L1_attn_a_Wk': _L1_attn_a_in['Wk'], 'L1_attn_a_Wv': _L1_attn_a_in['Wv'], 'L1_attn_a_Wr': _L1_attn_a_in['Wr'], 'L1_attn_a_Wo': _L1_attn_a_in['Wo'], 'L1_attn_a_spatial_decay': _L1_attn_a_in['spatial_decay'], 'L1_attn_a_spatial_first': _L1_attn_a_in['spatial_first'], 'L1_attn_a_mix_k': _L1_attn_a_in['mix_k'], 'L1_attn_a_mix_v': _L1_attn_a_in['mix_v'], 'L1_attn_a_mix_r': _L1_attn_a_in['mix_r'], 'L1_attn_b_w_qkv': _L1_attn_b_in['w_qkv'], 'L1_attn_b_b_qkv': _L1_attn_b_in['b_qkv'], 'L1_ffn_attention_mask': _L1_ffn_in['attention_mask'], 'L1_ffn_position_ids': _L1_ffn_in['position_ids'], 'L1_ffn_router_w': _L1_ffn_in['router_w'], 'L1_ffn_router_b': _L1_ffn_in['router_b'], 'L1_ffn_wq': _L1_ffn_in['wq'], 'L1_ffn_wk': _L1_ffn_in['wk'], 'L1_ffn_wv': _L1_ffn_in['wv'], 'L1_ffn_wo': _L1_ffn_in['wo'], 'L1_ffn_w1': _L1_ffn_in['w1'], 'L1_ffn_w2': _L1_ffn_in['w2'], 'L1_ffn_ln1': _L1_ffn_in['ln1'], 'L1_ffn_ln2': _L1_ffn_in['ln2']}
    _x0 = _d['L0_attn_a_h']
    _d['L0_attn_a_h'] = jax.random.normal(jax.random.fold_in(jax.random.key(seed), 1), (4, 512, 128), dtype=_x0.dtype)
    del _x0
    return _d

def reference(L0_attn_a_h, L0_attn_a_w_qc, L0_attn_a_w_qup, L0_attn_a_w_k, L0_attn_a_w_v, L0_attn_a_g_qnorm, L0_attn_a_g_knorm, L0_attn_a_w_gate, L0_attn_a_b_gate, L0_attn_a_sink_logit, L0_attn_a_w_out_group, L0_attn_a_w_out, L0_attn_b_attn_mask, L0_attn_b_Wq, L0_attn_b_bq, L0_attn_b_Wk, L0_attn_b_bk, L0_attn_b_Wv, L0_attn_b_bv, L0_attn_b_Wo, L0_attn_b_bo, L0_attn_b_ln1_g, L0_attn_b_ln1_b, L0_attn_b_W1, L0_attn_b_b1, L0_attn_b_W2, L0_attn_b_b2, L0_attn_b_ln2_g, L0_attn_b_ln2_b, L0_ffn_gate_w, L0_ffn_wi_gate, L0_ffn_wi_up, L0_ffn_wo, L1_attn_a_Wk, L1_attn_a_Wv, L1_attn_a_Wr, L1_attn_a_Wo, L1_attn_a_spatial_decay, L1_attn_a_spatial_first, L1_attn_a_mix_k, L1_attn_a_mix_v, L1_attn_a_mix_r, L1_attn_b_w_qkv, L1_attn_b_b_qkv, L1_ffn_attention_mask, L1_ffn_position_ids, L1_ffn_router_w, L1_ffn_router_b, L1_ffn_wq, L1_ffn_wk, L1_ffn_wv, L1_ffn_wo, L1_ffn_w1, L1_ffn_w2, L1_ffn_ln1, L1_ffn_ln2):

    def _L0_attn_a_ref(h, w_qc, w_qup, w_k, w_v, g_qnorm, g_knorm, w_gate, b_gate, sink_logit, w_out_group, w_out):
        import jax, jax.numpy as jnp
        import numpy as np
        H, D, CR, SEL_K = (8, 64, 32, 16)
        ROPE_DIM, THETA, WINDOW, GROUPS = (32, 10000.0, 64, 2)
        INTER, HID, QC = (64, 128, 32)
        NEG = -1e+30

        def _rope_cache(t):
            half = ROPE_DIM // 2
            inv = 1.0 / THETA ** (jnp.arange(half, dtype=jnp.float32) * 2.0 / ROPE_DIM)
            ang = jnp.arange(t, dtype=jnp.float32)[:, None] * inv[None, :]
            return (jnp.cos(ang), jnp.sin(ang))

        def _apply_partial_rope(x, cos, sin):
            half = ROPE_DIM // 2
            x1, x2, rest = (x[..., :half], x[..., half:ROPE_DIM], x[..., ROPE_DIM:])
            return jnp.concatenate([x1 * cos - x2 * sin, x1 * sin + x2 * cos, rest], -1)

        def _rmsnorm(x, g, eps=1e-06):
            return x * jax.lax.rsqrt(jnp.mean(x * x, -1, keepdims=True) + eps) * g
        b, t, _ = h.shape
        cos, sin = _rope_cache(t)
        q = (h @ w_qc @ w_qup).reshape(b, t, H, D).transpose(0, 2, 1, 3)
        q = _rmsnorm(_apply_partial_rope(q, cos, sin), g_qnorm)
        k = _rmsnorm(_apply_partial_rope(h @ w_k, cos, sin), g_knorm)
        v = h @ w_v
        scale = 1.0 / np.sqrt(D).astype(np.float32)
        qpos = jnp.arange(t)
        sink = jnp.broadcast_to(sink_logit[None, :, None, None], (b, H, t, 1))
        nb = t // CR
        kc = k[:, :nb * CR].reshape(b, nb, CR, D).mean(2)
        vc = v[:, :nb * CR].reshape(b, nb, CR, D).mean(2)
        comp_valid = ((jnp.arange(nb) + 1) * CR - 1)[None, :] <= qpos[:, None]
        any_blk = comp_valid.any(-1, keepdims=True)
        safe = jnp.where(any_blk, comp_valid, True)
        sc_raw = jnp.einsum('bhqd,bnd->bhqn', q, kc) * scale
        pc = jax.nn.softmax(jnp.concatenate([jnp.where(safe, sc_raw, NEG), sink], -1), -1)
        comp_out = jnp.einsum('bhqn,bnd->bhqd', pc[..., :nb], vc)
        comp_out = jnp.where(any_blk[None, None], comp_out, 0.0)
        sel_sc = jnp.where(comp_valid, sc_raw, -jnp.inf)
        top_idx = jax.lax.top_k(sel_sc, min(SEL_K, nb))[1]
        sel_blocks = (top_idx[..., :, None] == jnp.arange(nb)).any(-2)
        block_of = jnp.minimum(qpos // CR, nb - 1)
        causal = qpos[:, None] >= qpos[None, :]
        in_range = qpos < nb * CR
        tok_sel = sel_blocks[..., block_of] & (causal & in_range[None, :])[None, None]
        scores_full = jnp.einsum('bhqd,bkd->bhqk', q, k) * scale
        ps = jax.nn.softmax(jnp.where(tok_sel, scores_full, NEG), -1)
        sel_out = jnp.einsum('bhqk,bkd->bhqd', ps, v)
        sw = causal & (qpos[:, None] - qpos[None, :] < WINDOW)
        pw = jax.nn.softmax(jnp.concatenate([jnp.where(sw[None, None], scores_full, NEG), sink], -1), -1)
        sw_out = jnp.einsum('bhqk,bkd->bhqd', pw[..., :t], v)
        g = jax.nn.sigmoid(q @ w_gate + b_gate)
        g = g / jnp.clip(g.sum(-1, keepdims=True), 1e-06)
        mixed = g[..., 0:1] * comp_out + g[..., 1:2] * sel_out + g[..., 2:3] * sw_out
        x = mixed.transpose(0, 2, 1, 3).reshape(b, t, GROUPS, H // GROUPS * D)
        y = jnp.einsum('btgf,gfi->btgi', x, w_out_group).reshape(b, t, GROUPS * INTER)
        return y @ w_out

    def _L0_attn_b_ref(inputs, attn_mask, Wq, bq, Wk, bk, Wv, bv, Wo, bo, ln1_g, ln1_b, W1, b1, W2, b2, ln2_g, ln2_b):
        import jax, jax.numpy as jnp
        import numpy as np
        B, L, D, H, F = (2, 128, 128, 16, 512)
        DH = D // H
        EPS = 1e-06

        def _layernorm(x, g, b, eps=1e-05):
            m = jnp.mean(x, axis=-1, keepdims=True)
            v = jnp.mean((x - m) ** 2, axis=-1, keepdims=True)
            return (x - m) / jnp.sqrt(v + eps) * g + b

        def _decoder_layer(inputs, Wq, bq, Wk, bk, Wv, bv, Wo, bo, ln1_g, ln1_b, W1, b1, W2, b2, ln2_g, ln2_b):
            Bn, Ln, Dn = inputs.shape

            def heads(W, b):
                return (inputs @ W + b).reshape(Bn, Ln, H, DH).transpose(0, 2, 1, 3)
            q = jax.nn.sigmoid(heads(Wq, bq))
            k = jax.nn.sigmoid(heads(Wk, bk))
            v = heads(Wv, bv)
            normal = (jnp.arange(Ln, dtype=jnp.float32) + 1.0)[None, None, :]
            sink_in = normal / jnp.einsum('bhld,bhld->bhl', q + EPS, jnp.cumsum(k, axis=2) + EPS)
            src_out = normal / jnp.einsum('bhld,bhld->bhl', k + EPS, jnp.cumsum(q, axis=2) + EPS)
            cons_sink = jnp.einsum('bhld,bhld->bhl', q + EPS, jnp.cumsum(k * src_out[..., None], axis=2) + EPS) / normal
            cons_src = jnp.einsum('bhld,bhld->bhl', k + EPS, jnp.cumsum(q * sink_in[..., None], axis=2) + EPS) / normal
            cons_src = jnp.clip(cons_src, -1.0, 1.0)
            sink_alloc = jax.nn.sigmoid(cons_sink)
            cons_src = jnp.exp(cons_src)
            src_comp = cons_src / jnp.cumsum(cons_src, axis=-1) * normal
            qs = q * (sink_in / normal)[..., None]
            vs = v * src_comp[..., None]
            kv = jnp.cumsum(jnp.einsum('bhld,bhlm->bhldm', k, vs), axis=2)
            x = jnp.einsum('bhld,bhldm->bhlm', qs, kv) * sink_alloc[..., None]
            x = x.transpose(0, 2, 1, 3).reshape(Bn, Ln, Dn)
            attn = x @ Wo + bo
            h = _layernorm(inputs + attn, ln1_g, ln1_b)
            ffn = jax.nn.gelu(h @ W1 + b1, approximate=False) @ W2 + b2
            return _layernorm(h + ffn, ln2_g, ln2_b)
        return _decoder_layer(inputs, Wq, bq, Wk, bk, Wv, bv, Wo, bo, ln1_g, ln1_b, W1, b1, W2, b2, ln2_g, ln2_b)

    def _L0_ffn_ref(x, gate_w, wi_gate, wi_up, wo):
        import jax, jax.numpy as jnp
        import numpy as np
        TOP_K = 2
        CAPACITY_FACTOR = 1.25

        def _moe_forward(x, gate_w, wi_gate, wi_up, wo):
            B, S, D = x.shape
            E = wi_gate.shape[0]
            N = B * S
            capacity = max(int(N / E * CAPACITY_FACTOR), 1)
            x_flat = x.reshape(N, D)
            router_logits = x_flat @ gate_w.T
            router_probs = jax.nn.softmax(router_logits, axis=-1)
            top_k_probs, top_k_idx = jax.lax.top_k(router_probs, TOP_K)
            top_k_probs = top_k_probs / jnp.sum(top_k_probs, axis=-1, keepdims=True)
            out = jnp.zeros_like(x_flat)
            experts = jnp.arange(E, dtype=jnp.int32)
            for k in range(TOP_K):
                eid = top_k_idx[:, k]
                ew = top_k_probs[:, k]
                onehot = (eid[:, None] == experts[None, :]).astype(jnp.int32)
                pos_all = jnp.cumsum(onehot, axis=0) - 1
                pos = jnp.take_along_axis(pos_all, eid[:, None].astype(jnp.int32), axis=1)[:, 0]
                valid = pos < capacity
                pos_c = jnp.where(valid, pos, 0)
                disp = jnp.zeros((E, capacity, D), x_flat.dtype).at[eid, pos_c].add(jnp.where(valid[:, None], x_flat, 0.0))
                gate = jax.nn.silu(jnp.einsum('ecd,efd->ecf', disp, wi_gate))
                up = jnp.einsum('ecd,efd->ecf', disp, wi_up)
                expert_out = jnp.einsum('ecf,edf->ecd', gate * up, wo)
                tok_out = expert_out[eid, pos_c]
                out = out + jnp.where(valid[:, None], ew[:, None] * tok_out, 0.0)
            return out.reshape(B, S, D)
        return _moe_forward(x, gate_w, wi_gate, wi_up, wo)

    def _L1_attn_a_ref(x, Wk, Wv, Wr, Wo, spatial_decay, spatial_first, mix_k, mix_v, mix_r):
        import jax, jax.numpy as jnp
        import numpy as np
        from jax import lax
        SHIFT = 1
        GAMMA = 0.25

        def q_shift_1d(x, shift=SHIFT, gamma=GAMMA):
            B, T, C = x.shape
            c1 = int(C * gamma)
            c2 = int(C * gamma * 2)
            fwd = jnp.pad(x[:, :T - shift, :c1], ((0, 0), (shift, 0), (0, 0)))
            bwd = jnp.pad(x[:, shift:, c1:c2], ((0, 0), (0, shift), (0, 0)))
            return jnp.concatenate([fwd, bwd, x[:, :, c2:]], axis=-1)

        def wkv_scan(w, u, k, v):
            B, T, C = k.shape
            ew = jnp.exp(w)

            def step(carry, kv):
                a, b = carry
                kt, vt = kv
                eku = jnp.exp(u + kt)
                out = (a + eku * vt) / (b + eku)
                ek = jnp.exp(kt)
                return ((a * ew + ek * vt, b * ew + ek), out)
            k_t = jnp.moveaxis(k, 1, 0)
            v_t = jnp.moveaxis(v, 1, 0)
            init = (jnp.zeros((B, C), k.dtype), jnp.zeros((B, C), k.dtype))
            _, ys = lax.scan(step, init, (k_t, v_t))
            return jnp.moveaxis(ys, 0, 1)
        B, T, C = x.shape
        xx = q_shift_1d(x)
        xk = x * mix_k + xx * (1.0 - mix_k)
        xv = x * mix_v + xx * (1.0 - mix_v)
        xr = x * mix_r + xx * (1.0 - mix_r)
        k = jnp.einsum('btc,oc->bto', xk, Wk)
        v = jnp.einsum('btc,oc->bto', xv, Wv)
        r = jnp.einsum('btc,oc->bto', xr, Wr)
        sr = jax.nn.sigmoid(r)
        wkv_out = wkv_scan(spatial_decay / T, spatial_first / T, k, v)
        return jnp.einsum('btc,oc->bto', sr * wkv_out, Wo)

    def _L1_attn_b_ref(hidden_states, w_qkv, b_qkv):
        import jax, jax.numpy as jnp
        import numpy as np
        NUM_HEADS = 16
        HIDDEN = 128
        HEAD_DIM = HIDDEN // NUM_HEADS
        GROUP_SIZE = 32

        def _attention(q, k, v, head_dim):
            scores = jnp.einsum('bghqd,bghkd->bghqk', q, k) / head_dim ** 0.5
            w = jax.nn.softmax(scores, axis=-1)
            return jnp.einsum('bghqk,bghkd->bghqd', w, v)
        b, n, _ = hidden_states.shape
        h, d, G = (NUM_HEADS, HEAD_DIM, GROUP_SIZE)
        ng = n // G
        half = G // 2
        qkv = hidden_states @ w_qkv.T + b_qkv
        qkv = qkv.reshape(b, n, 3, h, d).transpose(2, 0, 3, 1, 4)
        q, k, v = (qkv[0], qkv[1], qkv[2])

        def grp(x):
            return x.reshape(b, h, ng, G, d).transpose(0, 2, 1, 3, 4)
        q, k, v = (grp(q), grp(k), grp(v))
        q1, q2 = (q[:, :, :, :half], q[:, :, :, half:])
        k1, k2 = (k[:, :, :, :half], k[:, :, :, half:])
        v1, v2 = (v[:, :, :, :half], v[:, :, :, half:])
        q2 = jnp.roll(q2, -half, axis=2)
        k2 = jnp.roll(k2, -half, axis=2)
        v2 = jnp.roll(v2, -half, axis=2)
        out1 = _attention(q1, k1, v1, d)
        out2 = _attention(q2, k2, v2, d)
        out = jnp.concatenate([out1, out2], axis=3)
        out = jnp.concatenate([out[:, :, :, :half], jnp.roll(out[:, :, :, half:], half, axis=2)], axis=3)
        out = out.transpose(0, 2, 1, 3, 4).reshape(b, n, h * d)
        return out

    def _L1_ffn_ref(x, attention_mask, position_ids, router_w, router_b, wq, wk, wv, wo, w1, w2, ln1, ln2):
        import jax, jax.numpy as jnp
        import numpy as np
        B, S, D, H, F = (4, 512, 128, 16, 512)
        CAP = 0.125
        ROPE_BASE = 10000.0

        def rmsnorm(x, g):
            return x * jax.lax.rsqrt(jnp.mean(x * x, -1, keepdims=True) + 1e-06) * g

        def rope(t, pos):
            hd = t.shape[-1]
            inv = 1.0 / ROPE_BASE ** (jnp.arange(0, hd, 2, dtype=jnp.float32) / hd)
            f = pos[:, None, :, None].astype(jnp.float32) * inv
            emb = jnp.concatenate([f, f], axis=-1)
            cos, sin = (jnp.cos(emb), jnp.sin(emb))
            rot = jnp.concatenate([-t[..., hd // 2:], t[..., :hd // 2]], axis=-1)
            return t * cos + rot * sin
        b, s, d = x.shape
        hd = d // H
        weights = (x @ router_w)[..., 0] + router_b[0]
        k = int(CAP * s)
        topv, topi = jax.lax.top_k(weights, k)
        thr = topv[:, -1]
        sel_mask = (weights > thr[:, None]).astype(x.dtype)
        kc = k - 1
        sel_idx = jnp.sort(topi[:, :kc], axis=1)
        bidx = jnp.arange(b)[:, None]
        x_sel = x[bidx, sel_idx]
        pos_sel = position_ids[bidx, sel_idx]
        w_sel = weights[bidx, sel_idx]
        m = attention_mask[:, 0]
        m_sel = m[bidx[:, :, None], sel_idx[:, :, None], sel_idx[:, None, :]]
        hn = rmsnorm(x_sel, ln1)

        def heads(t):
            return t.reshape(b, kc, H, hd).transpose(0, 2, 1, 3)
        q = rope(heads(hn @ wq), pos_sel)
        kk = rope(heads(hn @ wk), pos_sel)
        v = heads(hn @ wv)
        sc = jnp.einsum('bhqd,bhkd->bhqk', q, kk) / np.sqrt(hd).astype(np.float32)
        sc = sc + m_sel[:, None]
        a = jax.nn.softmax(sc, axis=-1)
        o = jnp.einsum('bhqk,bhkd->bhqd', a, v).transpose(0, 2, 1, 3).reshape(b, kc, d) @ wo
        x1 = x_sel + o
        x2 = x1 + jax.nn.gelu(rmsnorm(x1, ln2) @ w1) @ w2
        proc = x2 * w_sel[..., None]
        out = jnp.zeros_like(x).at[bidx, sel_idx].set(proc)
        return out + x * (1.0 - sel_mask)[..., None]
    x = L0_attn_a_h
    x = x + _L0_attn_a_ref(_layernorm(x, axis=-1), L0_attn_a_w_qc, L0_attn_a_w_qup, L0_attn_a_w_k, L0_attn_a_w_v, L0_attn_a_g_qnorm, L0_attn_a_g_knorm, L0_attn_a_w_gate, L0_attn_a_b_gate, L0_attn_a_sink_logit, L0_attn_a_w_out_group, L0_attn_a_w_out)
    x = x + _L0_ffn_ref(_layernorm(x, axis=-1), L0_ffn_gate_w, L0_ffn_wi_gate, L0_ffn_wi_up, L0_ffn_wo)
    x = x + _L0_attn_b_ref(_layernorm(x, axis=-1), L0_attn_b_attn_mask, L0_attn_b_Wq, L0_attn_b_bq, L0_attn_b_Wk, L0_attn_b_bk, L0_attn_b_Wv, L0_attn_b_bv, L0_attn_b_Wo, L0_attn_b_bo, L0_attn_b_ln1_g, L0_attn_b_ln1_b, L0_attn_b_W1, L0_attn_b_b1, L0_attn_b_W2, L0_attn_b_b2, L0_attn_b_ln2_g, L0_attn_b_ln2_b)
    x = x + _L0_ffn_ref(_layernorm(x, axis=-1), L0_ffn_gate_w, L0_ffn_wi_gate, L0_ffn_wi_up, L0_ffn_wo)
    x = x + _L1_attn_a_ref(_layernorm(x, axis=-1), L1_attn_a_Wk, L1_attn_a_Wv, L1_attn_a_Wr, L1_attn_a_Wo, L1_attn_a_spatial_decay, L1_attn_a_spatial_first, L1_attn_a_mix_k, L1_attn_a_mix_v, L1_attn_a_mix_r)
    x = x + _L1_ffn_ref(_layernorm(x, axis=-1), L1_ffn_attention_mask, L1_ffn_position_ids, L1_ffn_router_w, L1_ffn_router_b, L1_ffn_wq, L1_ffn_wk, L1_ffn_wv, L1_ffn_wo, L1_ffn_w1, L1_ffn_w2, L1_ffn_ln1, L1_ffn_ln2)
    x = x + _L1_attn_b_ref(_layernorm(x, axis=-1), L1_attn_b_w_qkv, L1_attn_b_b_qkv)
    x = x + _L1_ffn_ref(_layernorm(x, axis=-1), L1_ffn_attention_mask, L1_ffn_position_ids, L1_ffn_router_w, L1_ffn_router_b, L1_ffn_wq, L1_ffn_wk, L1_ffn_wv, L1_ffn_wo, L1_ffn_w1, L1_ffn_w2, L1_ffn_ln1, L1_ffn_ln2)
    return x

_drawn_inputs = setup_inputs


def setup_inputs(seed=0):
    import zlib

    import numpy as np

    out = dict(_drawn_inputs(seed))
    spreads = {'L0_attn_a_g_qnorm': (1.0, 0.6),
     'L0_attn_a_g_knorm': (1.0, 0.6),
     'L0_attn_a_b_gate': (0.0, 0.8),
     'L0_attn_b_bq': (0.0, 2.0),
     'L0_attn_b_bk': (0.0, 2.0),
     'L0_attn_b_bv': (0.0, 0.8),
     'L0_attn_b_bo': (0.0, 0.1),
     'L0_attn_b_ln1_g': (1.0, 0.2),
     'L0_attn_b_ln1_b': (0.0, 0.1),
     'L0_attn_b_b1': (0.0, 0.575),
     'L0_attn_b_b2': (0.0, 0.1),
     'L0_attn_b_ln2_g': (1.0, 0.2),
     'L0_attn_b_ln2_b': (0.0, 0.1),
     'L1_ffn_ln1': (1.0, 0.6),
     'L1_ffn_ln2': (1.0, 0.6)}
    factors = {'L0_attn_a_w_gate': 8.0,
     'L0_attn_a_sink_logit': 7.55,
     'L0_attn_b_Wq': 8.0,
     'L0_attn_b_Wk': 8.0,
     'L0_attn_b_Wv': 7.212,
     'L0_attn_b_Wo': 5.053,
     'L0_ffn_gate_w': 3.682,
     'L0_ffn_wi_gate': 3.444,
     'L0_ffn_wi_up': 3.328,
     'L0_ffn_wo': 2.985,
     'L1_attn_a_spatial_decay': 8.0,
     'L1_attn_a_spatial_first': 200.0,
     'L1_attn_a_mix_k': 4.383,
     'L1_attn_a_mix_r': 3.109,
     'L1_attn_b_b_qkv': 6.196,
     'L1_ffn_wq': 8.0,
     'L1_ffn_wk': 8.0,
     'L1_ffn_wv': 8.0,
     'L1_ffn_wo': 8.0,
     'L1_ffn_w1': 7.657,
     'L1_ffn_w2': 7.585}
    for name, (base, spread) in spreads.items():
        noise = np.random.default_rng([zlib.crc32(name.encode()), seed]).standard_normal(out[name].shape)
        drawn = base * np.exp(spread * noise) if base else spread * noise
        out[name] = jnp.asarray(drawn.astype(out[name].dtype))
    for name, factor in factors.items():
        out[name] = (out[name] * factor).astype(out[name].dtype)
    return out
```

```python
from contextlib import ExitStack

import numpy as np

import concourse.bass as bass
from concourse import mybir

ALU = mybir.AluOpType
ACT = mybir.ActivationFunctionType
AX = mybir.AxisListType.X
F32 = mybir.dt.float32
I32 = mybir.dt.int32

B, T, C = 4, 512, 128
P = 128
NC = T // P
A_H, A_D, A_CR = 8, 64, 32
A_NB = T // A_CR
A_WINDOW, A_QC, A_ROPE = 64, 32, 32
H, DH = 16, 8
F, E = 512, 8
NF = F // P
CAPACITY = int(B * T / E * 1.25)
SLOTS = T // 8
GROUP = 16
NBLK = B * T // GROUP
NEG = -1e30
PI_BELOW = 3.1415925


def split_two_pi():
    rest, parts = 2 * np.pi, []
    for bits in (2.0 ** -8, 2.0 ** -19):
        parts.append(float(np.floor(rest / bits) * bits))
        rest -= parts[-1]
    return parts + [float(np.float32(rest))]


TWO_PI = split_two_pi()


def constants():
    p = np.arange(P)
    f = lambda a: np.asarray(a, np.float32).reshape(P, -1)
    k = {}
    k["mean"] = f(np.full((P, P), 1.0 / C))
    k["ident"] = f(np.eye(P))
    k["ones"] = f(np.ones((P, T)))
    k["mean64"] = f((p[:, None] // 64 == p[None, :] // 64) / 64.0)
    k["same8"] = f(p[:, None] // DH == p[None, :] // DH)
    k["upto"] = f(p[:, None] <= p[None, :])
    half = A_ROPE // 2
    inv = (np.float32(1.0) / np.float32(10000.0) ** (np.arange(half, dtype=np.float32) * np.float32(2.0) / np.float32(A_ROPE))).astype(np.float32)
    ang = np.arange(T, dtype=np.float32)[:, None] * inv[None, :]
    cos, sin = np.cos(ang), np.sin(ang)
    c64, s64 = np.ones((A_D, T), np.float32), np.zeros((A_D, T), np.float32)
    c64[:half], c64[half:2 * half] = cos.T, cos.T
    s64[:half], s64[half:2 * half] = -sin.T, sin.T
    k["rope_cos"], k["rope_sin"] = f(np.tile(c64, (2, 1))), f(np.tile(s64, (2, 1)))
    causal = np.zeros((P, T))
    causal[:, T - P:] = np.where(p[:, None] >= p[None, :], 0.0, NEG)
    k["causal"] = f(causal)
    d = (p[:, None] + P) - np.arange(2 * P)[None, :]
    k["band"] = f(np.where((d >= 0) & (d < A_WINDOW), 0.0, NEG))
    blk_end = (np.arange(A_NB) + 1) * A_CR - 1
    q = p[:, None] + P * np.arange(NC)[None, :]
    k["blocks_seen"] = f(np.where(blk_end[None, None, :] <= q[:, :, None], 0.0, NEG))
    rep = np.zeros((P, NC, A_H, A_NB))
    for c in range(NC):
        rep[p, c, :, (P * c + p) // A_CR] = 1.0 / A_CR
    k["block_mean"] = f(rep)
    hn = p // A_NB
    vc = np.zeros((P, A_H // 2, 2, A_D))
    for h in range(A_H):
        vc[hn == h, h // 2, h % 2, :] = 1.0
    k["head_of_block"] = f(vc)
    k["head_in_quad"] = f((p[:, None] % 32) // DH == np.arange(4)[None, :])
    k["head"] = f(p[:, None] // DH == np.arange(H)[None, :])
    k["count"] = f(np.tile(np.arange(T) + 1.0, (P, 1)))
    k["inv_count"] = f(np.tile(1.0 / (np.arange(T) + 1.0), (P, 1)))
    k["expert_rank"] = f(np.tile(np.arange(E) - 99.0, (P, NC)))
    u = np.arange(T + (NC - 1) * P)
    k["before"] = f(u[None, :] < p[:, None] + (NC - 1) * P)
    k["slot"] = f(np.tile(np.arange(SLOTS), (P, 1)))
    k["last_slot"] = f(np.tile(np.where(np.arange(SLOTS) == SLOTS - 1, NEG, 0.0), (P, 1)))
    hinv = 1.0 / np.float32(10000.0) ** (np.arange(0, DH, 2, dtype=np.float32) / np.float32(DH))
    k["mod_inv"] = f(hinv[(p % DH) % (DH // 2)])
    k["mod_sign"] = f(np.where(p % DH < DH // 2, -1.0, 1.0))
    pair = np.zeros((P, H // 2, C))
    for m in range(H // 2):
        pair[:, m, :] = p[None, :] // DH == 2 * m + (p[:, None] // SLOTS)
    k["head_of_pair"] = f(pair)
    for name, v in (("eps5", 1e-5), ("eps6", 1e-6), ("zero", 0.0)):
        k[name] = f(np.full((P, 1), v))
    return k


def _swap(n, lo, hi):
    h = (hi - lo) // 2
    o = np.arange(n)
    o[lo:lo + h], o[lo + h:hi] = np.arange(lo + h, hi), np.arange(lo, lo + h)
    return o


def parameters(a):
    k = {}

    def col(v):
        return v.reshape(P, 1)

    def rows(m):
        return m.reshape(-1, P, m.shape[1]).transpose(1, 0, 2).reshape(P, -1)

    def tall(m):
        out = np.zeros((P, m.shape[1]), m.dtype)
        out[:m.shape[0]] = m
        return out

    rot = _swap(A_D, 0, A_ROPE)
    g = "L0_attn_a_"
    k["a_w_qc"] = a[g + "w_qc"]
    qup = a[g + "w_qup"]
    k["a_w_q"] = tall(qup)
    k["a_w_qr"] = tall(qup.reshape(A_QC, A_H, A_D)[:, :, rot].reshape(A_QC, -1))
    k["a_w_k"] = np.tile(a[g + "w_k"], (1, 2))
    k["a_w_kr"] = np.tile(a[g + "w_k"][:, rot], (1, 2))
    k["a_w_v"] = np.tile(a[g + "w_v"], (1, 2))
    k["a_gq"] = col(np.tile(a[g + "g_qnorm"], 2))
    k["a_gk"] = col(np.tile(a[g + "g_knorm"], 2))
    k["a_w_gate"] = np.tile(a[g + "w_gate"], (2, 1))
    k["a_b_gate"] = np.tile(a[g + "b_gate"], (P, A_H))
    k["a_sink"] = np.tile(a[g + "sink_logit"], (P, 1))
    wog = a[g + "w_out_group"]
    wide = np.zeros((4, P, P), wog.dtype)
    for pr in range(4):
        gg = pr // 2
        wide[pr, :, gg * 64:(gg + 1) * 64] = wog[gg, (pr % 2) * P:(pr % 2 + 1) * P]
    k["a_w_group"] = wide.transpose(1, 0, 2).reshape(P, -1)
    k["a_w_out"] = a[g + "w_out"]
    g = "L0_attn_b_"
    for n in ("Wq", "Wk", "Wv", "Wo", "W1"):
        k["f_" + n] = a[g + n]
    for n in ("bq", "bk", "bv", "bo", "b2", "ln1_g", "ln1_b", "ln2_g", "ln2_b"):
        k["f_" + n] = col(a[g + n])
    k["f_b1"] = a[g + "b1"].reshape(NF, P).T
    k["f_W2"] = rows(a[g + "W2"])
    k["e_gate"] = a["L0_ffn_gate_w"].T
    g = "L1_attn_a_"
    for n in ("Wk", "Wv", "Wr", "Wo"):
        k["r_" + n] = a[g + n].T
    for n in ("spatial_decay", "spatial_first", "mix_k", "mix_v", "mix_r"):
        k["r_" + n] = col(a[g + n])
    k["b_w"] = a["L1_attn_b_w_qkv"].T
    k["b_b"] = np.tile(a["L1_attn_b_b_qkv"], (P, 1))
    g = "L1_ffn_"
    rot = _swap(DH, 0, DH)
    k["m_router"] = a[g + "router_w"]
    k["m_router_b"] = np.tile(a[g + "router_b"], (P, 1))
    for n in ("wq", "wk"):
        k["m_" + n] = a[g + n]
        k["m_" + n + "r"] = a[g + n].reshape(C, H, DH)[:, :, rot].reshape(C, C)
    for n in ("wv", "wo", "w1"):
        k["m_" + n] = a[g + n]
    k["m_w2"] = rows(a[g + "w2"])
    k["m_ln1"], k["m_ln2"] = col(a[g + "ln1"]), col(a[g + "ln2"])
    return k


class Steps:

    def __init__(self, sem, order, turns):
        self.sem, self.order, self.turns, self.seen = sem, order, turns, []

    def mark(self, name):
        assert name not in self.seen, name
        self.seen.append(name)
        return self.sem, self.unit

    unit = 1

    def __call__(self, name, turn):
        if self.order is None:
            return self.sem, 1
        return self.sem, turn * (len(self.order) * self.unit) + ((self.order.index(name) + 1) * self.unit + 1)

    def end(self, turns=None):
        n = 1 if self.order is None else len(self.order)
        return self.sem, (self.turns if turns is None else turns) * (n * self.unit) + 1


class DmaSteps(Steps):
    unit = 16


class Stage:

    def __init__(self, name, sem, plan, turns=B):
        self.name = name
        self.counters = {}
        for engine in ("pe", "act", "dve", "pool", "dma"):
            kind = DmaSteps if engine == "dma" else Steps
            order = None if plan is None else plan[name][engine]
            if order is None or order:
                self.counters[engine] = kind(sem(f"{name}_{engine}"), order, turns)
            else:
                self.counters[engine] = kind(None, [], turns)
        self.pe, self.act, self.dve, self.pool, self.dma = (self.counters[k] for k in ("pe", "act", "dve", "pool", "dma"))

    def finished(self, e, turns=None):
        for c in self.counters.values():
            if c.order is None or c.order:
                e.wait_ge(*c.end(turns))


def norm_pe(e, M, L, b, tag, src, ready):
    for w in ready:
        e.wait_ge(*w)
    e.matmul(M.ps[0][:, :], M.k("mean"), src, start=True, stop=True).then_inc(*L.pe.mark(tag + "_mean"))
    e.wait_ge(*L.act(tag + "_square", b))
    e.matmul(M.ps[1][:, :], M.k("mean"), M.sq[:, :], start=True, stop=True).then_inc(*L.pe.mark(tag + "_var"))


def norm_act(e, M, L, b, tag):
    e.wait_ge(*L.dve(tag + "_centred", b))
    e.activation(M.sq[:, :], M.xc[:, :], ACT.Square).then_inc(*L.act.mark(tag + "_square"))
    e.wait_ge(*L.pe(tag + "_var", b))
    e.activation(M.sd[:, :], M.ps[1][:, :], ACT.Sqrt, bias=M.k("eps5")).then_inc(*L.act.mark(tag + "_sd"))


def norm_dve(e, M, L, b, tag, src, dst, gain=None, shift=None):
    e.wait_ge(*L.pe(tag + "_mean", b))
    e.tensor_tensor(M.xc[:, :], src, M.ps[0][:, :], ALU.subtract).then_inc(*L.dve.mark(tag + "_centred"))
    e.wait_ge(*L.act(tag + "_sd", b))
    e.reciprocal(M.rs[:, :], M.sd[:, :]).then_inc(*L.dve.mark(tag + "_rs"))
    e.wait_ge(*L.dve(tag + "_rs", b))
    if gain is None:
        e.tensor_tensor(dst, M.xc[:, :], M.rs[:, :], ALU.mult).then_inc(*L.dve.mark(tag))
        return
    e.scalar_tensor_tensor(M.xc[:, :], M.xc[:, :], gain, M.rs[:, :], ALU.mult, ALU.mult).then_inc(*L.dve.mark(tag + "_gained"))
    e.wait_ge(*L.dve(tag + "_gained", b))
    e.tensor_scalar(dst, M.xc[:, :], shift, None, ALU.add).then_inc(*L.dve.mark(tag))

class Layer:
    turns = B
    needs_experts = False
    pe = act = dve = pool = sp = None
    pe_after = act_after = dve_after = pool_after = sp_after = None

    def before(self, e, M, which, sem):
        pass

    def parts(self):
        return {"pe": (self.pe, self.pe_after), "act": (self.act, self.act_after), "dve": (self.dve, self.dve_after),
                "pool": (self.pool, self.pool_after), "sp": (self.sp, self.sp_after)}


class Experts(Layer):
    needs_experts = True

    def __init__(self, M):
        s = M.small
        self.lg, self.eq, self.tmp = (s[:, i * 32:(i + 1) * 32].rearrange("p (c e) -> p c e", e=E) for i in range(3))
        self.m1, self.m2, self.pick, self.e2, self.w1, self.w2 = (s[:, 96 + 4 * i:100 + 4 * i] for i in range(6))
        self.chosen = s[:, 128:192].rearrange("p (c k) -> p c k", c=NC)
        self.room = s[:, 192:256].rearrange("p (c k) -> p c k", c=NC)
        self.coef = s[:, 256:288].rearrange("p (c e) -> p c e", e=E)
        self.part = s[:, 288:320].rearrange("p (c e) -> p c e", e=E)
        self.taken = s[:, 320:336]
        self.scaled = [M.tile(0), M.tile(1)]
        self.act_out = [M.tile(2 + i) for i in range(3)]
        self.mid = [M.tile(5 + i) for i in range(3)]

    UNITS = [(x, f) for x in range(E) for f in range(NF)]

    def pe(self, e, M, L, b):
        L.finished(e, b)
        norm_pe(e, M, L, b, "norm", M.x[:, b, :], [])
        e.wait_ge(*L.dve("norm", b))
        logits = M.ps[7][:, 0:NC * E]
        for c in range(NC):
            e.matmul(logits[:, c * E:(c + 1) * E], M.h[:, c * P:(c + 1) * P], M.w("e_gate"), start=True, stop=True)\
                .then_inc(*L.pe.mark(f"logits{c}"))
        e.wait_ge(*L.dve("chosen2", b))
        for c in range(NC):
            out = M.ps[7][:, 64 + 16 * c:80 + 16 * c]
            e.matmul(out, M.k("upto"), self.chosen[:, c, :], start=True, stop=(c == 0))
            for d in range(c):
                e.matmul(out, M.k("ones")[:, 0:P], self.chosen[:, d, :], start=False, stop=(d == c - 1))
        out = M.ps[7][:, 128:144]
        for d in range(NC):
            mm = e.matmul(out, M.k("ones")[:, 0:P], self.chosen[:, d, :], start=(d == 0), stop=(d == NC - 1))
        mm.then_inc(*L.pe.mark("counted"))
        e.wait_ge(*L.dve("coef", b))

        def spread(x):
            if x >= 2:
                e.wait_ge(*L.dve(f"scaled{x - 2}", b))
            for c in range(NC):
                mm = e.transpose(M.ps[4 + x % 2][:, c * P:(c + 1) * P], self.coef[:, c, x:x + 1].broadcast_to([P, P]), M.k("ident"))
            mm.then_inc(*L.pe.mark(f"spread{x}"))

        def down(u):
            x, f = self.UNITS[u]
            e.wait_ge(*L.dve(f"mid{u}", b))
            e.matmul(M.ps[6][:, :], M.expert_out[:, x, f, :], self.mid[u % 3][:, :],
                     start=(u == 0), stop=(u == len(self.UNITS) - 1)).then_inc(*L.pe.mark(f"down{u}"))

        spread(0)
        for u, (x, f) in enumerate(self.UNITS):
            if f == 0 and x + 1 < E:
                spread(x + 1)
            if u >= 2:
                e.wait_ge(*L.act(f"silu{u - 2}", b))
            e.matmul(M.ps[u % 2][:, :], M.expert_gate[:, x, f * P:(f + 1) * P], M.h[:, :], start=True, stop=True)\
                .then_inc(*L.pe.mark(f"gate{u}"))
            if f == 0:
                e.wait_ge(*L.dve(f"scaled{x}", b))
            if u >= 2:
                e.wait_ge(*L.dve(f"mid{u - 2}", b))
            e.matmul(M.ps[2 + u % 2][:, :], M.expert_up[:, x, f * P:(f + 1) * P], self.scaled[x % 2][:, :], start=True, stop=True)\
                .then_inc(*L.pe.mark(f"up{u}"))
            if u >= 1:
                down(u - 1)
        down(len(self.UNITS) - 1)

    def act(self, e, M, L, b):
        L.finished(e, b)
        norm_act(e, M, L, b, "norm")
        e.wait_ge(*L.dve("gap", b))
        e.activation(self.e2, self.w1, ACT.Exp).then_inc(*L.act.mark("e2"))
        for u in range(len(self.UNITS)):
            e.wait_ge(*L.pe(f"gate{u}", b))
            if u >= 3:
                e.wait_ge(*L.dve(f"mid{u - 3}", b))
            e.activation(self.act_out[u % 3][:, :], M.ps[u % 2][:, :], ACT.Silu).then_inc(*L.act.mark(f"silu{u}"))

    def dve(self, e, M, L, b):
        L.finished(e, b)
        norm_dve(e, M, L, b, "norm", M.x[:, b, :], M.h[:, :])
        wide = lambda a: a.unsqueeze(2).broadcast_to([P, NC, E])
        rank = M.k("expert_rank").rearrange("p (c e) -> p c e", e=E)

        def step(name, ins):
            ins.then_inc(*L.dve.mark(name))
            e.wait_ge(*L.dve(name, b))

        e.wait_ge(*L.pe(f"logits{NC - 1}", b))
        step("logits", e.tensor_copy(self.lg, M.ps[7][:, 0:NC * E].rearrange("p (c e) -> p c e", e=E)))
        for k, m in ((0, self.m1), (1, self.m2)):
            step(f"max{k}", e.tensor_reduce(m, self.lg, AX, ALU.max))
            step(f"top{k}", e.tensor_tensor(self.eq, self.lg, wide(m), ALU.is_equal))
            step(f"rank{k}", e.tensor_tensor(self.tmp, self.eq, rank, ALU.mult))
            step(f"first{k}", e.tensor_reduce(self.pick, self.tmp, AX, ALU.min))
            step(f"chosen{k + 1}", e.tensor_tensor(self.chosen[:, :, k * E:(k + 1) * E], rank, wide(self.pick), ALU.is_equal))
            if k == 0:
                step("rest", e.scalar_tensor_tensor(self.lg, self.chosen[:, :, 0:E], NEG, self.lg, ALU.mult, ALU.add))
        step("gap", e.tensor_tensor(self.w1, self.m2, self.m1, ALU.subtract))
        e.wait_ge(*L.act("e2", b))
        step("norm_sum", e.tensor_scalar(self.w2, self.e2, 1.0, None, ALU.add))
        step("w1", e.reciprocal(self.w1, self.w2))
        step("w2", e.tensor_tensor(self.w2, self.w1, self.e2, ALU.mult))
        e.wait_ge(*L.pe("counted", b))
        taken = self.taken.unsqueeze(1).broadcast_to([P, NC, 2 * E])
        step("place", e.tensor_tensor(self.room, M.ps[7][:, 64:128].rearrange("p (c k) -> p c k", c=NC), taken, ALU.add))
        step("room", e.scalar_tensor_tensor(self.room, self.room, float(CAPACITY), self.chosen, ALU.is_le, ALU.mult))
        step("taken", e.tensor_tensor(self.taken, self.taken, M.ps[7][:, 128:144], ALU.add))
        step("coef1", e.tensor_tensor(self.coef, self.room[:, :, 0:E], wide(self.w1), ALU.mult))
        step("coef2", e.tensor_tensor(self.part, self.room[:, :, E:2 * E], wide(self.w2), ALU.mult))
        step("coef", e.tensor_tensor(self.coef, self.coef, self.part, ALU.add))

        def scaled(x):
            e.wait_ge(*L.pe(f"spread{x}", b))
            if x >= 2:
                e.wait_ge(*L.pe(f"up{4 * (x - 2) + 3}", b))
            e.tensor_tensor(self.scaled[x % 2][:, :], M.h[:, :], M.ps[4 + x % 2][:, :], ALU.mult).then_inc(*L.dve.mark(f"scaled{x}"))

        scaled(0)
        for u, (x, f) in enumerate(self.UNITS):
            if f == 1 and x + 1 < E:
                scaled(x + 1)
            e.wait_ge(*L.act(f"silu{u}", b))
            e.wait_ge(*L.pe(f"up{u}", b))
            if u >= 3:
                e.wait_ge(*L.pe(f"down{u - 3}", b))
            e.tensor_tensor(self.mid[u % 3][:, :], self.act_out[u % 3][:, :], M.ps[2 + u % 2][:, :], ALU.mult).then_inc(*L.dve.mark(f"mid{u}"))
        e.wait_ge(*L.pe(f"down{len(self.UNITS) - 1}", b))
        e.tensor_tensor(M.x[:, b, :], M.x[:, b, :], M.ps[6][:, :], ALU.add).then_inc(*L.dve.mark("residual"))

    def before(self, e, M, which, sem):
        if which == "dve":
            e.memset(self.taken, 0.0).then_inc(sem, 1)
            e.wait_ge(sem, 1)


class Flow(Layer):
    def __init__(self, M):
        t = M.tile
        self.q, self.k, self.v, self.qe, self.ke, self.ca, self.cb, self.da, self.db, self.ra, self.rb = (t(i) for i in range(11))
        self.masked_q = M.wide[:, 0:4, :]
        self.scores = [M.wide[:, 4, :], M.wide[:, 5, :], M.wide[:, 6, :]]
        self.k_tok, self.v_tok = M.wide[:, 7, :], M.wide[:, 8, :]
        self.state = M.wide[:, 9, 0:3 * P]
        wide = H * (P + DH)
        self.v_heads = [M.big[:, c * wide:c * wide + H * P].rearrange("p (h f) -> p h f", f=P) for c in range(2)]
        self.v_diagonal = [M.big[:, c * wide:(c + 1) * wide].rearrange("p (h f) -> p h f", f=P + DH)[:, :, 0:DH] for c in range(2)]
        self.mid = M.wide[:, 14:18, :]
        self.sink, self.src = M.wide[:, 18, :], M.wide[:, 19, :]
        self.eps = 1e-6

    def before(self, e, M, which, sem):
        if which == "pool":
            e.memset(M.big[:, 0:2 * H * (P + DH)], 0.0).then_inc(sem, 1)
            e.wait_ge(sem, 1)

    def pe(self, e, M, L, b):
        L.finished(e, b)
        norm_pe(e, M, L, b, "norm", M.x[:, b, :], [])
        e.wait_ge(*L.dve("norm", b))
        for n, w in enumerate(("f_Wq", "f_Wk", "f_Wv")):
            e.matmul(M.ps[2 + n][:, :], M.w(w), M.h[:, :], start=True, stop=True).then_inc(*L.pe.mark(f"proj{n}"))
        for n, (src, bank) in enumerate(((self.da, 5), (self.db, 6))):
            e.wait_ge(*L.dve(f"flow{n}", b))
            e.matmul(M.ps[bank][:, :], M.k("same8"), src[:, :], start=True, stop=True).then_inc(*L.pe.mark(f"flow{n}"))
        for n, (src, bank) in enumerate(((self.da, 7), (self.db, 5))):
            e.wait_ge(*L.dve(f"cons{n}", b))
            e.matmul(M.ps[bank][:, :], M.k("same8"), src[:, :], start=True, stop=True).then_inc(*L.pe.mark(f"cons{n}"))
        e.wait_ge(*L.dve("vs", b))
        for c in range(NC):
            e.transpose(M.ps[0][:, c * P:(c + 1) * P], self.k[:, c * P:(c + 1) * P], M.k("ident"))
            mm = e.transpose(M.ps[1][:, c * P:(c + 1) * P], self.v[:, c * P:(c + 1) * P], M.k("ident"))
        mm.then_inc(*L.pe.mark("turned"))
        e.wait_ge(*L.act("k_tok", b))
        e.wait_ge(*L.act("v_tok", b))
        for c in range(NC - 1):
            s = slice(c * P, (c + 1) * P)
            mm = e.matmul(M.ps[6][:, s], self.k_tok[:, s], self.v_tok[:, s], start=True, stop=True)
        mm.then_inc(*L.pe.mark("kv"))
        e.wait_ge(*L.dve("masked_q3", b))
        units = [(c, g) for c in range(NC) for g in range(4)]

        def apply(u):
            c, g = units[u]
            if g == 0:
                e.wait_ge(*L.pool(f"v_head{c}", b))
            e.wait_ge(*L.dve(f"causal{u}", b))
            for r in range(4):
                mm = e.matmul(M.ps[5][:, c * P:(c + 1) * P], self.v_diag(c, 4 * g + r), self.scores[u % 3][:, r * P:(r + 1) * P],
                              start=(u == 0 and r == 0), stop=False, skip_group_check=True)
            mm.then_inc(*L.pe.mark(f"apply{u}"))

        for u, (c, g) in enumerate(units):
            if u >= 3:
                e.wait_ge(*L.dve(f"causal{u - 3}", b))
            rows = slice(32 * g, 32 * g + 32)
            e.matmul(M.ps[2 + u % 3][:, :], self.k[rows, c * P:(c + 1) * P], self.masked_q[rows, :, c * P:(c + 1) * P],
                     start=True, stop=True).then_inc(*L.pe.mark(f"scores{u}"))
            if u >= 1:
                apply(u - 1)
        apply(len(units) - 1)
        e.wait_ge(*L.dve("state2", b))
        for c in range(1, NC):
            mm = e.matmul(M.ps[5][:, c * P:(c + 1) * P], self.state[:, (c - 1) * P:c * P], self.q[:, c * P:(c + 1) * P],
                          start=False, stop=(c == NC - 1), skip_group_check=True)
        mm.then_inc(*L.pe.mark("attended"))
        e.wait_ge(*L.dve("alloc", b))
        e.matmul(M.ps[2][:, :], M.w("f_Wo"), self.da[:, :], start=True, stop=True).then_inc(*L.pe.mark("out"))
        norm_pe(e, M, L, b, "ln1", self.db[:, :], [L.dve("with_in", b)])
        e.wait_ge(*L.dve("ln1", b))
        for f in range(NF):
            e.matmul(M.ps[2 + f][:, :], M.w("f_W1")[:, f * P:(f + 1) * P], self.qe[:, :], start=True, stop=True).then_inc(*L.pe.mark(f"up{f}"))
        for f in range(NF):
            e.wait_ge(*L.act(f"gelu{f}", b))
            mm = e.matmul(M.ps[6][:, :], M.w("f_W2")[:, f * P:(f + 1) * P], self.mid[:, f, :], start=(f == 0), stop=(f == NF - 1))
        mm.then_inc(*L.pe.mark("down"))
        norm_pe(e, M, L, b, "ln2", self.ke[:, :], [L.dve("with_ffn", b)])

    def v_diag(self, c, h):
        return self.v_heads[c % 2][:, h, :]

    def act(self, e, M, L, b):
        L.finished(e, b)
        norm_act(e, M, L, b, "norm")
        for n, (dst, bias, fn) in enumerate(((self.q, "f_bq", ACT.Sigmoid), (self.k, "f_bk", ACT.Sigmoid), (self.v, "f_bv", ACT.Identity))):
            e.wait_ge(*L.pe(f"proj{n}", b))
            e.activation(dst[:, :], M.ps[2 + n][:, :], fn, bias=M.w(bias)).then_inc(*L.act.mark(("q", "k", "v")[n]))
        e.wait_ge(*L.dve("sink", b))
        e.activation(self.sink, self.sink, ACT.Sigmoid).then_inc(*L.act.mark("sink"))
        e.wait_ge(*L.dve("src", b))
        e.activation(self.src, self.src, ACT.Exp).then_inc(*L.act.mark("src"))
        e.wait_ge(*L.pe("turned", b))
        e.activation(self.k_tok, M.ps[0][:, :], ACT.Copy).then_inc(*L.act.mark("k_tok"))
        e.activation(self.v_tok, M.ps[1][:, :], ACT.Copy).then_inc(*L.act.mark("v_tok"))
        norm_act(e, M, L, b, "ln1")
        for f in range(NF):
            e.wait_ge(*L.pe(f"up{f}", b))
            e.activation(self.mid[:, f, :], M.ps[2 + f][:, :], ACT.Gelu, bias=M.w("f_b1")[:, f:f + 1]).then_inc(*L.act.mark(f"gelu{f}"))
        norm_act(e, M, L, b, "ln2")

    def pool(self, e, M, L, b):
        L.finished(e, b)
        e.wait_ge(*L.act("v_tok", b))
        for c in range(NC):
            if c >= 2:
                e.wait_ge(*L.pe(f"apply{4 * (c - 2) + 3}", b))
            src = self.v_tok[:, c * P:(c + 1) * P].rearrange("p (h d) -> p h d", d=DH)
            ones = M.k("ones")[:, 0:P].rearrange("p (h d) -> p h d", d=DH)
            e.tensor_tensor(self.v_diagonal[c % 2], src, ones, ALU.mult).then_inc(*L.pool.mark(f"v_head{c}"))

    def dve(self, e, M, L, b):
        L.finished(e, b)
        norm_dve(e, M, L, b, "norm", M.x[:, b, :], M.h[:, :])
        q, k, v, qe, ke, ca, cb, da, db, ra, rb = (x[:, :] for x in (self.q, self.k, self.v, self.qe, self.ke, self.ca, self.cb, self.da, self.db, self.ra, self.rb))
        eps, ones = self.eps, M.k("ones")

        def step(name, ins, wait=True):
            ins.then_inc(*L.dve.mark(name))
            if wait:
                e.wait_ge(*L.dve(name, b))

        e.wait_ge(*L.act("q", b))
        step("qe", e.tensor_scalar(qe, q, eps, None, ALU.add), False)
        step("cum_q", e.tensor_tensor_scan(cb, ones, q, 0.0, ALU.mult, ALU.add), False)
        e.wait_ge(*L.act("k", b))
        step("ke", e.tensor_scalar(ke, k, eps, None, ALU.add), False)
        step("cum_k", e.tensor_tensor_scan(ca, ones, k, 0.0, ALU.mult, ALU.add))
        step("flow0", e.scalar_tensor_tensor(da, ca, eps, qe, ALU.add, ALU.mult), False)
        step("flow1", e.scalar_tensor_tensor(db, cb, eps, ke, ALU.add, ALU.mult), False)
        for n, r in enumerate((ra, rb)):
            e.wait_ge(*L.pe(f"flow{n}", b))
            step(f"inv{n}", e.reciprocal(r, M.ps[5 + n][:, :]), n == 1)
        step("k_out", e.tensor_tensor(cb, k, rb, ALU.mult))
        step("k_out_n", e.tensor_tensor(cb, cb, M.k("count"), ALU.mult))
        step("q_in", e.tensor_tensor(ca, q, ra, ALU.mult))
        step("q_in_n", e.tensor_tensor(ca, ca, M.k("count"), ALU.mult))
        step("cum_out", e.tensor_tensor_scan(self.sink, ones, cb, 0.0, ALU.mult, ALU.add), False)
        step("cum_in", e.tensor_tensor_scan(self.src, ones, ca, 0.0, ALU.mult, ALU.add))
        step("cons0", e.scalar_tensor_tensor(da, self.sink, eps, qe, ALU.add, ALU.mult), False)
        step("cons1", e.scalar_tensor_tensor(db, self.src, eps, ke, ALU.add, ALU.mult), False)
        e.wait_ge(*L.pe("cons0", b))
        step("sink", e.tensor_tensor(self.sink, M.ps[7][:, :], M.k("inv_count"), ALU.mult), False)
        e.wait_ge(*L.pe("cons1", b))
        step("src_n", e.tensor_tensor(self.src, M.ps[5][:, :], M.k("inv_count"), ALU.mult))
        step("src", e.tensor_scalar(self.src, self.src, -1.0, 1.0, ALU.max, ALU.min))
        step("qs", e.tensor_tensor(q, q, ra, ALU.mult))
        e.wait_ge(*L.act("src", b))
        step("cum_src", e.tensor_tensor_scan(ca, ones, self.src, 0.0, ALU.mult, ALU.add))
        step("inv_src", e.reciprocal(cb, ca))
        step("comp", e.tensor_tensor(cb, cb, self.src, ALU.mult))
        step("comp_n", e.tensor_tensor(cb, cb, M.k("count"), ALU.mult))
        e.wait_ge(*L.act("v", b))
        step("vs", e.tensor_tensor(v, v, cb, ALU.mult), False)
        for r in range(4):
            step(f"masked_q{r}", e.tensor_scalar(self.masked_q[:, r, :], q, M.k("head_in_quad")[:, r:r + 1], None, ALU.mult), False)
        e.wait_ge(*L.pe("kv", b))
        for c in range(NC - 1):
            s = slice(c * P, (c + 1) * P)
            step(f"kv{c}", e.tensor_tensor(self.state[:, s], M.ps[6][:, s], M.k("same8"), ALU.mult))
            if c:
                step(f"state{c}", e.tensor_tensor(self.state[:, s], self.state[:, s], self.state[:, (c - 1) * P:c * P], ALU.add))
        upto = M.k("upto").unsqueeze(1).broadcast_to([P, 4, P])
        for u in range(4 * NC):
            e.wait_ge(*L.pe(f"scores{u}", b))
            if u >= 3:
                e.wait_ge(*L.pe(f"apply{u - 3}", b))
            dst = self.scores[u % 3].rearrange("p (r l) -> p r l", r=4)
            step(f"causal{u}", e.tensor_tensor(dst, M.ps[2 + u % 3][:, :].rearrange("p (r l) -> p r l", r=4), upto, ALU.mult), False)
        e.wait_ge(*L.pe("attended", b))
        e.wait_ge(*L.act("sink", b))
        step("alloc", e.tensor_tensor(da, self.sink, M.ps[5][:, :], ALU.mult), False)
        e.wait_ge(*L.pe("out", b))
        step("with_in", e.scalar_tensor_tensor(db, M.ps[2][:, :], M.w("f_bo"), M.h[:, :], ALU.add, ALU.add))
        norm_dve(e, M, L, b, "ln1", db, qe, M.w("f_ln1_g"), M.w("f_ln1_b"))
        e.wait_ge(*L.pe("down", b))
        step("with_ffn", e.scalar_tensor_tensor(ke, M.ps[6][:, :], M.w("f_b2"), qe, ALU.add, ALU.add))
        norm_dve(e, M, L, b, "ln2", ke, da, M.w("f_ln2_g"), M.w("f_ln2_b"))
        e.wait_ge(*L.dve("ln2", b))
        e.tensor_tensor(M.x[:, b, :], M.x[:, b, :], da, ALU.add).then_inc(*L.dve.mark("residual"))


class TimeMix(Layer):

    def __init__(self, M):
        self.xx, self.xk, self.xv, self.xr, self.ek, self.eku, self.sr, self.v = (M.tile(i) for i in range(8))
        self.sa, self.sb, self.t, self.den, self.num = (M.wide[:, i, :] for i in range(5))
        self.one_less, self.cols = M.small[:, 0:3], M.small[:, 4:8]
        self.decay = M.tile(8)

    def pe(self, e, M, L, b):
        L.finished(e, b)
        norm_pe(e, M, L, b, "norm", M.x[:, b, :], [])
        for n, (w, s) in enumerate((("r_Wk", self.xk), ("r_Wv", self.xv), ("r_Wr", self.xr))):
            e.wait_ge(*L.dve(f"mixed{n}", b))
            e.matmul(M.ps[2 + n][:, :], M.w(w), s[:, :], start=True, stop=True).then_inc(*L.pe.mark(f"proj{n}"))
        e.wait_ge(*L.dve("gated", b))
        e.matmul(M.ps[5][:, :], M.w("r_Wo"), self.num, start=True, stop=True).then_inc(*L.pe.mark("out"))

    def act(self, e, M, L, b):
        L.finished(e, b)
        norm_act(e, M, L, b, "norm")
        e.activation(self.cols[:, 0:1], M.w("r_spatial_decay"), ACT.Exp, scale=1.0 / T).then_inc(*L.act.mark("decay_col"))
        e.activation(self.cols[:, 1:2], M.w("r_spatial_first"), ACT.Copy, scale=1.0 / T).then_inc(*L.act.mark("first_col"))
        e.wait_ge(*L.act("first_col", b))
        e.wait_ge(*L.pe("proj0", b))
        e.activation(self.ek[:, :], M.ps[2][:, :], ACT.Exp).then_inc(*L.act.mark("ek"))
        e.activation(self.eku[:, :], M.ps[2][:, :], ACT.Exp, bias=self.cols[:, 1:2]).then_inc(*L.act.mark("eku"))
        e.wait_ge(*L.pe("proj2", b))
        e.activation(self.sr[:, :], M.ps[4][:, :], ACT.Sigmoid).then_inc(*L.act.mark("sr"))

    def dve(self, e, M, L, b):
        L.finished(e, b)
        norm_dve(e, M, L, b, "norm", M.x[:, b, :], M.h[:, :])
        Q = C // 4
        e.wait_ge(*L.dve("norm", b))
        e.tensor_copy(self.xx[0:Q, 1:T], M.h[0:Q, 0:T - 1]).then_inc(*L.dve.mark("shift_a"))
        e.memset(self.xx[0:Q, 0:1], 0.0).then_inc(*L.dve.mark("shift_b"))
        e.tensor_copy(self.xx[Q:2 * Q, 0:T - 1], M.h[Q:2 * Q, 1:T]).then_inc(*L.dve.mark("shift_c"))
        e.memset(self.xx[Q:2 * Q, T - 1:T], 0.0).then_inc(*L.dve.mark("shift_d"))
        e.tensor_copy(self.xx[2 * Q:C, :], M.h[2 * Q:C, :]).then_inc(*L.dve.mark("shift_e"))
        mixes = [M.w(n) for n in ("r_mix_k", "r_mix_v", "r_mix_r")]
        for n, m in enumerate(mixes):
            e.tensor_scalar(self.one_less[:, n:n + 1], m, -1.0, 1.0, ALU.mult, ALU.add).then_inc(*L.dve.mark(f"less{n}"))
        e.wait_ge(*L.dve("less2", b))
        for n, (m, s) in enumerate(zip(mixes, (self.xk, self.xv, self.xr))):
            e.tensor_scalar(self.t, self.xx[:, :], self.one_less[:, n:n + 1], None, ALU.mult).then_inc(*L.dve.mark(f"other{n}"))
            e.wait_ge(*L.dve(f"other{n}", b))
            e.scalar_tensor_tensor(s[:, :], M.h[:, :], m, self.t, ALU.mult, ALU.add).then_inc(*L.dve.mark(f"mixed{n}"))
            e.wait_ge(*L.dve(f"mixed{n}", b))
        e.wait_ge(*L.act("decay_col", b))
        e.tensor_scalar(self.decay[:, :], M.k("ones"), self.cols[:, 0:1], None, ALU.mult).then_inc(*L.dve.mark("decay"))
        e.wait_ge(*L.dve("decay", b))
        e.wait_ge(*L.act("ek", b))
        e.wait_ge(*L.pe("proj1", b))
        e.tensor_tensor(self.t, self.ek[:, :], M.ps[3][:, :], ALU.mult).then_inc(*L.dve.mark("ekv"))
        e.wait_ge(*L.dve("ekv", b))
        e.tensor_tensor_scan(self.sa, self.decay[:, :], self.t, 0.0, ALU.mult, ALU.add).then_inc(*L.dve.mark("scan_a"))
        e.tensor_tensor_scan(self.sb, self.decay[:, :], self.ek[:, :], 0.0, ALU.mult, ALU.add).then_inc(*L.dve.mark("scan_b"))
        e.wait_ge(*L.act("eku", b))
        e.wait_ge(*L.dve("scan_b", b))
        e.tensor_tensor(self.num, self.eku[:, :], M.ps[3][:, :], ALU.mult).then_inc(*L.dve.mark("num0"))
        e.tensor_copy(self.den, self.eku[:, :]).then_inc(*L.dve.mark("den0"))
        e.wait_ge(*L.dve("den0", b))
        e.tensor_tensor(self.num[:, 1:T], self.num[:, 1:T], self.sa[:, 0:T - 1], ALU.add).then_inc(*L.dve.mark("num"))
        e.tensor_tensor(self.den[:, 1:T], self.den[:, 1:T], self.sb[:, 0:T - 1], ALU.add).then_inc(*L.dve.mark("den"))
        e.wait_ge(*L.dve("den", b))
        e.reciprocal(self.t, self.den).then_inc(*L.dve.mark("inv"))
        e.wait_ge(*L.dve("inv", b))
        e.tensor_tensor(self.num, self.num, self.t, ALU.mult).then_inc(*L.dve.mark("wkv"))
        e.wait_ge(*L.dve("wkv", b))
        e.wait_ge(*L.act("sr", b))
        e.tensor_tensor(self.num, self.num, self.sr[:, :], ALU.mult).then_inc(*L.dve.mark("gated"))
        e.wait_ge(*L.pe("out", b))
        e.tensor_tensor(M.x[:, b, :], M.x[:, b, :], M.ps[5][:, :], ALU.add).then_inc(*L.dve.mark("residual"))


class Depth(Layer):
    def __init__(self, M):
        t, s = M.tile, M.small
        self.h_tok = t(0)
        self.onehot = t(1)[:, 0:NC * SLOTS].rearrange("p (c s) -> p c s", s=SLOTS)
        self.slot_tok = t(1)[0:SLOTS, 256:512], t(2)[0:SLOTS, :]
        self.slot_rows = t(2)
        self.cmp = t(3)
        self.row = t(4)
        self.keep = t(5)
        self.masks = M.wide[:, 0:4, :]
        self.seen = M.wide[:, 4, 0:NC * SLOTS].rearrange("p (c s) -> p c s", s=SLOTS)
        self.key_head = M.wide[:, 5:7, :].rearrange("p r t -> p (r t)").rearrange("p (h s) -> p h s", s=SLOTS)
        self.prob = M.wide[0:SLOTS, 7:9, :].rearrange("p r t -> p (r t)").rearrange("p (h s) -> p h s", s=SLOTS)
        self.prob_t = M.wide[:, 9, :]
        self.v_pair = M.wide[:, 10:12, :].rearrange("p r t -> p (r t)").rearrange("p (m f) -> p m f", f=C)
        n = lambda i: M.wide[:, 12 + i // 4, (i % 4) * P:(i % 4 + 1) * P]
        self.xs, self.hn, self.q, self.kk, self.v, self.o, self.x1, self.t1, self.t2, self.t3, self.cos, self.sin, self.ang, self.ws, self.y, self.m_sel, self.ang2 = (n(i) for i in range(17))
        self.mid = M.wide[:, 18, 0:NF * SLOTS]
        self.proc_tok = M.wide[0:SLOTS, 19, 0:C]
        self.weight, self.rank, self.tie, self.reach, self.kept = (s[:, 4 * i:4 * i + 4] for i in range(5))
        self.posf = s[:, 32:36]
        self.mx, self.den = s[0:SLOTS, 48:64], s[0:SLOTS, 64:80]
        self.both = s[:, 128:256]

    def sp(self, e, M, L, b):
        L.finished(e, b)
        e.dma_start(self.masks, M.D["mask"][:, bass.ts(b, 1), :, :].rearrange("p b c t -> p (b c) t")).then_inc(*L.dma.mark("mask"))

    def pe(self, e, M, L, b):
        S = SLOTS
        L.finished(e, b)
        norm_pe(e, M, L, b, "norm", M.x[:, b, :], [])
        e.wait_ge(*L.dve("norm", b))
        ident = M.k("ident")
        for c in range(NC):
            e.matmul(M.ps[2][:, c:c + 1], M.h[:, c * P:(c + 1) * P], M.w("m_router"), start=True, stop=True)
            mm = e.transpose(M.ps[3][:, c * P:(c + 1) * P], M.h[:, c * P:(c + 1) * P], ident)
        mm.then_inc(*L.pe.mark("router"))
        e.wait_ge(*L.dve("weight", b))
        for c in range(NC):
            mm = e.transpose(M.ps[4][:, c * P:(c + 1) * P], self.weight[:, c:c + 1].broadcast_to([P, P]), ident)
        mm.then_inc(*L.pe.mark("weight_row"))
        e.wait_ge(*L.dve("onehot3", b))
        e.wait_ge(*L.dve("kept", b))
        e.wait_ge(*L.dve("posf", b))
        e.wait_ge(*L.act("h_tok", b))
        for i, lhs in enumerate((lambda c: self.h_tok[:, c * P:(c + 1) * P], lambda c: self.posf[:, c:c + 1].broadcast_to([P, P]),
                                 lambda c: self.weight[:, c:c + 1].broadcast_to([P, P]))):
            for c in range(NC):
                mm = e.matmul(M.ps[5][:, i * S:(i + 1) * S], lhs(c), self.onehot[:, c, :], start=(c == 0), stop=(c == NC - 1))
        mm.then_inc(*L.pe.mark("gathered"))
        for c in range(NC):
            e.transpose(M.ps[6][0:S, c * P:(c + 1) * P], self.onehot[:, c, :], ident)
            mm = e.transpose(M.ps[7][:, c * P:(c + 1) * P], self.kept[:, c:c + 1].broadcast_to([P, P]), ident)
        mm.then_inc(*L.pe.mark("slot_rows"))
        e.wait_ge(*L.dma("mask", b))
        for d in range(NC):
            for c in range(NC):
                mm = e.matmul(M.ps[2][:, d * S:(d + 1) * S], self.masks[:, c, d * P:(d + 1) * P], self.onehot[:, c, :],
                              start=(c == 0), stop=(c == NC - 1))
        mm.then_inc(*L.pe.mark("mask_rows"))
        e.wait_ge(*L.act("mask_rows", b))
        for d in range(NC):
            mm = e.matmul(M.ps[3][0:S, 0:S], self.seen[:, d, :], self.onehot[:, d, :], start=(d == 0), stop=(d == NC - 1))
        mm.then_inc(*L.pe.mark("mask"))

        e.wait_ge(*L.act("sq1", b))
        e.matmul(M.ps[4][:, 0:S], M.k("mean"), self.t1[:, 0:S], start=True, stop=True).then_inc(*L.pe.mark("ms1"))
        e.wait_ge(*L.dve("hn_twice", b))
        for i, w in enumerate(("m_wq", "m_wqr", "m_wk", "m_wkr")):
            mm = e.matmul(M.ps[2][:, i * S:(i + 1) * S], M.w(w), self.hn[:, 0:S], start=True, stop=True)
        mm.then_inc(*L.pe.mark("qk"))
        e.matmul(M.ps[5][:, 256:384], self.hn, M.w("m_wv"), start=True, stop=True).then_inc(*L.pe.mark("v"))
        e.wait_ge(*L.dve("key_head", b))
        for i in range(2):
            mm = e.matmul(M.ps[i][0:S, :], self.q[:, 0:S], self.key_head[:, 8 * i:8 * i + 8, :], start=True, stop=True)
        mm.then_inc(*L.pe.mark("scores"))
        e.wait_ge(*L.dve("prob", b))
        for m in range(H // 2):
            mm = e.matmul(M.ps[4][:, m * S:(m + 1) * S], self.prob[:, 2 * m:2 * m + 2, :].rearrange("p h s -> p (h s)"), ident[0:S, 0:S],
                          start=True, stop=True)
        mm.then_inc(*L.pe.mark("prob_t"))
        e.wait_ge(*L.act("prob_t", b))
        e.wait_ge(*L.dve("v_pair", b))
        for m in range(H // 2):
            mm = e.matmul(M.ps[0][:, 0:S], self.v_pair[:, m, :], self.prob_t[:, m * S:(m + 1) * S], start=(m == 0), stop=(m == H // 2 - 1))
        mm.then_inc(*L.pe.mark("attended"))
        e.wait_ge(*L.act("o", b))
        e.matmul(M.ps[1][:, 0:S], M.w("m_wo"), self.o[:, 0:S], start=True, stop=True).then_inc(*L.pe.mark("out"))
        e.wait_ge(*L.act("sq2", b))
        e.matmul(M.ps[0][:, 64:64 + S], M.k("mean"), self.t1[:, 0:S], start=True, stop=True).then_inc(*L.pe.mark("ms2"))
        e.wait_ge(*L.dve("h2", b))
        for f in range(NF):
            mm = e.matmul(M.ps[2][:, f * S:(f + 1) * S], M.w("m_w1")[:, f * P:(f + 1) * P], self.hn[:, 0:S], start=True, stop=True)
        mm.then_inc(*L.pe.mark("up"))
        e.wait_ge(*L.act("gelu", b))
        for f in range(NF):
            mm = e.matmul(M.ps[1][:, 64:64 + S], M.w("m_w2")[:, f * P:(f + 1) * P], self.mid[:, f * S:(f + 1) * S], start=(f == 0), stop=(f == NF - 1))
        mm.then_inc(*L.pe.mark("down"))
        e.wait_ge(*L.dve("proc", b))
        e.matmul(M.ps[0][0:S, 128:256], self.y[:, 0:S], ident, start=True, stop=True).then_inc(*L.pe.mark("proc_tok"))
        e.wait_ge(*L.act("proc_tok", b))
        e.wait_ge(*L.act("slot_rows", b))
        e.matmul(M.ps[4][:, :], self.proc_tok[0:S - 1, :], self.slot_rows[0:S - 1, :], start=True, stop=True).then_inc(*L.pe.mark("scattered"))

    def act(self, e, M, L, b):
        S = SLOTS
        L.finished(e, b)
        norm_act(e, M, L, b, "norm")
        e.wait_ge(*L.pe("router", b))
        e.activation(self.h_tok, M.ps[3][:, :], ACT.Copy).then_inc(*L.act.mark("h_tok"))
        e.wait_ge(*L.pe("weight_row", b))
        e.activation(self.row, M.ps[4][:, :], ACT.Copy).then_inc(*L.act.mark("weight_row"))
        e.wait_ge(*L.pe("slot_rows", b))
        e.activation(self.slot_rows[0:S, :], M.ps[6][0:S, :], ACT.Copy).then_inc(*L.act.mark("slot_rows"))
        e.wait_ge(*L.pe("mask_rows", b))
        e.activation(self.seen.rearrange("p c s -> p (c s)"), M.ps[2][:, 0:NC * S], ACT.Copy).then_inc(*L.act.mark("mask_rows"))
        e.wait_ge(*L.dve("xs", b))
        e.activation(self.t1[:, 0:S], self.xs[:, 0:S], ACT.Square).then_inc(*L.act.mark("sq1"))
        e.wait_ge(*L.pe("ms1", b))
        e.activation(self.t2[:, 0:S], M.ps[4][:, 0:S], ACT.Sqrt, bias=M.k("eps6")).then_inc(*L.act.mark("sd1"))
        e.wait_ge(*L.dve("reduced1", b))
        e.activation(self.sin[:, 0:S], self.ang[:, 0:S], ACT.Sin).then_inc(*L.act.mark("sin"))
        e.activation(self.cos[:, 0:S], self.ang2[:, 0:S], ACT.Sin).then_inc(*L.act.mark("cos"))
        e.wait_ge(*L.dve("centred", b))
        e.activation(self.prob.rearrange("p h s -> p (h s)"), self.prob.rearrange("p h s -> p (h s)"), ACT.Exp).then_inc(*L.act.mark("exp"))
        e.wait_ge(*L.pe("prob_t", b))
        e.activation(self.prob_t, M.ps[4][:, :], ACT.Copy).then_inc(*L.act.mark("prob_t"))
        e.wait_ge(*L.pe("attended", b))
        e.activation(self.o[:, 0:S], M.ps[0][:, 0:S], ACT.Copy).then_inc(*L.act.mark("o"))
        e.wait_ge(*L.dve("x1", b))
        e.activation(self.t1[:, 0:S], self.x1[:, 0:S], ACT.Square).then_inc(*L.act.mark("sq2"))
        e.wait_ge(*L.pe("ms2", b))
        e.activation(self.t2[:, 0:S], M.ps[0][:, 64:64 + S], ACT.Sqrt, bias=M.k("eps6")).then_inc(*L.act.mark("sd2"))
        e.wait_ge(*L.pe("up", b))
        e.activation(self.mid, M.ps[2][:, 0:NF * S], ACT.Gelu_apprx_tanh).then_inc(*L.act.mark("gelu"))
        e.wait_ge(*L.pe("proc_tok", b))
        e.activation(self.proc_tok, M.ps[0][0:S, 128:256], ACT.Copy).then_inc(*L.act.mark("proc_tok"))

    def dve(self, e, M, L, b):
        S = SLOTS
        L.finished(e, b)

        def step(name, ins, wait=True):
            ins.then_inc(*L.dve.mark(name))
            if wait:
                e.wait_ge(*L.dve(name, b))

        norm_dve(e, M, L, b, "norm", M.x[:, b, :], M.h[:, :])
        step("posf", e.tensor_copy(self.posf, M.pos[:, bass.ts(b, NC)]), False)
        e.wait_ge(*L.pe("router", b))
        step("weight", e.tensor_scalar(self.weight, M.ps[2][:, 0:NC], M.w("m_router_b"), None, ALU.add))
        e.wait_ge(*L.act("weight_row", b))
        for c in range(NC):
            w = self.weight[:, c:c + 1]
            before = M.k("before")[:, (NC - 1 - c) * P:(NC - 1 - c) * P + T]
            step(f"more{c}", e.scalar_tensor_tensor(self.cmp, self.row, w, M.k("ones"), ALU.is_gt, ALU.mult, accum_out=self.rank[:, c:c + 1]))
            step(f"tie{c}", e.scalar_tensor_tensor(self.cmp, self.row, w, before, ALU.is_equal, ALU.mult, accum_out=self.tie[:, c:c + 1]))
            step(f"reach{c}", e.scalar_tensor_tensor(self.cmp, self.row, w, M.k("ones"), ALU.is_ge, ALU.mult, accum_out=self.reach[:, c:c + 1]))
        step("rank", e.tensor_tensor(self.rank, self.rank, self.tie, ALU.add))
        step("kept", e.tensor_scalar(self.kept, self.reach, SLOTS - 0.5, None, ALU.is_gt), False)
        for c in range(NC):
            step(f"onehot{c}", e.tensor_scalar(self.onehot[:, c, :], M.k("slot"), self.rank[:, c:c + 1], None, ALU.is_equal), False)
        e.wait_ge(*L.pe("gathered", b))
        step("xs", e.tensor_copy(self.xs[:, 0:S], M.ps[5][:, 0:S]), False)
        step("ws", e.tensor_copy(self.ws[:, 0:S], M.ps[5][:, 2 * S:3 * S]), False)
        step("angle", e.tensor_scalar(self.t3[:, 0:S], M.ps[5][:, S:2 * S], M.k("mod_inv"), None, ALU.mult))
        for i, (dst, quarter) in enumerate(((self.ang2, 0.25), (self.ang, 0.0))):
            a = dst[:, 0:S]
            tmp = self.v[:, 0:S]
            step(f"turns{i}", e.tensor_scalar(tmp, self.t3[:, 0:S], 1.0 / (2 * np.pi), quarter, ALU.mult, ALU.add))
            step(f"round_up{i}", e.tensor_scalar(tmp, tmp, 12582912.0, None, ALU.add))
            step(f"round{i}", e.tensor_scalar(tmp, tmp, 12582912.0, None, ALU.subtract))
            src = self.t3[:, 0:S]
            for j, part in enumerate(TWO_PI):
                step(f"part{i}{j}", e.scalar_tensor_tensor(a, tmp, -part, src, ALU.mult, ALU.add))
                src = a
            if quarter:
                step(f"quarter{i}", e.tensor_scalar(a, a, float(np.pi / 2), None, ALU.add))
            step(f"reduced{i}", e.tensor_scalar(a, a, PI_BELOW, -PI_BELOW, ALU.min, ALU.max))
        e.wait_ge(*L.act("sd1", b))
        step("rms1", e.reciprocal(self.t3[:, 0:S], self.t2[:, 0:S]))
        step("hn", e.scalar_tensor_tensor(self.hn[:, 0:S], self.xs[:, 0:S], M.w("m_ln1"), self.t3[:, 0:S], ALU.mult, ALU.mult))
        step("hn_twice", e.tensor_copy(self.hn[:, S:2 * S], self.hn[:, 0:S]))
        e.wait_ge(*L.act("cos", b))
        step("signed", e.tensor_scalar(self.sin[:, 0:S], self.sin[:, 0:S], M.k("mod_sign"), None, ALU.mult))
        e.wait_ge(*L.pe("qk", b))
        for i, dst in enumerate((self.q, self.kk)):
            step(f"rope_a{i}", e.tensor_tensor(self.t2[:, 0:S], M.ps[2][:, 2 * i * S:(2 * i + 1) * S], self.cos[:, 0:S], ALU.mult))
            step(f"rope_b{i}", e.tensor_tensor(self.t3[:, 0:S], M.ps[2][:, (2 * i + 1) * S:(2 * i + 2) * S], self.sin[:, 0:S], ALU.mult))
            step(f"rope{i}", e.tensor_tensor(dst[:, 0:S], self.t2[:, 0:S], self.t3[:, 0:S], ALU.add))
        step("key_head", e.tensor_tensor(self.key_head, self.kk[:, 0:S].unsqueeze(1).broadcast_to([P, H, S]),
                                         M.k("head").unsqueeze(2).broadcast_to([P, H, S]), ALU.mult))
        e.wait_ge(*L.pe("v", b))
        step("v_pair", e.tensor_tensor(self.v_pair, M.k("head_of_pair").rearrange("p (m f) -> p m f", f=C),
                                       M.ps[5][:, 256:384].unsqueeze(1).broadcast_to([P, H // 2, C]), ALU.mult), False)
        e.wait_ge(*L.pe("mask", b))
        ms = self.m_sel[0:S, 0:S]
        step("mask", e.tensor_tensor(ms, M.ps[3][0:S, 0:S], M.k("last_slot")[0:S, :], ALU.add))
        e.wait_ge(*L.pe("scores", b))
        for i in range(2):
            step(f"masked{i}", e.scalar_tensor_tensor(self.prob[:, 8 * i:8 * i + 8, :], M.ps[i][0:S, :].rearrange("p (h s) -> p h s", s=S),
                                                      float(1.0 / np.sqrt(DH)), ms.unsqueeze(1).broadcast_to([S, 8, S]), ALU.mult, ALU.add))
        wide = lambda a: a.unsqueeze(2).broadcast_to([S, H, S])
        step("max", e.tensor_reduce(self.mx, self.prob, AX, ALU.max))
        step("centred", e.tensor_tensor(self.prob, self.prob, wide(self.mx), ALU.subtract))
        e.wait_ge(*L.act("exp", b))
        step("sum", e.tensor_reduce(self.den, self.prob, AX, ALU.add))
        step("inv_sum", e.reciprocal(self.den, self.den))
        step("prob", e.tensor_tensor(self.prob, self.prob, wide(self.den), ALU.mult), False)
        e.wait_ge(*L.pe("out", b))
        step("x1", e.tensor_tensor(self.x1[:, 0:S], self.xs[:, 0:S], M.ps[1][:, 0:S], ALU.add))
        e.wait_ge(*L.act("sd2", b))
        step("rms2", e.reciprocal(self.t3[:, 0:S], self.t2[:, 0:S]))
        step("h2", e.scalar_tensor_tensor(self.hn[:, 0:S], self.x1[:, 0:S], M.w("m_ln2"), self.t3[:, 0:S], ALU.mult, ALU.mult))
        e.wait_ge(*L.pe("down", b))
        step("x2", e.tensor_tensor(self.y[:, 0:S], self.x1[:, 0:S], M.ps[1][:, 64:64 + S], ALU.add))
        step("proc", e.tensor_tensor(self.y[:, 0:S], self.y[:, 0:S], self.ws[:, 0:S], ALU.mult), False)
        step("keep", e.tensor_tensor(self.keep, M.h[:, :], M.ps[7][:, :], ALU.mult))
        step("rest", e.tensor_tensor(self.keep, self.keep, M.x[:, b, :], ALU.add))
        e.wait_ge(*L.pe("scattered", b))
        step("residual", e.tensor_tensor(M.x[:, b, :], self.keep, M.ps[4][:, :], ALU.add), False)


class TokenAttention(Layer):
    SCALE = 1.0 / 8.0
    RING = 3

    def __init__(self, M):
        t, w, big, s = M.tile, M.wide, M.big, M.small
        self.q = [t(i) for i in range(4)]
        self.mix = M.tiles[:, 4:8, :]
        self.k, self.v_even, self.v_odd = t(8), t(9), t(10)
        self.prob = [t(11), w[:, 16, :], w[:, 17, :]]
        self.v_block, self.comp_t = w[:, 18, :], w[:, 19, :]
        self.prob_t = [w[:, 8 * i:8 * i + 8, :].rearrange("p a t -> p (a t)").rearrange("p (j o m q) -> p j o m q", j=4, o=2, m=4) for i in range(2)]
        self.band = [big[:, 260 * i:260 * i + 257] for i in range(3)]
        self.comp = big[:, 1024:1024 + 544].rearrange("p (s n) -> p s n", n=17)
        self.comp_p = big[:, 1568:2080]
        self.g = big[:, 2080:2176].rearrange("p (s n) -> p s n", n=3)
        self.t = [big[:, 5 * T:6 * T], big[:, 6 * T:7 * T]]
        self.t2, self.v_twice = big[:, 7 * T:8 * T], big[:, 8 * T:9 * T]
        self.low = big[:, 2560 - 384:2560]
        self.kcw = s[:, 0:32]
        self.sink = s[:, 32:40]
        self.cm, self.cd, self.gs = s[:, 64:96], s[:, 96:128], s[:, 128:160]
        self.stat = [s[:, 160 + 16 * i:176 + 16 * i] for i in range(3)]

    def before(self, e, M, which, sem):
        if which == "pool":
            e.memset(self.v_even, 0.0).then_inc(sem, 1)
            e.memset(self.v_odd, 0.0).then_inc(sem, 1)
        if which in ("pe", "act"):
            e.wait_ge(sem, 2)

    STEPS = [(c, h) for c in range(NC) for h in range(A_H)]

    def pe(self, e, M, L, b):
        L.finished(e, b)
        norm_pe(e, M, L, b, "norm", M.x[:, b, :], [])
        e.wait_ge(*L.dve("norm", b))
        e.matmul(M.ps[6][0:A_QC, :], M.w("a_w_qc"), M.h[:, :], start=True, stop=True).then_inc(*L.pe.mark("qc"))
        for c in range(NC):
            mm = e.matmul(M.ps[7][:, c * P:(c + 1) * P], M.h[:, c * P:(c + 1) * P], M.w("a_w_v"), start=True, stop=True)
        mm.then_inc(*L.pe.mark("v"))
        for u in range(5):
            if u == 1:
                e.wait_ge(*L.act("qc", b))
            if u >= 2:
                e.wait_ge(*L.dve(f"roped{u - 2}", b))
            for n, (wk, wq) in enumerate((("a_w_k", "a_w_q"), ("a_w_kr", "a_w_qr"))):
                if u == 0:
                    mm = e.matmul(M.ps[n][:, :], M.w(wk), M.h[:, :], start=True, stop=True)
                else:
                    mm = e.matmul(M.ps[2 * (u % 2) + n][:, :], M.w(wq, A_QC)[:, (u - 1) * P:u * P], self.qc_sb(M), start=True, stop=True)
            mm.then_inc(*L.pe.mark(f"raw{u}"))
            if u >= 1:
                self.pe_ms(e, M, L, b, u - 1)
        self.pe_ms(e, M, L, b, 4)
        e.wait_ge(*L.act("v_twice", b))
        for c in range(NC):
            mm = e.matmul(M.ps[6][:, 0:P], M.k("block_mean")[:, c * P:(c + 1) * P], self.v_twice[:, c * P:(c + 1) * P], start=(c == 0), stop=(c == NC - 1))
        mm.then_inc(*L.pe.mark("v_block"))
        e.wait_ge(*L.dve("kcw", b))
        e.wait_ge(*L.dve("normed4", b))
        for c, h in self.STEPS:
            rows = slice(64 * (h % 2), 64 * (h % 2) + 64)
            at = (c * 4 + h // 2) * 32
            mm = e.matmul(M.ps[(3, 7)[h % 2]][:, at:at + 19],
                          self.q[h // 2][rows, c * P:(c + 1) * P], self.kcw[rows, 0:19], start=True, stop=True)
        mm.then_inc(*L.pe.mark("block_scores"))
        n = len(self.STEPS)
        for s in range(n + 2):
            if s < n:
                c, h = self.STEPS[s]
                rows = slice(64 * (h % 2), 64 * (h % 2) + 64)
                if s >= self.RING:
                    e.wait_ge(*L.dve(f"window{s - self.RING}", b))
                e.matmul(M.ps[s % 3][:, 0:(c + 1) * P], self.q[h // 2][rows, c * P:(c + 1) * P], self.k[rows, 0:(c + 1) * P],
                         start=True, stop=True).then_inc(*L.pe.mark(f"scores{s}"))
            if s == 4:
                e.wait_ge(*L.dve("comp_p", b))
                for c in range(NC):
                    mm = e.transpose(M.ps[3][:, c * P:(c + 1) * P], self.comp_p[:, c * P:(c + 1) * P], M.k("ident"))
                mm.then_inc(*L.pe.mark("comp_t"))
            if s >= 2:
                r = s - 2
                c, h = self.STEPS[r]
                e.wait_ge(*L.dve(f"mixed{r}", b))
                if r >= 2:
                    e.wait_ge(*L.act(f"turned{r - 2}", b))
                for j in range(c + 1):
                    mm = e.transpose(M.ps[4 + r % 2][:, j * P:(j + 1) * P], self.prob[r % 3][:, j * P:(j + 1) * P], M.k("ident"))
                mm.then_inc(*L.pe.mark(f"turned{r}"))
                if h == A_H - 1:
                    self.pe_values(e, M, L, b, c)
        e.wait_ge(*L.act(f"mix{NC - 1}", b))
        for m in range(4):
            mm = e.matmul(M.ps[0][:, :], M.w("a_w_group")[:, m * P:(m + 1) * P], self.mix[:, m, :], start=(m == 0), stop=(m == 3))
        mm.then_inc(*L.pe.mark("grouped"))
        e.wait_ge(*L.act("grouped", b))
        e.matmul(M.ps[1][:, :], M.w("a_w_out"), M.sq[:, :], start=True, stop=True).then_inc(*L.pe.mark("out"))

    def qc_sb(self, M):
        return M.h2[0:A_QC, :]

    def pe_ms(self, e, M, L, b, u):
        e.wait_ge(*L.act(f"square{u}", b))
        if u >= 2:
            e.wait_ge(*L.act(f"sd{u - 2}", b))
        e.matmul(M.ps[4 + u % 2][:, :], M.k("mean64"), M.sq[:, :], start=True, stop=True).then_inc(*L.pe.mark(f"ms{u}"))

    def pe_values(self, e, M, L, b, c):
        e.wait_ge(*L.act(f"turned{c * A_H + A_H - 1}", b))
        if c == 0:
            e.wait_ge(*L.act("comp_t", b))
            e.wait_ge(*L.dve("v_block", b))
        else:
            e.wait_ge(*L.act(f"mix{c - 1}", b))
        for j in range(c + 1):
            for o, v in enumerate((self.v_even, self.v_odd)):
                e.matmul(M.ps[6][:, :], v[:, j * P:(j + 1) * P], self.prob_t[c % 2][:, j, o, :, :], start=(j == 0 and o == 0), stop=False,
                         skip_group_check=True)
        for m in range(4):
            mm = e.matmul(M.ps[6][:, m * P:(m + 1) * P], self.v_block[:, m * P:(m + 1) * P], self.comp_t[:, c * P:(c + 1) * P],
                          start=False, stop=(m == 3), skip_group_check=True)
        mm.then_inc(*L.pe.mark(f"values{c}"))

    def act(self, e, M, L, b):
        L.finished(e, b)
        norm_act(e, M, L, b, "norm")
        e.wait_ge(*L.pe("qc", b))
        e.activation(self.qc_sb(M), M.ps[6][0:A_QC, :], ACT.Copy).then_inc(*L.act.mark("qc"))
        e.wait_ge(*L.pe("v", b))
        v = M.ps[7][:, :].rearrange("p (c d) -> p c d", d=P)
        for dst, lo in ((self.v_even, 0), (self.v_odd, A_D)):
            e.activation(dst.rearrange("p (c d) -> p c d", d=P)[:, :, lo:lo + A_D], v[:, :, lo:lo + A_D], ACT.Copy).then_inc(*L.act.mark(f"v{lo}"))
        e.activation(self.v_twice, M.ps[7][:, :], ACT.Copy).then_inc(*L.act.mark("v_twice"))
        for u in range(6):
            if u < 5:
                e.wait_ge(*L.dve(f"roped{u}", b))
                if u >= 1:
                    e.wait_ge(*L.pe(f"ms{u - 1}", b))
                e.activation(M.sq[:, :], self.t[u % 2], ACT.Square).then_inc(*L.act.mark(f"square{u}"))
            if u >= 1:
                e.wait_ge(*L.pe(f"ms{u - 1}", b))
                if u >= 2:
                    e.wait_ge(*L.dve(f"inv{u - 2}", b))
                e.activation(M.sd[:, :], M.ps[4 + (u - 1) % 2][:, :], ACT.Sqrt, bias=M.k("eps6")).then_inc(*L.act.mark(f"sd{u - 1}"))
        e.wait_ge(*L.dve("gate_in", b))
        e.activation(self.g, self.g, ACT.Exp, scale=-1.0).then_inc(*L.act.mark("gate_exp"))
        e.wait_ge(*L.dve("comp_c", b))
        e.activation(self.comp, self.comp, ACT.Exp, scale=self.SCALE).then_inc(*L.act.mark("comp_exp"))
        n = len(self.STEPS)
        for s in range(n + 2):
            if s < n:
                c, h = self.STEPS[s]
                st, W, bw = self.stat[s % 3], (c + 1) * P, min(c + 1, 2) * P
                e.wait_ge(*L.dve(f"bias{s}", b))
                e.activation(self.prob[s % 3][:, 0:W], self.prob[s % 3][:, 0:W], ACT.Exp, bias=st[:, 2:3], scale=self.SCALE,
                             accum_out=st[:, 4:5]).then_inc(*L.act.mark(f"exp{s}"))
                e.activation(self.band[s % 3][:, 256 - bw:257], self.band[s % 3][:, 256 - bw:257], ACT.Exp, bias=st[:, 3:4], scale=self.SCALE,
                             accum_out=st[:, 5:6]).then_inc(*L.act.mark(f"exp_window{s}"))
            if s == 5:
                e.wait_ge(*L.pe("comp_t", b))
                e.activation(self.comp_t, M.ps[3][:, :], ACT.Copy).then_inc(*L.act.mark("comp_t"))
            if s >= 2:
                r = s - 2
                c, h = self.STEPS[r]
                e.wait_ge(*L.pe(f"turned{r}", b))
                if c >= 2 and h == 0:
                    e.wait_ge(*L.pe(f"values{c - 2}", b))
                e.activation(self.prob_t[c % 2][:, 0:c + 1, h % 2, h // 2, :], M.ps[4 + r % 2][:, 0:(c + 1) * P].rearrange("p (j q) -> p j q", q=P),
                             ACT.Copy).then_inc(*L.act.mark(f"turned{r}"))
                if h == A_H - 1:
                    e.wait_ge(*L.pe(f"values{c}", b))
                    e.activation(self.mix[:, :, c * P:(c + 1) * P], M.ps[6][:, :].rearrange("p (m q) -> p m q", q=P), ACT.Copy)\
                        .then_inc(*L.act.mark(f"mix{c}"))
        e.wait_ge(*L.pe("grouped", b))
        e.activation(M.sq[:, :], M.ps[0][:, :], ACT.Copy).then_inc(*L.act.mark("grouped"))

    def dve(self, e, M, L, b):
        L.finished(e, b)

        def step(name, ins, wait=True):
            ins.then_inc(*L.dve.mark(name))
            if wait:
                e.wait_ge(*L.dve(name, b))

        norm_dve(e, M, L, b, "norm", M.x[:, b, :], M.h[:, :])
        step("sink", e.tensor_scalar(self.sink, M.w("a_sink"), 1.0 / self.SCALE, None, ALU.mult), False)
        step("gate_w", e.tensor_copy(self.kcw[:, 16:19], M.w("a_w_gate")), False)
        for u in range(6):
            if u < 5:
                t = self.t[u % 2]
                e.wait_ge(*L.pe(f"raw{u}", b))
                step(f"rope_a{u}", e.tensor_tensor(t, M.ps[2 * (u % 2)][:, :], M.k("rope_cos"), ALU.mult), False)
                step(f"rope_b{u}", e.tensor_tensor(self.t2, M.ps[2 * (u % 2) + 1][:, :], M.k("rope_sin"), ALU.mult))
                step(f"roped{u}", e.tensor_tensor(t, t, self.t2, ALU.add))
            if u >= 1:
                v = u - 1
                e.wait_ge(*L.act(f"sd{v}", b))
                step(f"inv{v}", e.reciprocal(M.rs[:, :], M.sd[:, :]))
                dst, g = (self.k, "a_gk") if v == 0 else (self.q[v - 1], "a_gq")
                step(f"normed{v}", e.scalar_tensor_tensor(dst, self.t[v % 2], M.w(g), M.rs[:, :], ALU.mult, ALU.mult))
            if u == 1:
                step("k_sum", e.tensor_reduce(self.kcw[:, 0:16], self.k.rearrange("p (n r) -> p n r", r=A_CR), AX, ALU.add))
                step("kcw", e.tensor_scalar(self.kcw[:, 0:16], self.kcw[:, 0:16], 1.0 / A_CR, None, ALU.mult))
        e.wait_ge(*L.pe("v_block", b))
        step("v_block", e.tensor_tensor(self.v_block.rearrange("p (m f) -> p m f", f=P), M.k("head_of_block").rearrange("p (m f) -> p m f", f=P),
                                        M.ps[6][:, 0:P].unsqueeze(1).broadcast_to([P, 4, P]), ALU.mult), False)
        e.wait_ge(*L.pe("block_scores", b))
        seen = M.k("blocks_seen").rearrange("p (c n) -> p c n", n=A_NB)
        gate = M.w("a_b_gate").rearrange("p (h n) -> p h n", n=3)[:, 0:4, :]
        for o, bank in enumerate((3, 7)):
            raw = M.ps[bank][:, :].rearrange("p (c m n) -> p c m n", m=4, n=32)
            comp = self.comp.rearrange("p (c m o) n -> p c m o n", m=4, o=2)[:, :, :, o, :]
            gates = self.g.rearrange("p (c m o) n -> p c m o n", m=4, o=2)[:, :, :, o, :]
            for c in range(NC):
                step(f"comp_raw{o}{c}", e.tensor_tensor(comp[:, c, :, 0:16], raw[:, c, :, 0:16], seen[:, c, :].unsqueeze(1).broadcast_to([P, 4, A_NB]), ALU.add), False)
                step(f"gate_in{o}{c}", e.tensor_tensor(gates[:, c, :, :], raw[:, c, :, 16:19], gate, ALU.add), False)
        step("gate_in", e.tensor_copy(self.comp.rearrange("p (c h) n -> p c h n", h=A_H)[:, :, :, 16],
                                      self.sink.unsqueeze(1).broadcast_to([P, NC, A_H])))
        wide = lambda a, n: a.unsqueeze(2).broadcast_to([P, NC * A_H, n])
        step("comp_max", e.tensor_reduce(self.cm, self.comp, AX, ALU.max))
        step("comp_c", e.tensor_tensor(self.comp, self.comp, wide(self.cm, 17), ALU.subtract), False)
        e.wait_ge(*L.act("gate_exp", b))
        step("gate_1", e.tensor_scalar(self.g, self.g, 1.0, None, ALU.add))
        step("gate_s", e.reciprocal(self.g, self.g))
        step("gate_sum", e.tensor_reduce(self.gs, self.g, AX, ALU.add))
        step("gate_clip", e.tensor_scalar(self.gs, self.gs, 1e-6, None, ALU.max))
        step("gate_inv", e.reciprocal(self.gs, self.gs))
        step("gates", e.tensor_tensor(self.g, self.g, wide(self.gs, 3), ALU.mult))
        e.wait_ge(*L.act("comp_exp", b))
        step("comp_sum", e.tensor_reduce(self.cd, self.comp, AX, ALU.add))
        step("comp_inv", e.reciprocal(self.cd, self.cd))
        step("comp_coef", e.tensor_tensor(self.cd, self.cd, self.g[:, :, 0], ALU.mult))
        step("comp_p", e.tensor_tensor(self.comp_p.rearrange("p (s n) -> p s n", n=A_NB), self.comp[:, :, 0:16], wide(self.cd, 16), ALU.mult), False)
        n = len(self.STEPS)
        for s in range(n + 1):
            if s < n:
                c, h = self.STEPS[s]
                st, W, bw = self.stat[s % 3], (c + 1) * P, min(c + 1, 2) * P
                S, pr, bd = M.ps[s % 3], self.prob[s % 3], self.band[s % 3]
                e.wait_ge(*L.pe(f"scores{s}", b))
                if s >= self.RING:
                    e.wait_ge(*L.pe(f"turned{s - self.RING}", b))
                step(f"window_sink{s}", e.tensor_copy(bd[:, 256:257], self.sink[:, h:h + 1]), False)
                step(f"all{s}", e.tensor_tensor_reduce(pr[:, 0:W], S[:, 0:W], M.k("causal")[:, T - W:T], 1.0, 3.0 * NEG, ALU.add, ALU.max, st[:, 0:1]), False)
                step(f"window{s}", e.tensor_tensor_reduce(bd[:, 256 - bw:256], S[:, W - bw:W], M.k("band")[:, 256 - bw:256], 1.0, self.sink[:, h:h + 1],
                                                          ALU.add, ALU.max, st[:, 1:2]))
                step(f"bias{s}", e.tensor_scalar(st[:, 2:4], st[:, 0:2], -self.SCALE, None, ALU.mult), False)
            if s >= 1:
                r = s - 1
                c, h = self.STEPS[r]
                st, W, bw = self.stat[r % 3], (c + 1) * P, min(c + 1, 2) * P
                pr, bd = self.prob[r % 3], self.band[r % 3]
                e.wait_ge(*L.act(f"exp_window{r}", b))
                step(f"inv_sum{r}", e.reciprocal(st[:, 6:8], st[:, 4:6]))
                step(f"coef{r}", e.tensor_tensor(st[:, 6:8], st[:, 6:8], self.g[:, r, 1:3], ALU.mult))
                step(f"scaled{r}", e.tensor_scalar(pr[:, 0:W], pr[:, 0:W], st[:, 6:7], None, ALU.mult))
                step(f"mixed{r}", e.scalar_tensor_tensor(pr[:, W - bw:W], bd[:, 256 - bw:256], st[:, 7:8], pr[:, W - bw:W], ALU.mult, ALU.add), False)
        e.wait_ge(*L.pe("out", b))
        step("residual", e.tensor_tensor(M.x[:, b, :], M.x[:, b, :], M.ps[1][:, :], ALU.add), False)


class BlockProject(Layer):
    def __init__(self, M):
        self.rows = M.wide[:, 0:3, :].rearrange("p a t -> p (a t)").rearrange("p (c n) -> p c n", c=NC)

    def pe(self, e, M, L, b):
        L.finished(e, b)
        norm_pe(e, M, L, b, "norm", M.x[:, b, :], [])
        e.wait_ge(*L.dve("norm", b))
        for c in range(NC):
            e.matmul(M.ps[2 + c][:, 0:3 * C], M.h[:, c * P:(c + 1) * P], M.w("b_w"), start=True, stop=True).then_inc(*L.pe.mark(f"qkv{c}"))

    def act(self, e, M, L, b):
        L.finished(e, b)
        norm_act(e, M, L, b, "norm")
        e.wait_ge(*L.dve(f"rows{NC - 1}", b))
        e.dma_start(M.D["qkv"][bass.ts(b, T), :].rearrange("(c p) n -> p c n", p=P), self.rows).then_inc(*L.dma.mark("store"))

    def dve(self, e, M, L, b):
        L.finished(e, b)
        norm_dve(e, M, L, b, "norm", M.x[:, b, :], M.h[:, :])
        for c in range(NC):
            e.wait_ge(*L.pe(f"qkv{c}", b))
            e.tensor_tensor(self.rows[:, c, :], M.ps[2 + c][:, 0:3 * C], M.w("b_b"), ALU.add).then_inc(*L.dve.mark(f"rows{c}"))


class BlockAttend(Layer):
    turns = 1
    POOL_PRODUCTS = 2

    def __init__(self, M):
        self.qkv = M.tiles[:, :, :].rearrange("p a t -> p (a t)").rearrange("p (t n) -> p t n", t=GROUP)
        join = lambda lo, hi: M.wide[:, lo:hi, :].rearrange("p a t -> p (a t)")
        self.prod = [join(0, 4), join(4, 8), M.big[:, 0:2048], M.big[:, 2048:4096]]
        self.s = join(8, 16).rearrange("p (q k h) -> p q k h", q=GROUP, k=GROUP)
        self.out = join(16, 20).rearrange("p (h q d) -> p h q d", q=GROUP, d=DH)
        self.mx, self.den = (M.small[:, 256 * i:256 * (i + 1)].rearrange("p (q h) -> p q h", h=H) for i in range(2))

    def before(self, e, M, which, sem):
        if which == "sp":
            e.dma_start(self.qkv, M.D["qkv"].rearrange("(p t) n -> p t n", t=GROUP)).then_inc(sem, 16)
        if which in ("pool", "dve"):
            e.wait_ge(sem, 16)

    def on_pool(self, i):
        return i % 5 in (1, 3)

    def product(self, e, kind, i):
        q = i
        out = self.prod[i % 4]
        K, V = self.qkv[:, :, C:2 * C], self.qkv[:, :, 2 * C:3 * C]
        if kind == "score":
            return e.tensor_tensor(out.rearrange("p (k f) -> p k f", f=C), K, self.qkv[:, q, 0:C].unsqueeze(1).broadcast_to([P, GROUP, C]), ALU.mult)
        return e.tensor_tensor(out.rearrange("p (k h d) -> p k h d", h=H, d=DH), V.rearrange("p k (h d) -> p k h d", d=DH),
                               self.s[:, q, :, :].unsqueeze(3).broadcast_to([P, GROUP, H, DH]), ALU.mult)

    def pool(self, e, M, L, b):
        for kind in ("score", "value"):
            if kind == "value":
                e.wait_ge(*L.dve("prob", b))
            for i in range(GROUP):
                if self.on_pool(i):
                    if i >= 4:
                        e.wait_ge(*L.dve(f"{kind}_sum{i - 4}", b))
                    self.product(e, kind, i).then_inc(*L.pool.mark(f"{kind}{i}"))

    def dve(self, e, M, L, b):
        def step(name, ins):
            ins.then_inc(*L.dve.mark(name))
            e.wait_ge(*L.dve(name, b))

        def products(kind):
            for i in range(GROUP):
                if self.on_pool(i):
                    e.wait_ge(*L.pool(f"{kind}{i}", b))
                else:
                    step(f"{kind}{i}", self.product(e, kind, i))
                if kind == "score":
                    ins = e.tensor_reduce(self.s[:, i, :, :], self.prod[i % 4].rearrange("p (k h d) -> p k h d", h=H, d=DH), AX, ALU.add)
                else:
                    ins = e.tensor_reduce(self.out[:, :, i, :], self.prod[i % 4].rearrange("p (k h d) -> p h d k", h=H, d=DH), AX, ALU.add)
                ins.then_inc(*L.dve.mark(f"{kind}_sum{i}"))

        products("score")
        e.wait_ge(*L.dve(f"score_sum{GROUP - 1}", b))
        over_k = self.s.rearrange("p q k h -> p q h k")
        wide = lambda a: a.unsqueeze(2).broadcast_to([P, GROUP, GROUP, H])
        step("max", e.tensor_reduce(self.mx, over_k, AX, ALU.max))
        step("centred", e.tensor_tensor(self.s, self.s, wide(self.mx), ALU.subtract))
        e.wait_ge(*L.act("exp", b))
        step("sum", e.tensor_reduce(self.den, over_k, AX, ALU.add))
        step("inv", e.reciprocal(self.den, self.den))
        step("prob", e.tensor_tensor(self.s, self.s, wide(self.den), ALU.mult))
        products("value")

    def act(self, e, M, L, b):
        e.wait_ge(*L.dve("centred", b))
        flat = self.s.rearrange("p q k h -> p (q k h)")
        e.activation(flat, flat, ACT.Exp, scale=float(1.0 / np.sqrt(DH))).then_inc(*L.act.mark("exp"))

    def sp(self, e, M, L, b):
        e.wait_ge(*L.dve(f"value_sum{GROUP - 1}", b))
        rows = M.D["attended"].rearrange("(b h j) f -> b j h f", b=B, h=H)
        runs = T // GROUP
        for n in range(B):
            e.dma_start(rows[n], self.out[n * runs:(n + 1) * runs, :, :, :].rearrange("p h q d -> p h (q d)")).then_inc(*L.dma.mark(f"store{n}"))


class BlockMerge(Layer):
    def __init__(self, M):
        self.rows = M.tile(0)

    def act(self, e, M, L, b):
        L.finished(e, b)
        e.dma_start(self.rows.rearrange("p (c f) -> p c f", c=NC), M.D["attended"][bass.ts(b, T), :].rearrange("(c p) f -> p c f", p=P))\
            .then_inc(*L.dma.mark("load"))

    def pe(self, e, M, L, b):
        L.finished(e, b)
        e.wait_ge(*L.dma("load", b))
        for c in range(NC):
            mm = e.transpose(M.ps[0][:, c * P:(c + 1) * P], self.rows[:, c * P:(c + 1) * P], M.k("ident"))
        mm.then_inc(*L.pe.mark("turned"))

    def dve(self, e, M, L, b):
        e.wait_ge(*L.pe("turned", b))
        e.tensor_tensor(M.x[:, b, :], M.x[:, b, :], M.ps[0][:, :], ALU.add).then_inc(*L.dve.mark("residual"))


class Memory:
    def __init__(self, nc, ctx, const_cols, param_cols):
        def sb(name, shape, dt=F32):
            return ctx.enter_context(nc.sbuf_tensor(name, shape, dt))

        self.const_cols, self.param_cols = const_cols, param_cols
        self.consts = sb("consts", [P, max(b for a, b in const_cols.values())])
        self.params = sb("params", [P, max(b for a, b in param_cols.values())])
        self.x = sb("x", [P, B, T])
        self.h = sb("h", [P, T])
        self.h2 = sb("h2", [P, T])
        self.xc, self.sq, self.sd, self.rs = (sb(n, [P, T]) for n in ("xc", "sq", "sd", "rs"))
        self.tiles = sb("tiles", [P, 12, T])
        self.wide = sb("wide", [P, 20, T])
        self.big = sb("big", [P, 9 * T])
        self.small = sb("small", [P, 640])
        self.expert_gate = sb("expert_gate", [P, E, F])
        self.expert_up = sb("expert_up", [P, E, F])
        self.expert_out = sb("expert_out", [P, E, NF, C])
        self.pos = sb("pos", [P, B * NC], I32)
        self.ps = [ctx.enter_context(nc.psum_tensor(f"bank{i}", [P, T], F32)) for i in range(8)]

    def k(self, name):
        a, b = self.const_cols[name]
        return self.consts[:, a:b]

    def w(self, name, rows=P):
        a, b = self.param_cols[name]
        return self.params[0:rows, a:b]

    def tile(self, i):
        return self.tiles[:, i, :]


KINDS = {1: [TokenAttention], 2: [Experts], 3: [Flow], 4: [Experts], 5: [TimeMix], 6: [Depth],
         7: [BlockProject, BlockAttend, BlockMerge], 8: [Depth]}
LAYERS = [1, 2, 3, 4, 5, 6, 7, 8]


def program(nc, D, const_cols, param_cols, plan=None):
    with ExitStack() as ctx:
        def sem(name):
            return ctx.enter_context(nc.semaphore(name))

        M = Memory(nc, ctx, const_cols, param_cols)
        M.D = D
        loaded, experts_loaded, stored = sem("loaded"), sem("experts_loaded"), sem("stored")
        layers, prepared = [], {}
        for n in LAYERS:
            for i, cls in enumerate(KINDS[n]):
                name = f"l{n}_{i}"
                layers.append((cls(M), Stage(name, sem, plan, cls.turns)))
                prepared[name] = sem(f"{name}_prepared")
        block = ctx.enter_context(nc.Block())

        def run(e, which):
            before = None
            for layer, L in layers:
                work, after = layer.parts()[which]
                if before is not None:
                    before.finished(e)
                counter = L.counters["dma" if which == "sp" else which]
                if counter.order is None or counter.order:
                    e.sem_inc(counter.sem, 1)
                layer.before(e, M, which, prepared[L.name])
                if work is not None:
                    if layer.needs_experts and which == "pe":
                        e.wait_ge(experts_loaded, 3 * 16)
                    if layer.turns == 1:
                        work(e, M, L, 0)
                    else:
                        with e.Fori(0, layer.turns) as b:
                            work(e, M, L, b)
                if after is not None:
                    after(e, M, L)
                before = L
            return before

        @block.tensor
        def _(pe):
            pe.wait_ge(loaded, 4 * 16)
            run(pe, "pe")

        @block.scalar
        def _(act):
            act.wait_ge(loaded, 4 * 16)
            run(act, "act")

        @block.vector
        def _(dve):
            dve.wait_ge(loaded, 4 * 16)
            run(dve, "dve")

        @block.gpsimd
        def _(pool):
            pool.wait_ge(loaded, 4 * 16)
            run(pool, "pool")

        @block.sync
        def _(sp):
            sp.dma_start(M.x[:, :, :], D["x"]).then_inc(loaded, 16)
            sp.dma_start(M.consts[:, :], D["consts"]).then_inc(loaded, 16)
            sp.dma_start(M.params[:, :], D["params"]).then_inc(loaded, 16)
            sp.dma_start(M.pos[:, :], D["pos"]).then_inc(loaded, 16)
            sp.dma_start(M.expert_gate[:, :, :], D["wi_gate"]).then_inc(experts_loaded, 16)
            sp.dma_start(M.expert_up[:, :, :], D["wi_up"]).then_inc(experts_loaded, 16)
            sp.dma_start(M.expert_out[:, :, :, :], D["wo"]).then_inc(experts_loaded, 16)
            last = run(sp, "sp")
            last.finished(sp)
            sp.dma_start(D["out"], M.x[:, :, :]).then_inc(stored, 16)
            sp.wait_ge(stored, 16)
            sp.wait_ge(experts_loaded, 3 * 16)
        return {L.name: {k: c.seen for k, c in L.counters.items()} for _, L in layers}


def kernel(**inputs):
    import concourse.bacc as bacc
    from concourse.bass_utils import run_bass_kernel_spmd

    a = {k: np.asarray(v) for k, v in inputs.items()}

    def pack(named):
        cols, at = {}, 0
        for n, m in named.items():
            cols[n] = (at, at + m.shape[1])
            at += m.shape[1]
        return np.ascontiguousarray(np.concatenate(list(named.values()), axis=1)), cols

    consts, const_cols = pack(constants())
    params, param_cols = pack(parameters(a))
    lay = lambda m: np.ascontiguousarray(m)
    arrays = {
        "x": lay(a["L0_attn_a_h"].transpose(2, 0, 1)),
        "consts": consts,
        "params": params,
        "pos": lay(a["L1_ffn_position_ids"].reshape(B, NC, P).transpose(2, 0, 1).reshape(P, B * NC)),
        "wi_gate": lay(a["L0_ffn_wi_gate"].transpose(2, 0, 1)),
        "wi_up": lay(a["L0_ffn_wi_up"].transpose(2, 0, 1)),
        "wo": lay(a["L0_ffn_wo"].reshape(E, C, NF, P).transpose(3, 0, 2, 1)),
        "mask": lay(a["L1_ffn_attention_mask"].reshape(B, NC, P, T).transpose(2, 0, 1, 3)),
    }

    def declare(nc):
        D = {n: nc.dram_tensor(f"in_{n}", m.shape, mybir.dt.from_np(m.dtype), kind="ExternalInput").ap() for n, m in arrays.items()}
        D["out"] = nc.dram_tensor("out_x", (P, B, T), F32, kind="ExternalOutput").ap()
        D["qkv"] = nc.dram_tensor("qkv_tokens", (B * T, 3 * C), F32).ap()
        D["attended"] = nc.dram_tensor("attended_tokens", (B * T, C), F32).ap()
        return D

    draft = bacc.Bacc("TRN2", target_bir_lowering=False, num_devices=1)
    plan = program(draft, declare(draft), const_cols, param_cols)
    nc = bacc.Bacc("TRN2", target_bir_lowering=False, num_devices=1)
    assert program(nc, declare(nc), const_cols, param_cols, plan) == plan
    r = run_bass_kernel_spmd(nc, [{f"in_{n}": m for n, m in arrays.items()}], core_ids=[0])
    return lay(r.results[0]["out_x"].transpose(1, 2, 0))
```

```python
from contextlib import ExitStack

import numpy as np

import concourse.bass as bass
from concourse import mybir

ALU = mybir.AluOpType
ACT = mybir.ActivationFunctionType
AX = mybir.AxisListType.X
F32 = mybir.dt.float32
I32 = mybir.dt.int32

B, T, C = 4, 512, 128
P = 128
NC = T // P
A_H, A_D, A_CR = 8, 64, 32
A_NB = T // A_CR
A_WINDOW, A_QC, A_ROPE = 64, 32, 32
H, DH = 16, 8
F, E = 512, 8
NF = F // P
CAPACITY = int(B * T / E * 1.25)
SLOTS = T // 8
GROUP = 16
NBLK = B * T // GROUP
CHUNKS = B * T // P
TOP = 2
HOLD = TOP * CAPACITY
PIECES = HOLD // P
NEG = -1e30
PI_BELOW = 3.1415925


def split_two_pi():
    rest, parts = 2 * np.pi, []
    for bits in (2.0 ** -8, 2.0 ** -19):
        parts.append(float(np.floor(rest / bits) * bits))
        rest -= parts[-1]
    return parts + [float(np.float32(rest))]


TWO_PI = split_two_pi()


def constants():
    p = np.arange(P)
    f = lambda a: np.asarray(a, np.float32).reshape(P, -1)
    k = {}
    k["mean"] = f(np.full((P, P), 1.0 / C))
    k["ident"] = f(np.eye(P))
    k["ones"] = f(np.ones((P, T)))
    k["mean64"] = f((p[:, None] // 64 == p[None, :] // 64) / 64.0)
    k["head2"] = f(np.where(p[:, None] // 64 == np.arange(2)[None, :], 1.0 / 64, 0.0))
    k["same8"] = f(p[:, None] // DH == p[None, :] // DH)
    k["upto"] = f(p[:, None] <= p[None, :])
    half = A_ROPE // 2
    inv = (np.float32(1.0) / np.float32(10000.0) ** (np.arange(half, dtype=np.float32) * np.float32(2.0) / np.float32(A_ROPE))).astype(np.float32)
    ang = np.arange(T, dtype=np.float32)[:, None] * inv[None, :]
    cos, sin = np.cos(ang), np.sin(ang)
    c64, s64 = np.ones((A_D, T), np.float32), np.zeros((A_D, T), np.float32)
    c64[:half], c64[half:2 * half] = cos.T, cos.T
    s64[:half], s64[half:2 * half] = -sin.T, sin.T
    k["rope_cos"], k["rope_sin"] = f(np.tile(c64, (2, 1))), f(np.tile(s64, (2, 1)))
    causal = np.zeros((P, T))
    causal[:, T - P:] = np.where(p[:, None] >= p[None, :], 0.0, NEG)
    k["causal"] = f(causal)
    d = (p[:, None] + P) - np.arange(2 * P)[None, :]
    k["band"] = f(np.where((d >= 0) & (d < A_WINDOW), 0.0, NEG))
    blk_end = (np.arange(A_NB) + 1) * A_CR - 1
    q = p[:, None] + P * np.arange(NC)[None, :]
    k["blocks_seen"] = f(np.where(blk_end[None, None, :] <= q[:, :, None], 0.0, NEG))
    rep = np.zeros((P, NC, A_H, A_NB))
    for c in range(NC):
        rep[p, c, :, (P * c + p) // A_CR] = 1.0 / A_CR
    k["block_mean"] = f(rep)
    hn = p // A_NB
    vc = np.zeros((P, A_H // 2, 2, A_D))
    for h in range(A_H):
        vc[hn == h, h // 2, h % 2, :] = 1.0
    k["head_of_block"] = f(vc)
    k["head_in_quad"] = f((p[:, None] % 32) // DH == np.arange(4)[None, :])
    k["head"] = f(p[:, None] // DH == np.arange(H)[None, :])
    k["count_tok"] = f(P * np.arange(NC)[None, :] + p[:, None] + 1.0)
    k["inv_count_tok"] = f(1.0 / (P * np.arange(NC)[None, :] + p[:, None] + 1.0))
    k["inv_count"] = f(np.tile(1.0 / (np.arange(T) + 1.0), (P, 1)))
    k["expert_rank"] = f(np.tile(np.arange(E) - 99.0, (P, 1)))
    k["slot_before"] = f(np.tile((np.arange(E)[None, :] * HOLD + np.arange(TOP)[:, None] * CAPACITY - 1.0).reshape(-1), (P, 1)))
    k["spare_slot"] = f(E * HOLD + np.arange(TOP)[None, :, None] * B * T + np.arange(CHUNKS)[None, None, :] * P + p[:, None, None])
    u = np.arange(T + (NC - 1) * P)
    k["before"] = f(u[None, :] < p[:, None] + (NC - 1) * P)
    k["slot"] = f(np.tile(np.arange(SLOTS), (P, 1)))
    k["last_slot"] = f(np.tile(np.where(np.arange(SLOTS) == SLOTS - 1, NEG, 0.0), (P, 1)))
    hinv = 1.0 / np.float32(10000.0) ** (np.arange(0, DH, 2, dtype=np.float32) / np.float32(DH))
    k["mod_inv"] = f(hinv[(p % DH) % (DH // 2)])
    k["mod_sign"] = f(np.where(p % DH < DH // 2, -1.0, 1.0))
    pair = np.zeros((P, H // 2, C))
    for m in range(H // 2):
        pair[:, m, :] = p[None, :] // DH == 2 * m + (p[:, None] // SLOTS)
    k["head_of_pair"] = f(pair)
    k["minus_half"] = f(np.full((P, 64), -0.5))
    for name, v in (("eps5", 1e-5), ("eps6", 1e-6), ("zero", 0.0)):
        k[name] = f(np.full((P, 1), v))
    return k


def _swap(n, lo, hi):
    h = (hi - lo) // 2
    o = np.arange(n)
    o[lo:lo + h], o[lo + h:hi] = np.arange(lo + h, hi), np.arange(lo, lo + h)
    return o


def parameters(a):
    k = {}

    def col(v):
        return v.reshape(P, 1)

    def rows(m):
        return m.reshape(-1, P, m.shape[1]).transpose(1, 0, 2).reshape(P, -1)

    def tall(m):
        out = np.zeros((P, m.shape[1]), m.dtype)
        out[:m.shape[0]] = m
        return out

    rot = _swap(A_D, 0, A_ROPE)
    g = "L0_attn_a_"
    k["a_w_qc"] = a[g + "w_qc"]
    qup = a[g + "w_qup"]
    k["a_w_q"] = tall(qup)
    k["a_w_qr"] = tall(qup.reshape(A_QC, A_H, A_D)[:, :, rot].reshape(A_QC, -1))
    k["a_w_k"] = np.tile(a[g + "w_k"], (1, 2))
    k["a_w_kr"] = np.tile(a[g + "w_k"][:, rot], (1, 2))
    k["a_w_v"] = np.tile(a[g + "w_v"], (1, 2))
    k["a_gq"] = col(np.tile(a[g + "g_qnorm"], 2))
    k["a_gk"] = col(np.tile(a[g + "g_knorm"], 2))
    k["a_w_gate"] = np.tile(a[g + "w_gate"], (2, 1))
    k["a_b_gate"] = np.tile(a[g + "b_gate"], (P, A_H))
    k["a_sink"] = np.tile(a[g + "sink_logit"], (P, 1))
    wog = a[g + "w_out_group"]
    wide = np.zeros((4, P, P), wog.dtype)
    for pr in range(4):
        gg = pr // 2
        wide[pr, :, gg * 64:(gg + 1) * 64] = wog[gg, (pr % 2) * P:(pr % 2 + 1) * P]
    k["a_w_group"] = wide.transpose(1, 0, 2).reshape(P, -1)
    k["a_w_out"] = a[g + "w_out"]
    g = "L0_attn_b_"
    for n in ("Wq", "Wk", "Wv", "Wo", "W1"):
        k["f_" + n] = a[g + n]
    for n in ("bq", "bk", "bv", "bo", "b2", "ln1_g", "ln1_b", "ln2_g", "ln2_b"):
        k["f_" + n] = col(a[g + n])
    k["f_b1"] = a[g + "b1"].reshape(NF, P).T
    k["f_W2"] = rows(a[g + "W2"])
    k["e_gate"] = a["L0_ffn_gate_w"].T
    g = "L1_attn_a_"
    for n in ("Wk", "Wv", "Wr", "Wo"):
        k["r_" + n] = a[g + n].T
    for n in ("spatial_decay", "spatial_first", "mix_k", "mix_v", "mix_r"):
        k["r_" + n] = col(a[g + n])
    k["b_w"] = a["L1_attn_b_w_qkv"].T
    k["b_b"] = np.tile(a["L1_attn_b_b_qkv"], (P, 1))
    g = "L1_ffn_"
    rot = _swap(DH, 0, DH)
    k["m_router"] = a[g + "router_w"]
    k["m_router_b"] = np.tile(a[g + "router_b"], (P, 1))
    for n in ("wq", "wk"):
        k["m_" + n] = a[g + n]
        k["m_" + n + "r"] = a[g + n].reshape(C, H, DH)[:, :, rot].reshape(C, C)
    for n in ("wv", "wo", "w1"):
        k["m_" + n] = a[g + n]
    k["m_w2"] = rows(a[g + "w2"])
    k["m_ln1"], k["m_ln2"] = col(a[g + "ln1"]), col(a[g + "ln2"])
    return k


class Steps:

    def __init__(self, sem, order, turns):
        self.sem, self.order, self.turns, self.seen = sem, order, turns, []

    def mark(self, name):
        if self.seen and name == self.seen[0]:
            self.seen = []
        assert name not in self.seen, name
        self.seen.append(name)
        return self.sem, self.unit

    unit = 1
    entered = 1

    def __call__(self, name, turn):
        if self.order is None:
            return self.sem, 1
        return self.sem, turn * (len(self.order) * self.unit) + ((self.order.index(name) + 1) * self.unit + self.entered)

    def end(self, turns=None):
        n = 1 if self.order is None else len(self.order)
        return self.sem, (self.turns if turns is None else turns) * (n * self.unit) + self.entered


class DmaSteps(Steps):
    unit = 16


class LaneSteps(DmaSteps):
    entered = 0


class Stage:

    def __init__(self, name, sem, plan, turns=B, lanes=()):
        self.name = name
        self.counters = {}
        for lane in lanes:
            order = None if plan is None else plan[name][lane]
            self.counters[lane] = LaneSteps(sem(f"{name}_{lane}"), order, turns)
            self.lanes = self.counters
        for engine in ("pe", "act", "dve", "pool", "dma"):
            kind = DmaSteps if engine == "dma" else Steps
            order = None if plan is None else plan[name][engine]
            if order is None or order:
                self.counters[engine] = kind(sem(f"{name}_{engine}"), order, turns)
            else:
                self.counters[engine] = kind(None, [], turns)
        self.pe, self.act, self.dve, self.pool, self.dma = (self.counters[k] for k in ("pe", "act", "dve", "pool", "dma"))

    def finished(self, e, turns=None):
        for c in self.counters.values():
            if c.order is None or c.order:
                e.wait_ge(*c.end(turns))


def norm_pe(e, M, L, b, tag, src, ready):
    for w in ready:
        e.wait_ge(*w)
    e.matmul(M.ps[0][:, :], M.k("mean"), src, start=True, stop=True).then_inc(*L.pe.mark(tag + "_mean"))
    e.wait_ge(*L.act(tag + "_square", b))
    for c in range(NC):
        mm = e.matmul(M.ps[1][:, c:c + 1], M.sq[:, c * P:(c + 1) * P], M.k("mean")[:, 0:1], start=True, stop=True)
    mm.then_inc(*L.pe.mark(tag + "_var"))
    e.wait_ge(*L.pool(tag + "_rs", b))
    for c in range(NC):
        mm = e.transpose(M.ps[1][:, c * P:(c + 1) * P], M.norm_cols[:, NC + c:NC + c + 1].broadcast_to([P, P]), M.k("ident"))
    mm.then_inc(*L.pe.mark(tag + "_rs"))


def norm_act(e, M, L, b, tag):
    e.wait_ge(*L.dve(tag + "_centred", b))
    e.activation(M.sq[:, :], M.xc[:, :], ACT.Square).then_inc(*L.act.mark(tag + "_square"))


def norm_pool(e, M, L, b, tag):
    e.wait_ge(*L.dve(tag + "_var", b))
    e.tensor_tensor(M.norm_cols[:, NC:2 * NC], M.norm_cols[:, 0:NC], M.k("minus_half")[:, 0:NC], ALU.pow).then_inc(*L.pool.mark(tag + "_rs"))


def norm_dve(e, M, L, b, tag, src, dst, gain=None, shift=None):
    e.wait_ge(*L.pe(tag + "_mean", b))
    e.tensor_tensor(M.xc[:, :], src, M.ps[0][:, :], ALU.subtract).then_inc(*L.dve.mark(tag + "_centred"))
    e.wait_ge(*L.pe(tag + "_var", b))
    e.tensor_scalar(M.norm_cols[:, 0:NC], M.ps[1][:, 0:NC], 1e-5, None, ALU.add).then_inc(*L.dve.mark(tag + "_var"))
    e.wait_ge(*L.pe(tag + "_rs", b))
    if gain is None:
        e.tensor_tensor(dst, M.xc[:, :], M.ps[1][:, :], ALU.mult).then_inc(*L.dve.mark(tag))
        return
    e.scalar_tensor_tensor(M.xc[:, :], M.xc[:, :], gain, M.ps[1][:, :], ALU.mult, ALU.mult).then_inc(*L.dve.mark(tag + "_gained"))
    e.wait_ge(*L.dve(tag + "_gained", b))
    e.tensor_scalar(dst, M.xc[:, :], shift, None, ALU.add).then_inc(*L.dve.mark(tag))

class Layer:
    turns = B
    needs_experts = False
    lanes = ()
    pe = act = dve = pool = sp = None
    pe_after = act_after = dve_after = pool_after = sp_after = None

    def before(self, e, M, which, sem):
        pass

    def parts(self):
        return {"pe": (self.pe, self.pe_after), "act": (self.act, self.act_after), "dve": (self.dve, self.dve_after),
                "pool": (self.pool, self.pool_after), "sp": (self.sp, self.sp_after)}


class Route(Layer):

    def __init__(self, M):
        self.h_tok = M.wide[:, 0:B, :]
        self.lg = M.wide[:, 12, 0:CHUNKS * E]

    def pe(self, e, M, L, b):
        L.finished(e, b)
        norm_pe(e, M, L, b, "norm", M.x[:, b, :], [])
        e.wait_ge(*L.dve("norm", b))
        for c in range(NC):
            e.matmul(M.ps[3][:, c * E:(c + 1) * E], M.h[:, c * P:(c + 1) * P], M.w("e_gate"), start=True, stop=True)
            mm = e.transpose(M.ps[2][:, c * P:(c + 1) * P], M.h[:, c * P:(c + 1) * P], M.k("ident"))
        mm.then_inc(*L.pe.mark("logits"))

    def pool(self, e, M, L, b):
        norm_pool(e, M, L, b, "norm")

    def act(self, e, M, L, b):
        L.finished(e, b)
        norm_act(e, M, L, b, "norm")
        e.wait_ge(*L.pe("logits", b))
        e.activation(self.h_tok[:, b, :], M.ps[2][:, :], ACT.Copy).then_inc(*L.act.mark("h_tok"))

    def dve(self, e, M, L, b):
        L.finished(e, b)
        norm_dve(e, M, L, b, "norm", M.x[:, b, :], M.h[:, :])
        e.wait_ge(*L.pe("logits", b))
        e.tensor_copy(self.lg.rearrange("p (b k) -> p b k", b=B)[:, b, :], M.ps[3][:, 0:NC * E]).then_inc(*L.dve.mark("lg"))


class Experts(Layer):
    needs_experts = True
    turns = 1
    lanes = ("scatter", "load0", "load1", "store0", "store1") + tuple(f"fetch{b}" for b in range(B))

    def __init__(self, M):
        self.h_tok = M.wide[:, 0:B, :].rearrange("p b (c f) -> p (b c) f", f=C)
        self.fetched = M.wide[:, 4:12, :].rearrange("p (k b) (c f) -> p k (b c) f", k=TOP, f=C)
        self.combined = self.h_tok
        w = M.wide[:, 12:19, :].rearrange("p r t -> p (r t)")
        at = [0]

        def take(*dims):
            n = int(np.prod(dims))
            a = w[:, at[0]:at[0] + n]
            at[0] += n
            return a.rearrange("p (c k) -> p c k", k=dims[1]) if len(dims) == 2 else a

        self.lg = take(CHUNKS, E)
        self.eq, self.tmp = take(CHUNKS, E), take(CHUNKS, E)
        self.chosen, self.place, self.free = (take(CHUNKS, TOP * E) for _ in range(3))
        self.sums = [take(CHUNKS // 2 + CHUNKS, TOP * E) for _ in range(2)]
        self.m1, self.m2, self.pick, self.e2, self.w1, self.w2 = (take(CHUNKS) for _ in range(6))
        self.row, self.valid, self.weight, self.to, self.gather = (take(TOP * CHUNKS).rearrange("p (k c) -> p k c", k=TOP) for _ in range(5))
        self.scatter_i, self.gather_i = M.slot_index[:, 0:TOP * CHUNKS], M.slot_index[:, TOP * CHUNKS:2 * TOP * CHUNKS]
        big = M.big[:, 0:6 * HOLD].rearrange("p (i s) -> p i s", s=HOLD)
        self.rows_in, self.x_in, self.rows_out = ([big[:, 2 * i + j, :] for j in range(2)] for i in range(3))
        t = M.tiles.rearrange("p r t -> p (r t)")
        self.mid = [t[:, i * NF * HOLD:(i + 1) * NF * HOLD].rearrange("p (f s) -> p f s", f=NF) for i in range(2)]
        self.silu = [M.h, M.h2, M.xc]

    HALVES = [(0, HOLD // P // 2 * P + P), (HOLD // P // 2 * P + P, HOLD)]
    UNITS = [(f, h) for f in range(NF) for h in range(2)]
    N = len(UNITS)

    def sp(self, e, M, L, b):
        slots = M.D["slots"][0:E * HOLD, :].rearrange("(x p r) c -> x p (r c)", x=E, p=P)
        out = M.D["slots_out"].rearrange("(x p r) c -> x p (r c)", x=E, p=P)
        e.wait_ge(*L.counters["scatter"].end())

        def load(x):
            if x >= 2:
                e.wait_ge(*L.pe(f"x_in{x - 2}", 0))
            e.dma_start(self.rows_in[x % 2], slots[x, :, :]).then_inc(*L.counters[f"load{x % 2}"].mark(f"rows{x}"))

        load(0)
        load(1)
        for x in range(E):
            if x + 2 < E:
                load(x + 2)
            e.wait_ge(*L.dve(f"rows_out{x}_1", 0))
            e.dma_start(out[x, :, :], self.rows_out[x % 2]).then_inc(*L.counters[f"store{x % 2}"].mark(f"stored{x}"))

    def pool(self, e, M, L, b):
        e.wait_ge(M.slots_cleared, 16)
        e.wait_ge(*L.dve("scatter_i", 0))
        for i in range(TOP * CHUNKS):
            e.indirect_dma_start(M.D["slots"], bass.IndirectOffsetOnAxis(self.scatter_i[:, i:i + 1], 0), self.h_tok[:, i % CHUNKS, :], None)\
                .then_inc(*L.counters["scatter"].mark(f"scatter{i}"))
        e.wait_ge(*L.dve("gather_i", 0))
        e.wait_ge(*L.counters["store0"].end())
        e.wait_ge(*L.counters["store1"].end())
        for c in range(CHUNKS):
            for k in range(TOP):
                i = k * CHUNKS + c
                e.indirect_dma_start(self.fetched[:, k, c, :], None, M.D["slots_out"], bass.IndirectOffsetOnAxis(self.gather_i[:, i:i + 1], 0))\
                    .then_inc(*L.counters[f"fetch{c // NC}"].mark(f"fetch{i}"))

    def pe(self, e, M, L, b):
        e.wait_ge(*L.dve("chosen2", 0))
        chosen = self.chosen.rearrange("p c k -> p (c k)")
        n = CHUNKS * TOP * E
        e.matmul(M.ps[0][:, 0:n], M.k("upto"), chosen, start=True, stop=True)
        e.matmul(M.ps[1][:, 0:n], M.k("ones")[:, 0:P], chosen, start=True, stop=True).then_inc(*L.pe.mark("counted"))
        e.wait_ge(*L.dve("free", 0))

        def rows_to_columns(x):
            e.wait_ge(*L.counters[f"load{x % 2}"](f"rows{x}", 0))
            if x >= 1:
                e.wait_ge(*L.act(f"x_in{x - 1}_1", 0))
            for h, (lo, hi) in enumerate(self.HALVES):
                for s in range(lo, hi, P):
                    mm = e.transpose(M.ps[4 + h][:, s - lo:s - lo + P], self.rows_in[x % 2][:, s:s + P], M.k("ident"))
            mm.then_inc(*L.pe.mark(f"x_in{x}"))

        def down(x, i):
            h = 0 if i * P < self.HALVES[0][1] else 1
            lo = self.HALVES[h][0]
            e.wait_ge(*L.dve(f"mid{x}_{self.N - 1}", 0))
            if x >= 1:
                e.wait_ge(*L.dve(f"rows_out{x - 1}_{h}", 0))
            for f in range(NF):
                mm = e.matmul(M.ps[6 + h][:, i * P - lo:(i + 1) * P - lo], self.mid[x % 2][:, f, i * P:(i + 1) * P], M.expert_out[:, x, f, :],
                              start=(f == 0), stop=(f == NF - 1))
            mm.then_inc(*L.pe.mark(f"down{x}_{i}"))

        rows_to_columns(0)
        for x in range(E):
            for u, (f, h) in enumerate(self.UNITS):
                lo, hi = self.HALVES[h]
                g = x * self.N + u
                e.wait_ge(*L.act(f"x_in{x}_{h}", 0))
                if g >= 2:
                    e.wait_ge(*L.act(f"silu{g - 2}", 0))
                e.matmul(M.ps[g % 2][:, 0:hi - lo], M.expert_gate[:, x, f * P:(f + 1) * P], self.x_in[x % 2][:, lo:hi], start=True, stop=True)\
                    .then_inc(*L.pe.mark(f"gate{g}"))
                if g >= 2:
                    e.wait_ge(*L.dve(f"mid{(g - 2) // self.N}_{(g - 2) % self.N}", 0))
                e.matmul(M.ps[2 + g % 2][:, 0:hi - lo], M.expert_up[:, x, f * P:(f + 1) * P], self.x_in[x % 2][:, lo:hi], start=True, stop=True)\
                    .then_inc(*L.pe.mark(f"up{g}"))
                if x >= 1 and u >= 1 and u - 1 < PIECES:
                    down(x - 1, u - 1)
                if u == self.N - 2 and x + 1 < E:
                    rows_to_columns(x + 1)
        for i in range(PIECES):
            down(E - 1, i)
        for bb in range(B):
            e.wait_ge(*L.dve(f"combined{bb}", 0))
            for c in range(NC):
                mm = e.transpose(M.ps[bb][:, c * P:(c + 1) * P], self.combined[:, bb * NC + c, :], M.k("ident"))
            mm.then_inc(*L.pe.mark(f"back{bb}"))

    def act(self, e, M, L, b):
        e.wait_ge(*L.dve("gap", 0))
        e.activation(self.e2, self.w1, ACT.Exp).then_inc(*L.act.mark("e2"))

        def x_in(x):
            e.wait_ge(*L.pe(f"x_in{x}", 0))
            if x >= 2:
                e.wait_ge(*L.pe(f"up{(x - 1) * self.N - 1}", 0))
            for h, (lo, hi) in enumerate(self.HALVES):
                e.activation(self.x_in[x % 2][:, lo:hi], M.ps[4 + h][:, 0:hi - lo], ACT.Copy).then_inc(*L.act.mark(f"x_in{x}_{h}"))

        x_in(0)
        for x in range(E):
            for u, (f, h) in enumerate(self.UNITS):
                lo, hi = self.HALVES[h]
                g = x * self.N + u
                e.wait_ge(*L.pe(f"gate{g}", 0))
                if g >= 3:
                    e.wait_ge(*L.dve(f"mid{(g - 3) // self.N}_{(g - 3) % self.N}", 0))
                e.activation(self.silu[g % 3][:, 0:hi - lo], M.ps[g % 2][:, 0:hi - lo], ACT.Silu).then_inc(*L.act.mark(f"silu{g}"))
                if u == self.N - 2 and x + 1 < E:
                    x_in(x + 1)

    def dve(self, e, M, L, b):
        wide = lambda a: a.unsqueeze(2).broadcast_to([P, CHUNKS, E])
        rank = M.k("expert_rank").unsqueeze(1).broadcast_to([P, CHUNKS, E])

        def step(name, ins, wait=True):
            ins.then_inc(*L.dve.mark(name))
            if wait:
                e.wait_ge(*L.dve(name, 0))

        for i in range(2):
            step(f"pad{i}", e.memset(self.sums[i][:, 0:CHUNKS // 2, :], 0.0), False)
        for k, m in ((0, self.m1), (1, self.m2)):
            step(f"max{k}", e.tensor_reduce(m, self.lg, AX, ALU.max))
            step(f"top{k}", e.tensor_tensor(self.eq, self.lg, wide(m), ALU.is_equal))
            step(f"rank{k}", e.tensor_tensor(self.tmp, self.eq, rank, ALU.mult))
            step(f"first{k}", e.tensor_reduce(self.pick, self.tmp, AX, ALU.min))
            step(f"chosen{k + 1}", e.tensor_tensor(self.chosen[:, :, k * E:(k + 1) * E], rank, wide(self.pick), ALU.is_equal))
            if k == 0:
                step("rest", e.scalar_tensor_tensor(self.lg, self.chosen[:, :, 0:E], NEG, self.lg, ALU.mult, ALU.add))
        step("gap", e.tensor_tensor(self.w1, self.m2, self.m1, ALU.subtract), False)
        e.wait_ge(*L.pe("counted", 0))
        half = CHUNKS // 2
        total = M.ps[1][:, 0:CHUNKS * TOP * E].rearrange("p (c k) -> p c k", c=CHUNKS)
        step("total", e.tensor_copy(self.sums[0][:, half:, :], total))
        s, i = 1, 0
        while s < CHUNKS:
            a = self.sums[i]
            step(f"sum{s}", e.tensor_tensor(self.sums[1 - i][:, half:, :], a[:, half:, :], a[:, half - s:half + CHUNKS - s, :], ALU.add))
            s, i = 2 * s, 1 - i
        upto = M.ps[0][:, 0:CHUNKS * TOP * E].rearrange("p (c k) -> p c k", c=CHUNKS)
        step("others", e.tensor_tensor(self.place, self.sums[i][:, half:, :], total, ALU.subtract))
        step("place", e.tensor_tensor(self.place, self.place, upto, ALU.add))
        step("free", e.scalar_tensor_tensor(self.free, self.place, float(CAPACITY), self.chosen, ALU.is_le, ALU.mult), False)
        step("slot_at", e.tensor_tensor(self.place, self.place, M.k("slot_before").unsqueeze(1).broadcast_to([P, CHUNKS, TOP * E]), ALU.add))
        step("slot_of", e.tensor_tensor(self.place, self.place, self.free, ALU.mult))
        for k in range(TOP):
            step(f"row{k}", e.tensor_reduce(self.row[:, k, :], self.place[:, :, k * E:(k + 1) * E], AX, ALU.add), False)
            step(f"valid{k}", e.tensor_reduce(self.valid[:, k, :], self.free[:, :, k * E:(k + 1) * E], AX, ALU.add))
        spare = M.k("spare_slot").rearrange("p (k c) -> p k c", k=TOP)
        step("full", e.tensor_tensor(self.to, self.valid, spare, ALU.mult))
        step("spare", e.tensor_tensor(self.to, spare, self.to, ALU.subtract))
        step("to", e.tensor_tensor(self.to, self.to, self.row, ALU.add))
        step("scatter_i", e.tensor_copy(self.scatter_i, self.to.rearrange("p k c -> p (k c)")), False)
        step("gather_i", e.tensor_copy(self.gather_i, self.row.rearrange("p k c -> p (k c)")), False)
        e.wait_ge(*L.act("e2", 0))
        step("norm_sum", e.tensor_scalar(self.w2, self.e2, 1.0, None, ALU.add))
        step("w1", e.reciprocal(self.w1, self.w2))
        step("w2", e.tensor_tensor(self.w2, self.w1, self.e2, ALU.mult))
        for k, w in ((0, self.w1), (1, self.w2)):
            step(f"weight{k}", e.tensor_tensor(self.weight[:, k, :], self.valid[:, k, :], w, ALU.mult))

        def rows_out(x):
            for h, (lo, hi) in enumerate(self.HALVES):
                e.wait_ge(*L.pe(f"down{x}_{hi // P - 1}", 0))
                if x >= 2:
                    e.wait_ge(*L.counters[f"store{x % 2}"](f"stored{x - 2}", 0))
                e.tensor_copy(self.rows_out[x % 2][:, lo:hi], M.ps[6 + h][:, 0:hi - lo]).then_inc(*L.dve.mark(f"rows_out{x}_{h}"))

        for x in range(E):
            for u, (f, h) in enumerate(self.UNITS):
                lo, hi = self.HALVES[h]
                g = x * self.N + u
                e.wait_ge(*L.act(f"silu{g}", 0))
                e.wait_ge(*L.pe(f"up{g}", 0))
                if x >= 2:
                    e.wait_ge(*L.pe(f"down{x - 2}_{PIECES - 1}", 0))
                e.tensor_tensor(self.mid[x % 2][:, f, lo:hi], self.silu[g % 3][:, 0:hi - lo], M.ps[2 + g % 2][:, 0:hi - lo], ALU.mult)\
                    .then_inc(*L.dve.mark(f"mid{x}_{u}"))
                if u == PIECES + 1 and x >= 1:
                    rows_out(x - 1)
        rows_out(E - 1)

        def residual(bb):
            e.wait_ge(*L.pe(f"back{bb}", 0))
            e.tensor_tensor(M.x[:, bb, :], M.x[:, bb, :], M.ps[bb][:, :], ALU.add).then_inc(*L.dve.mark(f"residual{bb}"))

        for bb in range(B):
            e.wait_ge(*L.counters[f"fetch{bb}"].end())
            for c in range(bb * NC, (bb + 1) * NC):
                e.tensor_scalar(self.combined[:, c, :], self.fetched[:, 0, c, :], self.weight[:, 0, c:c + 1], None, ALU.mult)\
                    .then_inc(*L.dve.mark(f"first_result{c}"))
            for c in range(bb * NC, (bb + 1) * NC):
                e.wait_ge(*L.dve(f"first_result{c}", 0))
                ins = e.scalar_tensor_tensor(self.combined[:, c, :], self.fetched[:, 1, c, :], self.weight[:, 1, c:c + 1],
                                             self.combined[:, c, :], ALU.mult, ALU.add)
            ins.then_inc(*L.dve.mark(f"combined{bb}"))
            if bb:
                residual(bb - 1)
        residual(B - 1)


class Flow(Layer):
    def __init__(self, M):
        t = M.tile
        self.q, self.k, self.v, self.qe, self.ke, self.ca, self.cb, self.da, self.db = (t(i) for i in range(9))
        self.masked_q = M.wide[:, 0:4, :]
        self.scores = [M.wide[:, 4, :], M.wide[:, 5, :], M.wide[:, 6, :]]
        self.k_tok, self.v_tok = M.wide[:, 7, :], M.wide[:, 8, :]
        self.state = M.wide[:, 9, 0:3 * P]
        wide = H * (P + DH)
        self.v_heads = [M.big[:, c * wide:c * wide + H * P].rearrange("p (h f) -> p h f", f=P) for c in range(2)]
        self.v_diagonal = [M.big[:, c * wide:(c + 1) * wide].rearrange("p (h f) -> p h f", f=P + DH)[:, :, 0:DH] for c in range(2)]
        self.mid = M.wide[:, 14:18, :]
        self.sink, self.src = M.wide[:, 18, :], M.wide[:, 19, :]
        self.cols = M.small[:, 0:128]
        self.sink_cols, self.src_cols, self.comp_cols = (M.small[:, 128 + 64 * i:192 + 64 * i] for i in range(3))
        self.rows = [M.tile(9), M.tile(10)]
        self.eps = 1e-6

    def before(self, e, M, which, sem):
        if which == "pool":
            e.memset(M.big[:, 0:2 * H * (P + DH)], 0.0).then_inc(sem, 1)
            e.wait_ge(sem, 1)

    def pe(self, e, M, L, b):
        L.finished(e, b)
        norm_pe(e, M, L, b, "norm", M.x[:, b, :], [])
        e.wait_ge(*L.dve("norm", b))
        for n, w in enumerate(("f_Wq", "f_Wk", "f_Wv")):
            e.matmul(M.ps[2 + n][:, :], M.w(w), M.h[:, :], start=True, stop=True).then_inc(*L.pe.mark(f"proj{n}"))
        def head_sums(tag, base):
            for n, src in enumerate((self.da, self.db)):
                e.wait_ge(*L.dve(f"{tag}{n}", b))
                for c in range(NC):
                    at = base + 64 * n + H * c
                    mm = e.matmul(M.ps[7][:, at:at + H], src[:, c * P:(c + 1) * P], M.k("head"), start=True, stop=True)
                mm.then_inc(*L.pe.mark(f"{tag}{n}"))

        def turn_back(bank, cols, name):
            for c in range(NC):
                mm = e.transpose(M.ps[bank][:, c * P:(c + 1) * P], cols[:, c * P:(c + 1) * P], M.k("ident"))
            mm.then_inc(*L.pe.mark(name))

        head_sums("flow", 0)
        e.wait_ge(*L.dve("inv_n", b))
        turn_back(5, self.rows[0], "in_back")
        turn_back(6, self.rows[1], "out_back")
        head_sums("cons", 128)
        e.wait_ge(*L.act("src", b))
        for c in range(NC):
            out = M.ps[7][:, 256 + H * c:256 + H * (c + 1)]
            src = lambda d: self.src_cols[:, H * d:H * (d + 1)]
            mm = e.matmul(out, M.k("upto"), src(c), start=True, stop=(c == 0))
            for d in range(c):
                mm = e.matmul(out, M.k("ones")[:, 0:P], src(d), start=False, stop=(d == c - 1))
        mm.then_inc(*L.pe.mark("cum_src"))
        e.wait_ge(*L.dve("comp", b))
        turn_back(5, self.rows[0], "comp_back")
        e.wait_ge(*L.act("sink", b))
        turn_back(6, self.rows[1], "sink_back")
        e.wait_ge(*L.dve("vs", b))
        for c in range(NC):
            e.transpose(M.ps[0][:, c * P:(c + 1) * P], self.k[:, c * P:(c + 1) * P], M.k("ident"))
            mm = e.transpose(M.ps[1][:, c * P:(c + 1) * P], self.v[:, c * P:(c + 1) * P], M.k("ident"))
        mm.then_inc(*L.pe.mark("turned"))
        e.wait_ge(*L.act("sink_row", b))
        e.wait_ge(*L.act("k_tok", b))
        e.wait_ge(*L.act("v_tok", b))
        for c in range(NC - 1):
            s = slice(c * P, (c + 1) * P)
            mm = e.matmul(M.ps[6][:, s], self.k_tok[:, s], self.v_tok[:, s], start=True, stop=True)
        mm.then_inc(*L.pe.mark("kv"))
        e.wait_ge(*L.dve("masked_q3", b))
        units = [(c, g) for c in range(NC) for g in range(4)]

        def apply(u):
            c, g = units[u]
            if g == 0:
                e.wait_ge(*L.pool(f"v_head{c}", b))
            e.wait_ge(*L.dve(f"causal{u}", b))
            for r in range(4):
                mm = e.matmul(M.ps[5][:, c * P:(c + 1) * P], self.v_diag(c, 4 * g + r), self.scores[u % 3][:, r * P:(r + 1) * P],
                              start=(u == 0 and r == 0), stop=False, skip_group_check=True)
            mm.then_inc(*L.pe.mark(f"apply{u}"))

        for u, (c, g) in enumerate(units):
            if u >= 3:
                e.wait_ge(*L.dve(f"causal{u - 3}", b))
            rows = slice(32 * g, 32 * g + 32)
            e.matmul(M.ps[2 + u % 3][:, :], self.k[rows, c * P:(c + 1) * P], self.masked_q[rows, :, c * P:(c + 1) * P],
                     start=True, stop=True).then_inc(*L.pe.mark(f"scores{u}"))
            if u >= 2:
                apply(u - 2)
        apply(len(units) - 2)
        apply(len(units) - 1)
        e.wait_ge(*L.dve("state2", b))
        for c in range(1, NC):
            mm = e.matmul(M.ps[5][:, c * P:(c + 1) * P], self.state[:, (c - 1) * P:c * P], self.q[:, c * P:(c + 1) * P],
                          start=False, stop=(c == NC - 1), skip_group_check=True)
        mm.then_inc(*L.pe.mark("attended"))
        e.wait_ge(*L.dve("alloc", b))
        e.matmul(M.ps[2][:, :], M.w("f_Wo"), self.da[:, :], start=True, stop=True).then_inc(*L.pe.mark("out"))
        norm_pe(e, M, L, b, "ln1", self.db[:, :], [L.dve("with_in", b)])
        e.wait_ge(*L.dve("ln1", b))
        for f in range(NF):
            e.matmul(M.ps[2 + f][:, :], M.w("f_W1")[:, f * P:(f + 1) * P], self.qe[:, :], start=True, stop=True).then_inc(*L.pe.mark(f"up{f}"))
        for f in range(NF):
            e.wait_ge(*L.act(f"gelu{f}", b))
            mm = e.matmul(M.ps[6][:, :], M.w("f_W2")[:, f * P:(f + 1) * P], self.mid[:, f, :], start=(f == 0), stop=(f == NF - 1))
        mm.then_inc(*L.pe.mark("down"))
        norm_pe(e, M, L, b, "ln2", self.ke[:, :], [L.dve("with_ffn", b)])

    def v_diag(self, c, h):
        return self.v_heads[c % 2][:, h, :]

    def act(self, e, M, L, b):
        L.finished(e, b)
        norm_act(e, M, L, b, "norm")
        for n, (dst, bias, fn) in enumerate(((self.q, "f_bq", ACT.Sigmoid), (self.k, "f_bk", ACT.Sigmoid), (self.v, "f_bv", ACT.Identity))):
            e.wait_ge(*L.pe(f"proj{n}", b))
            e.activation(dst[:, :], M.ps[2 + n][:, :], fn, bias=M.w(bias)).then_inc(*L.act.mark(("q", "k", "v")[n]))
        e.wait_ge(*L.dve("src", b))
        e.activation(self.rows[1].rearrange("p (h d) -> p h d", d=DH), self.sink_cols.unsqueeze(2).broadcast_to([P, NC * H, DH]), ACT.Sigmoid)\
            .then_inc(*L.act.mark("sink"))
        e.activation(self.src_cols, self.src_cols, ACT.Exp).then_inc(*L.act.mark("src"))
        e.wait_ge(*L.pe("sink_back", b))
        e.activation(self.sink, M.ps[6][:, :], ACT.Copy).then_inc(*L.act.mark("sink_row"))
        e.wait_ge(*L.pe("turned", b))
        e.activation(self.k_tok, M.ps[0][:, :], ACT.Copy).then_inc(*L.act.mark("k_tok"))
        e.activation(self.v_tok, M.ps[1][:, :], ACT.Copy).then_inc(*L.act.mark("v_tok"))
        norm_act(e, M, L, b, "ln1")
        for f in range(NF):
            e.wait_ge(*L.pe(f"up{f}", b))
            e.activation(self.mid[:, f, :], M.ps[2 + f][:, :], ACT.Gelu, bias=M.w("f_b1")[:, f:f + 1]).then_inc(*L.act.mark(f"gelu{f}"))
        norm_act(e, M, L, b, "ln2")

    def pool(self, e, M, L, b):
        L.finished(e, b)
        norm_pool(e, M, L, b, "norm")
        e.wait_ge(*L.act("v_tok", b))
        for c in range(NC):
            if c >= 2:
                e.wait_ge(*L.pe(f"apply{4 * (c - 2) + 3}", b))
            src = self.v_tok[:, c * P:(c + 1) * P].rearrange("p (h d) -> p h d", d=DH)
            ones = M.k("ones")[:, 0:P].rearrange("p (h d) -> p h d", d=DH)
            e.tensor_tensor(self.v_diagonal[c % 2], src, ones, ALU.mult).then_inc(*L.pool.mark(f"v_head{c}"))
        norm_pool(e, M, L, b, "ln1")
        norm_pool(e, M, L, b, "ln2")

    def dve(self, e, M, L, b):
        L.finished(e, b)
        norm_dve(e, M, L, b, "norm", M.x[:, b, :], M.h[:, :])
        q, k, v, qe, ke, ca, cb, da, db = (x[:, :] for x in (self.q, self.k, self.v, self.qe, self.ke, self.ca, self.cb, self.da, self.db))
        eps, ones = self.eps, M.k("ones")

        def step(name, ins, wait=True):
            ins.then_inc(*L.dve.mark(name))
            if wait:
                e.wait_ge(*L.dve(name, b))

        e.wait_ge(*L.act("q", b))
        step("qe", e.tensor_scalar(qe, q, eps, None, ALU.add), False)
        step("cum_q", e.tensor_tensor_scan(cb, ones, q, 0.0, ALU.mult, ALU.add), False)
        e.wait_ge(*L.act("k", b))
        step("ke", e.tensor_scalar(ke, k, eps, None, ALU.add), False)
        step("cum_k", e.tensor_tensor_scan(ca, ones, k, 0.0, ALU.mult, ALU.add))
        step("flow0", e.scalar_tensor_tensor(da, ca, eps, qe, ALU.add, ALU.mult), False)
        step("flow1", e.scalar_tensor_tensor(db, cb, eps, ke, ALU.add, ALU.mult), False)
        count = M.k("count_tok").unsqueeze(2).broadcast_to([P, NC, H])
        inv_count = M.k("inv_count_tok").unsqueeze(2).broadcast_to([P, NC, H])
        heads = lambda a: a.rearrange("p (c h) -> p c h", h=H)
        features = lambda a: a.rearrange("p (c h d) -> p c h d", h=H, d=DH)
        spread = lambda a: a.unsqueeze(3).broadcast_to([P, NC, H, DH])
        e.wait_ge(*L.pe("flow0", b))
        e.wait_ge(*L.pe("flow1", b))
        step("inv", e.reciprocal(self.cols, M.ps[7][:, 0:128]))
        for n, name in enumerate(("inv_in_n", "inv_n")):
            half = heads(self.cols[:, 64 * n:64 * (n + 1)])
            step(name, e.tensor_tensor(features(self.rows[n]), spread(half), spread(count), ALU.mult), False)
        e.wait_ge(*L.pe("in_back", b))
        step("q_in_n", e.tensor_tensor(ca, q, M.ps[5][:, :], ALU.mult), False)
        e.wait_ge(*L.pe("out_back", b))
        step("k_out_n", e.tensor_tensor(cb, k, M.ps[6][:, :], ALU.mult))
        step("cum_out", e.tensor_tensor_scan(self.sink, ones, cb, 0.0, ALU.mult, ALU.add), False)
        step("cum_in", e.tensor_tensor_scan(self.src, ones, ca, 0.0, ALU.mult, ALU.add))
        step("cons0", e.scalar_tensor_tensor(da, self.sink, eps, qe, ALU.add, ALU.mult), False)
        step("cons1", e.scalar_tensor_tensor(db, self.src, eps, ke, ALU.add, ALU.mult), False)
        step("qs", e.tensor_tensor(q, ca, M.k("inv_count"), ALU.mult))
        e.wait_ge(*L.pe("cons0", b))
        e.wait_ge(*L.pe("cons1", b))
        step("sink", e.tensor_tensor(heads(self.sink_cols), heads(M.ps[7][:, 128:192]), inv_count, ALU.mult), False)
        step("src_n", e.tensor_tensor(heads(self.src_cols), heads(M.ps[7][:, 192:256]), inv_count, ALU.mult))
        step("src", e.tensor_scalar(self.src_cols, self.src_cols, -1.0, 1.0, ALU.max, ALU.min))
        e.wait_ge(*L.pe("cum_src", b))
        step("inv_src", e.reciprocal(self.comp_cols, M.ps[7][:, 256:320]))
        step("comp_n", e.tensor_tensor(self.comp_cols, self.comp_cols, self.src_cols, ALU.mult))
        step("comp", e.tensor_tensor(features(self.rows[0]), spread(heads(self.comp_cols)), spread(count), ALU.mult), False)
        e.wait_ge(*L.act("v", b))
        e.wait_ge(*L.pe("comp_back", b))
        step("vs", e.tensor_tensor(v, v, M.ps[5][:, :], ALU.mult), False)
        for r in range(4):
            step(f"masked_q{r}", e.tensor_scalar(self.masked_q[:, r, :], q, M.k("head_in_quad")[:, r:r + 1], None, ALU.mult), False)
        e.wait_ge(*L.pe("kv", b))
        for c in range(NC - 1):
            s = slice(c * P, (c + 1) * P)
            step(f"kv{c}", e.tensor_tensor(self.state[:, s], M.ps[6][:, s], M.k("same8"), ALU.mult))
            if c:
                step(f"state{c}", e.tensor_tensor(self.state[:, s], self.state[:, s], self.state[:, (c - 1) * P:c * P], ALU.add))
        upto = M.k("upto").unsqueeze(1).broadcast_to([P, 4, P])
        for u in range(4 * NC):
            e.wait_ge(*L.pe(f"scores{u}", b))
            if u >= 3:
                e.wait_ge(*L.pe(f"apply{u - 3}", b))
            dst = self.scores[u % 3].rearrange("p (r l) -> p r l", r=4)
            step(f"causal{u}", e.tensor_tensor(dst, M.ps[2 + u % 3][:, :].rearrange("p (r l) -> p r l", r=4), upto, ALU.mult), False)
        e.wait_ge(*L.pe("attended", b))
        e.wait_ge(*L.act("sink_row", b))
        step("alloc", e.tensor_tensor(da, self.sink, M.ps[5][:, :], ALU.mult), False)
        e.wait_ge(*L.pe("out", b))
        step("with_in", e.scalar_tensor_tensor(db, M.ps[2][:, :], M.w("f_bo"), M.h[:, :], ALU.add, ALU.add))
        norm_dve(e, M, L, b, "ln1", db, qe, M.w("f_ln1_g"), M.w("f_ln1_b"))
        e.wait_ge(*L.pe("down", b))
        step("with_ffn", e.scalar_tensor_tensor(ke, M.ps[6][:, :], M.w("f_b2"), qe, ALU.add, ALU.add))
        norm_dve(e, M, L, b, "ln2", ke, da, M.w("f_ln2_g"), M.w("f_ln2_b"))
        e.wait_ge(*L.dve("ln2", b))
        e.tensor_tensor(M.x[:, b, :], M.x[:, b, :], da, ALU.add).then_inc(*L.dve.mark("residual"))


class TimeMix(Layer):

    def __init__(self, M):
        self.xx, self.xk, self.xv, self.xr, self.ek, self.eku, self.sr, self.v = (M.tile(i) for i in range(8))
        self.sa, self.sb, self.t, self.den, self.num = (M.wide[:, i, :] for i in range(5))
        self.one_less, self.cols = M.small[:, 0:3], M.small[:, 4:8]
        self.decay = M.tile(8)

    def pe(self, e, M, L, b):
        L.finished(e, b)
        norm_pe(e, M, L, b, "norm", M.x[:, b, :], [])
        for n, (w, s) in enumerate((("r_Wk", self.xk), ("r_Wv", self.xv), ("r_Wr", self.xr))):
            e.wait_ge(*L.dve(f"mixed{n}", b))
            e.matmul(M.ps[2 + n][:, :], M.w(w), s[:, :], start=True, stop=True).then_inc(*L.pe.mark(f"proj{n}"))
        e.wait_ge(*L.dve("gated", b))
        e.matmul(M.ps[5][:, :], M.w("r_Wo"), self.num, start=True, stop=True).then_inc(*L.pe.mark("out"))

    def pool(self, e, M, L, b):
        norm_pool(e, M, L, b, "norm")

    def act(self, e, M, L, b):
        L.finished(e, b)
        norm_act(e, M, L, b, "norm")
        e.activation(self.cols[:, 0:1], M.w("r_spatial_decay"), ACT.Exp, scale=1.0 / T).then_inc(*L.act.mark("decay_col"))
        e.activation(self.cols[:, 1:2], M.w("r_spatial_first"), ACT.Copy, scale=1.0 / T).then_inc(*L.act.mark("first_col"))
        e.wait_ge(*L.act("first_col", b))
        e.wait_ge(*L.pe("proj0", b))
        e.activation(self.ek[:, :], M.ps[2][:, :], ACT.Exp).then_inc(*L.act.mark("ek"))
        e.activation(self.eku[:, :], M.ps[2][:, :], ACT.Exp, bias=self.cols[:, 1:2]).then_inc(*L.act.mark("eku"))
        e.wait_ge(*L.pe("proj2", b))
        e.activation(self.sr[:, :], M.ps[4][:, :], ACT.Sigmoid).then_inc(*L.act.mark("sr"))

    def dve(self, e, M, L, b):
        L.finished(e, b)
        norm_dve(e, M, L, b, "norm", M.x[:, b, :], M.h[:, :])
        Q = C // 4
        e.wait_ge(*L.dve("norm", b))
        e.tensor_copy(self.xx[0:Q, 1:T], M.h[0:Q, 0:T - 1]).then_inc(*L.dve.mark("shift_a"))
        e.memset(self.xx[0:Q, 0:1], 0.0).then_inc(*L.dve.mark("shift_b"))
        e.tensor_copy(self.xx[Q:2 * Q, 0:T - 1], M.h[Q:2 * Q, 1:T]).then_inc(*L.dve.mark("shift_c"))
        e.memset(self.xx[Q:2 * Q, T - 1:T], 0.0).then_inc(*L.dve.mark("shift_d"))
        e.tensor_copy(self.xx[2 * Q:C, :], M.h[2 * Q:C, :]).then_inc(*L.dve.mark("shift_e"))
        mixes = [M.w(n) for n in ("r_mix_k", "r_mix_v", "r_mix_r")]
        for n, m in enumerate(mixes):
            e.tensor_scalar(self.one_less[:, n:n + 1], m, -1.0, 1.0, ALU.mult, ALU.add).then_inc(*L.dve.mark(f"less{n}"))
        e.wait_ge(*L.dve("less2", b))
        for n, (m, s) in enumerate(zip(mixes, (self.xk, self.xv, self.xr))):
            e.tensor_scalar(self.t, self.xx[:, :], self.one_less[:, n:n + 1], None, ALU.mult).then_inc(*L.dve.mark(f"other{n}"))
            e.wait_ge(*L.dve(f"other{n}", b))
            e.scalar_tensor_tensor(s[:, :], M.h[:, :], m, self.t, ALU.mult, ALU.add).then_inc(*L.dve.mark(f"mixed{n}"))
            e.wait_ge(*L.dve(f"mixed{n}", b))
        e.wait_ge(*L.act("decay_col", b))
        e.tensor_scalar(self.decay[:, :], M.k("ones"), self.cols[:, 0:1], None, ALU.mult).then_inc(*L.dve.mark("decay"))
        e.wait_ge(*L.dve("decay", b))
        e.wait_ge(*L.act("ek", b))
        e.wait_ge(*L.pe("proj1", b))
        e.tensor_tensor(self.t, self.ek[:, :], M.ps[3][:, :], ALU.mult).then_inc(*L.dve.mark("ekv"))
        e.wait_ge(*L.dve("ekv", b))
        e.tensor_tensor_scan(self.sa, self.decay[:, :], self.t, 0.0, ALU.mult, ALU.add).then_inc(*L.dve.mark("scan_a"))
        e.tensor_tensor_scan(self.sb, self.decay[:, :], self.ek[:, :], 0.0, ALU.mult, ALU.add).then_inc(*L.dve.mark("scan_b"))
        e.wait_ge(*L.act("eku", b))
        e.wait_ge(*L.dve("scan_b", b))
        e.tensor_tensor(self.num, self.eku[:, :], M.ps[3][:, :], ALU.mult).then_inc(*L.dve.mark("num0"))
        e.tensor_copy(self.den, self.eku[:, :]).then_inc(*L.dve.mark("den0"))
        e.wait_ge(*L.dve("den0", b))
        e.tensor_tensor(self.num[:, 1:T], self.num[:, 1:T], self.sa[:, 0:T - 1], ALU.add).then_inc(*L.dve.mark("num"))
        e.tensor_tensor(self.den[:, 1:T], self.den[:, 1:T], self.sb[:, 0:T - 1], ALU.add).then_inc(*L.dve.mark("den"))
        e.wait_ge(*L.dve("den", b))
        e.reciprocal(self.t, self.den).then_inc(*L.dve.mark("inv"))
        e.wait_ge(*L.dve("inv", b))
        e.tensor_tensor(self.num, self.num, self.t, ALU.mult).then_inc(*L.dve.mark("wkv"))
        e.wait_ge(*L.dve("wkv", b))
        e.wait_ge(*L.act("sr", b))
        e.tensor_tensor(self.num, self.num, self.sr[:, :], ALU.mult).then_inc(*L.dve.mark("gated"))
        e.wait_ge(*L.pe("out", b))
        e.tensor_tensor(M.x[:, b, :], M.x[:, b, :], M.ps[5][:, :], ALU.add).then_inc(*L.dve.mark("residual"))


class Depth(Layer):
    def __init__(self, M):
        t, s = M.tile, M.small
        self.h_tok = t(0)
        self.onehot = t(1)[:, 0:NC * SLOTS].rearrange("p (c s) -> p c s", s=SLOTS)
        self.slot_tok = t(1)[0:SLOTS, 256:512], t(2)[0:SLOTS, :]
        self.slot_rows = t(2)
        self.cmp = t(3)
        self.row = t(4)
        self.keep = t(5)
        self.masks = M.wide[:, 0:4, :]
        self.seen = M.wide[:, 4, 0:NC * SLOTS].rearrange("p (c s) -> p c s", s=SLOTS)
        self.key_head = M.wide[:, 5:7, :].rearrange("p r t -> p (r t)").rearrange("p (h s) -> p h s", s=SLOTS)
        self.prob = M.wide[0:SLOTS, 7:9, :].rearrange("p r t -> p (r t)").rearrange("p (h s) -> p h s", s=SLOTS)
        self.prob_t = M.wide[:, 9, :]
        self.v_pair = M.wide[:, 10:12, :].rearrange("p r t -> p (r t)").rearrange("p (m f) -> p m f", f=C)
        n = lambda i: M.wide[:, 12 + i // 4, (i % 4) * P:(i % 4 + 1) * P]
        self.xs, self.hn, self.q, self.kk, self.v, self.o, self.x1, self.t1, self.t2, self.t3, self.cos, self.sin, self.ang, self.ws, self.y, self.m_sel, self.ang2 = (n(i) for i in range(17))
        self.mid = M.wide[:, 18, 0:NF * SLOTS]
        self.proc_tok = M.wide[0:SLOTS, 19, 0:C]
        self.weight, self.rank, self.tie, self.reach, self.kept = (s[:, 4 * i:4 * i + 4] for i in range(5))
        self.posf = s[:, 32:36]
        self.mx, self.den = s[0:SLOTS, 48:64], s[0:SLOTS, 64:80]
        self.both = s[:, 128:256]

    def pe(self, e, M, L, b):
        S = SLOTS
        L.finished(e, b)
        norm_pe(e, M, L, b, "norm", M.x[:, b, :], [])
        e.wait_ge(*L.dve("norm", b))
        ident = M.k("ident")
        for c in range(NC):
            e.matmul(M.ps[2][:, c:c + 1], M.h[:, c * P:(c + 1) * P], M.w("m_router"), start=True, stop=True)
            mm = e.transpose(M.ps[3][:, c * P:(c + 1) * P], M.h[:, c * P:(c + 1) * P], ident)
        mm.then_inc(*L.pe.mark("router"))
        e.wait_ge(*L.dve("weight", b))
        for c in range(NC):
            mm = e.transpose(M.ps[4][:, c * P:(c + 1) * P], self.weight[:, c:c + 1].broadcast_to([P, P]), ident)
        mm.then_inc(*L.pe.mark("weight_row"))
        e.wait_ge(*L.dve("onehot3", b))
        e.wait_ge(*L.dve("kept", b))
        e.wait_ge(*L.dve("posf", b))
        e.wait_ge(*L.act("h_tok", b))
        for i, lhs in enumerate((lambda c: self.h_tok[:, c * P:(c + 1) * P], lambda c: self.posf[:, c:c + 1].broadcast_to([P, P]),
                                 lambda c: self.weight[:, c:c + 1].broadcast_to([P, P]))):
            for c in range(NC):
                mm = e.matmul(M.ps[5][:, i * S:(i + 1) * S], lhs(c), self.onehot[:, c, :], start=(c == 0), stop=(c == NC - 1))
        mm.then_inc(*L.pe.mark("gathered"))
        for c in range(NC):
            e.transpose(M.ps[6][0:S, c * P:(c + 1) * P], self.onehot[:, c, :], ident)
            mm = e.transpose(M.ps[7][:, c * P:(c + 1) * P], self.kept[:, c:c + 1].broadcast_to([P, P]), ident)
        mm.then_inc(*L.pe.mark("slot_rows"))
        e.wait_ge(*L.dma("mask", b))
        for d in range(NC):
            for c in range(NC):
                mm = e.matmul(M.ps[2][:, d * S:(d + 1) * S], self.masks[:, c, d * P:(d + 1) * P], self.onehot[:, c, :],
                              start=(c == 0), stop=(c == NC - 1))
        mm.then_inc(*L.pe.mark("mask_rows"))
        e.wait_ge(*L.act("mask_rows", b))
        for d in range(NC):
            mm = e.matmul(M.ps[3][0:S, 0:S], self.seen[:, d, :], self.onehot[:, d, :], start=(d == 0), stop=(d == NC - 1))
        mm.then_inc(*L.pe.mark("mask"))

        e.wait_ge(*L.act("sq1", b))
        e.matmul(M.ps[4][:, 0:S], M.k("mean"), self.t1[:, 0:S], start=True, stop=True).then_inc(*L.pe.mark("ms1"))
        e.wait_ge(*L.dve("hn_twice", b))
        for i, w in enumerate(("m_wq", "m_wqr", "m_wk", "m_wkr")):
            mm = e.matmul(M.ps[2][:, i * S:(i + 1) * S], M.w(w), self.hn[:, 0:S], start=True, stop=True)
        mm.then_inc(*L.pe.mark("qk"))
        e.matmul(M.ps[5][:, 256:384], self.hn, M.w("m_wv"), start=True, stop=True).then_inc(*L.pe.mark("v"))
        e.wait_ge(*L.dve("key_head", b))
        for i in range(2):
            mm = e.matmul(M.ps[i][0:S, :], self.q[:, 0:S], self.key_head[:, 8 * i:8 * i + 8, :], start=True, stop=True)
        mm.then_inc(*L.pe.mark("scores"))
        e.wait_ge(*L.dve("prob", b))
        for m in range(H // 2):
            mm = e.matmul(M.ps[4][:, m * S:(m + 1) * S], self.prob[:, 2 * m:2 * m + 2, :].rearrange("p h s -> p (h s)"), ident[0:S, 0:S],
                          start=True, stop=True)
        mm.then_inc(*L.pe.mark("prob_t"))
        e.wait_ge(*L.act("prob_t", b))
        e.wait_ge(*L.dve("v_pair", b))
        for m in range(H // 2):
            mm = e.matmul(M.ps[0][:, 0:S], self.v_pair[:, m, :], self.prob_t[:, m * S:(m + 1) * S], start=(m == 0), stop=(m == H // 2 - 1))
        mm.then_inc(*L.pe.mark("attended"))
        e.wait_ge(*L.act("o", b))
        e.matmul(M.ps[1][:, 0:S], M.w("m_wo"), self.o[:, 0:S], start=True, stop=True).then_inc(*L.pe.mark("out"))
        e.wait_ge(*L.act("sq2", b))
        e.matmul(M.ps[0][:, 64:64 + S], M.k("mean"), self.t1[:, 0:S], start=True, stop=True).then_inc(*L.pe.mark("ms2"))
        e.wait_ge(*L.dve("h2", b))
        for f in range(NF):
            mm = e.matmul(M.ps[2][:, f * S:(f + 1) * S], M.w("m_w1")[:, f * P:(f + 1) * P], self.hn[:, 0:S], start=True, stop=True)
        mm.then_inc(*L.pe.mark("up"))
        e.wait_ge(*L.act("gelu", b))
        for f in range(NF):
            mm = e.matmul(M.ps[1][:, 64:64 + S], M.w("m_w2")[:, f * P:(f + 1) * P], self.mid[:, f * S:(f + 1) * S], start=(f == 0), stop=(f == NF - 1))
        mm.then_inc(*L.pe.mark("down"))
        e.wait_ge(*L.dve("proc", b))
        e.matmul(M.ps[0][0:S, 128:256], self.y[:, 0:S], ident, start=True, stop=True).then_inc(*L.pe.mark("proc_tok"))
        e.wait_ge(*L.act("proc_tok", b))
        e.wait_ge(*L.act("slot_rows", b))
        e.matmul(M.ps[4][:, :], self.proc_tok[0:S - 1, :], self.slot_rows[0:S - 1, :], start=True, stop=True).then_inc(*L.pe.mark("scattered"))

    def pool(self, e, M, L, b):
        norm_pool(e, M, L, b, "norm")

    def act(self, e, M, L, b):
        S = SLOTS
        L.finished(e, b)
        e.dma_start(self.masks, M.D["mask"][:, bass.ts(b, 1), :, :].rearrange("p b c t -> p (b c) t")).then_inc(*L.dma.mark("mask"))
        norm_act(e, M, L, b, "norm")
        e.wait_ge(*L.pe("router", b))
        e.activation(self.h_tok, M.ps[3][:, :], ACT.Copy).then_inc(*L.act.mark("h_tok"))
        e.wait_ge(*L.pe("weight_row", b))
        e.activation(self.row, M.ps[4][:, :], ACT.Copy).then_inc(*L.act.mark("weight_row"))
        e.wait_ge(*L.pe("slot_rows", b))
        e.activation(self.slot_rows[0:S, :], M.ps[6][0:S, :], ACT.Copy).then_inc(*L.act.mark("slot_rows"))
        e.wait_ge(*L.pe("mask_rows", b))
        e.activation(self.seen.rearrange("p c s -> p (c s)"), M.ps[2][:, 0:NC * S], ACT.Copy).then_inc(*L.act.mark("mask_rows"))
        e.wait_ge(*L.dve("xs", b))
        e.activation(self.t1[:, 0:S], self.xs[:, 0:S], ACT.Square).then_inc(*L.act.mark("sq1"))
        e.wait_ge(*L.pe("ms1", b))
        e.activation(self.t2[:, 0:S], M.ps[4][:, 0:S], ACT.Sqrt, bias=M.k("eps6")).then_inc(*L.act.mark("sd1"))
        e.wait_ge(*L.dve("reduced1", b))
        e.activation(self.sin[:, 0:S], self.ang[:, 0:S], ACT.Sin).then_inc(*L.act.mark("sin"))
        e.activation(self.cos[:, 0:S], self.ang2[:, 0:S], ACT.Sin).then_inc(*L.act.mark("cos"))
        e.wait_ge(*L.dve("centred", b))
        e.activation(self.prob.rearrange("p h s -> p (h s)"), self.prob.rearrange("p h s -> p (h s)"), ACT.Exp).then_inc(*L.act.mark("exp"))
        e.wait_ge(*L.pe("prob_t", b))
        e.activation(self.prob_t, M.ps[4][:, :], ACT.Copy).then_inc(*L.act.mark("prob_t"))
        e.wait_ge(*L.pe("attended", b))
        e.activation(self.o[:, 0:S], M.ps[0][:, 0:S], ACT.Copy).then_inc(*L.act.mark("o"))
        e.wait_ge(*L.dve("x1", b))
        e.activation(self.t1[:, 0:S], self.x1[:, 0:S], ACT.Square).then_inc(*L.act.mark("sq2"))
        e.wait_ge(*L.pe("ms2", b))
        e.activation(self.t2[:, 0:S], M.ps[0][:, 64:64 + S], ACT.Sqrt, bias=M.k("eps6")).then_inc(*L.act.mark("sd2"))
        e.wait_ge(*L.pe("up", b))
        e.activation(self.mid, M.ps[2][:, 0:NF * S], ACT.Gelu_apprx_tanh).then_inc(*L.act.mark("gelu"))
        e.wait_ge(*L.pe("proc_tok", b))
        e.activation(self.proc_tok, M.ps[0][0:S, 128:256], ACT.Copy).then_inc(*L.act.mark("proc_tok"))

    def dve(self, e, M, L, b):
        S = SLOTS
        L.finished(e, b)

        def step(name, ins, wait=True):
            ins.then_inc(*L.dve.mark(name))
            if wait:
                e.wait_ge(*L.dve(name, b))

        norm_dve(e, M, L, b, "norm", M.x[:, b, :], M.h[:, :])
        step("posf", e.tensor_copy(self.posf, M.pos[:, bass.ts(b, NC)]), False)
        e.wait_ge(*L.pe("router", b))
        step("weight", e.tensor_scalar(self.weight, M.ps[2][:, 0:NC], M.w("m_router_b"), None, ALU.add))
        e.wait_ge(*L.act("weight_row", b))
        for c in range(NC):
            w = self.weight[:, c:c + 1]
            before = M.k("before")[:, (NC - 1 - c) * P:(NC - 1 - c) * P + T]
            step(f"more{c}", e.scalar_tensor_tensor(self.cmp, self.row, w, M.k("ones"), ALU.is_gt, ALU.mult, accum_out=self.rank[:, c:c + 1]))
            step(f"tie{c}", e.scalar_tensor_tensor(self.cmp, self.row, w, before, ALU.is_equal, ALU.mult, accum_out=self.tie[:, c:c + 1]))
            step(f"reach{c}", e.scalar_tensor_tensor(self.cmp, self.row, w, M.k("ones"), ALU.is_ge, ALU.mult, accum_out=self.reach[:, c:c + 1]))
        step("rank", e.tensor_tensor(self.rank, self.rank, self.tie, ALU.add))
        step("kept", e.tensor_scalar(self.kept, self.reach, SLOTS - 0.5, None, ALU.is_gt), False)
        for c in range(NC):
            step(f"onehot{c}", e.tensor_scalar(self.onehot[:, c, :], M.k("slot"), self.rank[:, c:c + 1], None, ALU.is_equal), False)
        e.wait_ge(*L.pe("gathered", b))
        step("xs", e.tensor_copy(self.xs[:, 0:S], M.ps[5][:, 0:S]), False)
        step("ws", e.tensor_copy(self.ws[:, 0:S], M.ps[5][:, 2 * S:3 * S]), False)
        step("angle", e.tensor_scalar(self.t3[:, 0:S], M.ps[5][:, S:2 * S], M.k("mod_inv"), None, ALU.mult))
        for i, (dst, quarter) in enumerate(((self.ang2, 0.25), (self.ang, 0.0))):
            a = dst[:, 0:S]
            tmp = self.v[:, 0:S]
            step(f"turns{i}", e.tensor_scalar(tmp, self.t3[:, 0:S], 1.0 / (2 * np.pi), quarter, ALU.mult, ALU.add))
            step(f"round_up{i}", e.tensor_scalar(tmp, tmp, 12582912.0, None, ALU.add))
            step(f"round{i}", e.tensor_scalar(tmp, tmp, 12582912.0, None, ALU.subtract))
            src = self.t3[:, 0:S]
            for j, part in enumerate(TWO_PI):
                step(f"part{i}{j}", e.scalar_tensor_tensor(a, tmp, -part, src, ALU.mult, ALU.add))
                src = a
            if quarter:
                step(f"quarter{i}", e.tensor_scalar(a, a, float(np.pi / 2), None, ALU.add))
            step(f"reduced{i}", e.tensor_scalar(a, a, PI_BELOW, -PI_BELOW, ALU.min, ALU.max))
        e.wait_ge(*L.act("sd1", b))
        step("rms1", e.reciprocal(self.t3[:, 0:S], self.t2[:, 0:S]))
        step("hn", e.scalar_tensor_tensor(self.hn[:, 0:S], self.xs[:, 0:S], M.w("m_ln1"), self.t3[:, 0:S], ALU.mult, ALU.mult))
        step("hn_twice", e.tensor_copy(self.hn[:, S:2 * S], self.hn[:, 0:S]))
        e.wait_ge(*L.act("cos", b))
        step("signed", e.tensor_scalar(self.sin[:, 0:S], self.sin[:, 0:S], M.k("mod_sign"), None, ALU.mult))
        e.wait_ge(*L.pe("qk", b))
        for i, dst in enumerate((self.q, self.kk)):
            step(f"rope_a{i}", e.tensor_tensor(self.t2[:, 0:S], M.ps[2][:, 2 * i * S:(2 * i + 1) * S], self.cos[:, 0:S], ALU.mult))
            step(f"rope_b{i}", e.tensor_tensor(self.t3[:, 0:S], M.ps[2][:, (2 * i + 1) * S:(2 * i + 2) * S], self.sin[:, 0:S], ALU.mult))
            step(f"rope{i}", e.tensor_tensor(dst[:, 0:S], self.t2[:, 0:S], self.t3[:, 0:S], ALU.add))
        step("key_head", e.tensor_tensor(self.key_head, self.kk[:, 0:S].unsqueeze(1).broadcast_to([P, H, S]),
                                         M.k("head").unsqueeze(2).broadcast_to([P, H, S]), ALU.mult))
        e.wait_ge(*L.pe("v", b))
        step("v_pair", e.tensor_tensor(self.v_pair, M.k("head_of_pair").rearrange("p (m f) -> p m f", f=C),
                                       M.ps[5][:, 256:384].unsqueeze(1).broadcast_to([P, H // 2, C]), ALU.mult), False)
        e.wait_ge(*L.pe("mask", b))
        ms = self.m_sel[0:S, 0:S]
        step("mask", e.tensor_tensor(ms, M.ps[3][0:S, 0:S], M.k("last_slot")[0:S, :], ALU.add))
        e.wait_ge(*L.pe("scores", b))
        for i in range(2):
            step(f"masked{i}", e.scalar_tensor_tensor(self.prob[:, 8 * i:8 * i + 8, :], M.ps[i][0:S, :].rearrange("p (h s) -> p h s", s=S),
                                                      float(1.0 / np.sqrt(DH)), ms.unsqueeze(1).broadcast_to([S, 8, S]), ALU.mult, ALU.add))
        wide = lambda a: a.unsqueeze(2).broadcast_to([S, H, S])
        step("max", e.tensor_reduce(self.mx, self.prob, AX, ALU.max))
        step("centred", e.tensor_tensor(self.prob, self.prob, wide(self.mx), ALU.subtract))
        e.wait_ge(*L.act("exp", b))
        step("sum", e.tensor_reduce(self.den, self.prob, AX, ALU.add))
        step("inv_sum", e.reciprocal(self.den, self.den))
        step("prob", e.tensor_tensor(self.prob, self.prob, wide(self.den), ALU.mult), False)
        e.wait_ge(*L.pe("out", b))
        step("x1", e.tensor_tensor(self.x1[:, 0:S], self.xs[:, 0:S], M.ps[1][:, 0:S], ALU.add))
        e.wait_ge(*L.act("sd2", b))
        step("rms2", e.reciprocal(self.t3[:, 0:S], self.t2[:, 0:S]))
        step("h2", e.scalar_tensor_tensor(self.hn[:, 0:S], self.x1[:, 0:S], M.w("m_ln2"), self.t3[:, 0:S], ALU.mult, ALU.mult))
        e.wait_ge(*L.pe("down", b))
        step("x2", e.tensor_tensor(self.y[:, 0:S], self.x1[:, 0:S], M.ps[1][:, 64:64 + S], ALU.add))
        step("proc", e.tensor_tensor(self.y[:, 0:S], self.y[:, 0:S], self.ws[:, 0:S], ALU.mult), False)
        step("keep", e.tensor_tensor(self.keep, M.h[:, :], M.ps[7][:, :], ALU.mult))
        step("rest", e.tensor_tensor(self.keep, self.keep, M.x[:, b, :], ALU.add))
        e.wait_ge(*L.pe("scattered", b))
        step("residual", e.tensor_tensor(M.x[:, b, :], self.keep, M.ps[4][:, :], ALU.add), False)


class TokenAttention(Layer):
    SCALE = 1.0 / 8.0
    RING = 4
    MIX, TURN = 2, 3

    def __init__(self, M):
        t, w, big, s = M.tile, M.wide, M.big, M.small
        self.q = [t(i) for i in range(4)]
        self.mix = M.tiles[:, 4:8, :]
        self.k, self.v_even, self.v_odd = t(8), t(9), t(10)
        tiles = [t(11), w[:, 16, :], w[:, 17, :], M.xc[:, :], M.h2[:, :], M.rs[:, :], M.sq[:, :], M.h[:, :]]
        self.prob = [tiles[2 * i:2 * i + 2] for i in range(4)]
        self.rms_wide = M.wide[:, 0:5, :].rearrange("p a t -> p (a t)")
        self.v_block, self.comp_t = w[:, 18, :], w[:, 19, :]
        self.prob_t = [w[:, 8 * i:8 * i + 8, :].rearrange("p a t -> p (a t)").rearrange("p (j o m q) -> p j o m q", j=4, o=2, m=4) for i in range(2)]
        self.band = [big[:, 520 * i:520 * i + 514].rearrange("p (o k) -> p o k", o=2) for i in range(4)]
        self.rms = M.small[:, 240:280]
        self.comp = big[:, 2560:3104].rearrange("p (s n) -> p s n", n=17)
        self.comp_p = big[:, 3104:3616]
        self.g = big[:, 3616:3712].rearrange("p (s n) -> p s n", n=3)
        self.t = [big[:, 5 * T:6 * T], big[:, 6 * T:7 * T]]
        self.t2, self.v_twice = big[:, 7 * T:8 * T], big[:, 8 * T:9 * T]
        self.kcw = s[:, 0:32]
        self.sink = s[:, 32:40]
        self.cm, self.cd, self.gs = s[:, 64:96], s[:, 96:128], s[:, 128:160]
        self.stat = [s[:, 160 + 16 * i:176 + 16 * i] for i in range(4)]

    def before(self, e, M, which, sem):
        if which == "pool":
            e.memset(self.v_even, 0.0).then_inc(sem, 1)
            e.memset(self.v_odd, 0.0).then_inc(sem, 1)
        if which in ("pe", "act"):
            e.wait_ge(sem, 2)

    STEPS = [(c, m) for c in range(NC) for m in range(A_H // 2)]
    HEADS = [(c, h) for c in range(NC) for h in range(A_H)]

    def pe(self, e, M, L, b):
        L.finished(e, b)
        norm_pe(e, M, L, b, "norm", M.x[:, b, :], [])
        e.wait_ge(*L.dve("norm", b))
        e.matmul(M.ps[6][0:A_QC, :], M.w("a_w_qc"), M.h[:, :], start=True, stop=True).then_inc(*L.pe.mark("qc"))
        for c in range(NC):
            mm = e.matmul(M.ps[7][:, c * P:(c + 1) * P], M.h[:, c * P:(c + 1) * P], M.w("a_w_v"), start=True, stop=True)
        mm.then_inc(*L.pe.mark("v"))
        for u in range(5):
            if u == 1:
                e.wait_ge(*L.act("qc", b))
            if u >= 2:
                e.wait_ge(*L.dve(f"roped{u - 2}", b))
            for n, (wk, wq) in enumerate((("a_w_k", "a_w_q"), ("a_w_kr", "a_w_qr"))):
                if u == 0:
                    mm = e.matmul(M.ps[n][:, :], M.w(wk), M.h[:, :], start=True, stop=True)
                else:
                    mm = e.matmul(M.ps[2 * (u % 2) + n][:, :], M.w(wq, A_QC)[:, (u - 1) * P:u * P], self.qc_sb(M), start=True, stop=True)
            mm.then_inc(*L.pe.mark(f"raw{u}"))
            if u >= 1:
                self.pe_ms(e, M, L, b, u - 1)
        self.pe_ms(e, M, L, b, 4)
        e.wait_ge(*L.act("v_twice", b))
        for c in range(NC):
            mm = e.matmul(M.ps[6][:, 0:P], M.k("block_mean")[:, c * P:(c + 1) * P], self.v_twice[:, c * P:(c + 1) * P], start=(c == 0), stop=(c == NC - 1))
        mm.then_inc(*L.pe.mark("v_block"))
        for u in range(5):
            e.wait_ge(*L.act(f"rms_wide{0 if u == 0 else 1}", b))
            if u >= 2:
                e.wait_ge(*L.dve(f"normed{u - 2}", b))
            for c in range(NC):
                mm = e.transpose(M.ps[u % 2][:, c * P:(c + 1) * P], self.rms_wide[:, (u * NC + c) * P:(u * NC + c + 1) * P], M.k("ident"))
            mm.then_inc(*L.pe.mark(f"rms{u}"))
        e.wait_ge(*L.dve("kcw", b))
        e.wait_ge(*L.dve("normed4", b))
        for c, h in self.HEADS:
            rows = slice(64 * (h % 2), 64 * (h % 2) + 64)
            at = (c * 4 + h // 2) * 32
            mm = e.matmul(M.ps[(2, 7)[h % 2]][:, at:at + 19],
                          self.q[h // 2][rows, c * P:(c + 1) * P], self.kcw[rows, 0:19], start=True, stop=True)
        mm.then_inc(*L.pe.mark("block_scores"))
        n = len(self.STEPS)
        for s in range(n + self.TURN):
            if s < n:
                c, m = self.STEPS[s]
                if s == 1:
                    e.wait_ge(*L.dve("gate_in", b))
                if s >= 2:
                    e.wait_ge(*L.dve(f"window{s - 2}", b))
                for o in range(2):
                    rows = slice(64 * o, 64 * o + 64)
                    mm = e.matmul(M.ps[2 * (s % 2) + o][:, 0:(c + 1) * P], self.q[m][rows, c * P:(c + 1) * P], self.k[rows, 0:(c + 1) * P],
                                  start=True, stop=True)
                mm.then_inc(*L.pe.mark(f"scores{s}"))
            if s == 3:
                e.wait_ge(*L.dve("comp_p", b))
                for c in range(NC):
                    mm = e.transpose(M.ps[7][:, c * P:(c + 1) * P], self.comp_p[:, c * P:(c + 1) * P], M.k("ident"))
                mm.then_inc(*L.pe.mark("comp_t"))
            if s >= self.TURN:
                r = s - self.TURN
                c, m = self.STEPS[r]
                e.wait_ge(*L.dve(f"mixed{r}", b))
                if r >= 1:
                    e.wait_ge(*L.act(f"turned{r - 1}", b))
                for o in range(2):
                    for j in range(c + 1):
                        mm = e.transpose(M.ps[4 + o][:, j * P:(j + 1) * P], self.prob[r % self.RING][o][:, j * P:(j + 1) * P], M.k("ident"))
                mm.then_inc(*L.pe.mark(f"turned{r}"))
                if c >= 1:
                    self.pe_values(e, M, L, b, c - 1, m)
        for m in range(A_H // 2):
            self.pe_values(e, M, L, b, NC - 1, m)
        e.wait_ge(*L.act(f"mix{NC - 1}", b))
        for m in range(4):
            mm = e.matmul(M.ps[0][:, :], M.w("a_w_group")[:, m * P:(m + 1) * P], self.mix[:, m, :], start=(m == 0), stop=(m == 3))
        mm.then_inc(*L.pe.mark("grouped"))
        e.wait_ge(*L.act("grouped", b))
        e.matmul(M.ps[1][:, :], M.w("a_w_out"), M.sq[:, :], start=True, stop=True).then_inc(*L.pe.mark("out"))

    def qc_sb(self, M):
        return M.h2[0:A_QC, :]

    def pe_ms(self, e, M, L, b, u):
        e.wait_ge(*L.act(f"square{u}", b))
        for c in range(NC):
            mm = e.matmul(M.ps[4][:, (u * NC + c) * 2:(u * NC + c) * 2 + 2], self.square(M, u)[:, c * P:(c + 1) * P], M.k("head2"), start=True, stop=True)
        mm.then_inc(*L.pe.mark(f"ms{u}"))

    def square(self, M, u):
        return (M.sq, M.sd)[u % 2][:, :]

    def pool(self, e, M, L, b):
        norm_pool(e, M, L, b, "norm")
    def pe_values(self, e, M, L, b, c, part):
        if part == 0:
            e.wait_ge(*L.act(f"turned{(c + 1) * A_H // 2 - 1}", b))
            if c == 0:
                e.wait_ge(*L.act("comp_t", b))
                e.wait_ge(*L.dve("v_block", b))
            else:
                e.wait_ge(*L.act(f"mix{c - 1}", b))
        products = [(j, o) for j in range(c + 1) for o in range(2)]
        n = len(products)
        for j, o in products[n * part // 4:n * (part + 1) // 4]:
            e.matmul(M.ps[6][:, :], (self.v_even, self.v_odd)[o][:, j * P:(j + 1) * P], self.prob_t[c % 2][:, j, o, :, :], start=(j == 0 and o == 0), stop=False,
                     skip_group_check=True)
        if part == 3:
            for m in range(4):
                mm = e.matmul(M.ps[6][:, m * P:(m + 1) * P], self.v_block[:, m * P:(m + 1) * P], self.comp_t[:, c * P:(c + 1) * P],
                              start=False, stop=(m == 3), skip_group_check=True)
            mm.then_inc(*L.pe.mark(f"values{c}"))

    def act(self, e, M, L, b):
        L.finished(e, b)
        norm_act(e, M, L, b, "norm")
        e.wait_ge(*L.pe("qc", b))
        e.activation(self.qc_sb(M), M.ps[6][0:A_QC, :], ACT.Copy).then_inc(*L.act.mark("qc"))
        e.wait_ge(*L.pe("v", b))
        v = M.ps[7][:, :].rearrange("p (c d) -> p c d", d=P)
        for dst, lo in ((self.v_even, 0), (self.v_odd, A_D)):
            e.activation(dst.rearrange("p (c d) -> p c d", d=P)[:, :, lo:lo + A_D], v[:, :, lo:lo + A_D], ACT.Copy).then_inc(*L.act.mark(f"v{lo}"))
        e.activation(self.v_twice, M.ps[7][:, :], ACT.Copy).then_inc(*L.act.mark("v_twice"))
        for u in range(5):
            e.wait_ge(*L.dve(f"roped{u}", b))
            if u >= 2:
                e.wait_ge(*L.pe(f"ms{u - 2}", b))
            e.activation(self.square(M, u), (self.k, *self.q)[u], ACT.Square).then_inc(*L.act.mark(f"square{u}"))
        e.wait_ge(*L.pe("ms4", b))
        e.activation(self.rms, M.ps[4][:, 0:10 * NC], ACT.Sqrt, bias=M.k("eps6")).then_inc(*L.act.mark("root"))
        e.wait_ge(*L.dve("rms", b))
        for n, (lo, hi) in enumerate(((0, 1), (1, 5))):
            e.activation(self.rms_wide[:, lo * T:hi * T].rearrange("p (s d) -> p s d", d=A_D),
                         self.rms[:, lo * 8:hi * 8].unsqueeze(2).broadcast_to([P, 8 * (hi - lo), A_D]), ACT.Copy).then_inc(*L.act.mark(f"rms_wide{n}"))
        e.wait_ge(*L.dve("gate_in", b))
        e.activation(self.g, self.g, ACT.Exp, scale=-1.0).then_inc(*L.act.mark("gate_exp"))
        e.wait_ge(*L.dve("comp_c", b))
        e.activation(self.comp, self.comp, ACT.Exp, scale=self.SCALE).then_inc(*L.act.mark("comp_exp"))
        n = len(self.STEPS)
        for s in range(n + self.TURN):
            if s < n:
                c, m = self.STEPS[s]
                st, W, bw = self.stat[s % self.RING], (c + 1) * P, min(c + 1, 2) * P
                e.wait_ge(*L.dve(f"bias{s}", b))
                for o in range(2):
                    pr, bd = self.prob[s % self.RING][o][:, 0:W], self.band[s % self.RING][:, o, 256 - bw:257]
                    e.activation(pr, pr, ACT.Exp, bias=st[:, 4 + 2 * o:5 + 2 * o], scale=self.SCALE, accum_out=st[:, 8 + 2 * o:9 + 2 * o])\
                        .then_inc(*L.act.mark(f"exp{s}{'eo'[o]}"))
                    e.activation(bd, bd, ACT.Exp, bias=st[:, 5 + 2 * o:6 + 2 * o], scale=self.SCALE, accum_out=st[:, 9 + 2 * o:10 + 2 * o])\
                        .then_inc(*L.act.mark(f"exp_window{s}{'eo'[o]}"))
            if s == 3:
                e.wait_ge(*L.pe("comp_t", b))
                e.activation(self.comp_t, M.ps[7][:, :], ACT.Copy).then_inc(*L.act.mark("comp_t"))
            if s >= self.TURN:
                r = s - self.TURN
                c, m = self.STEPS[r]
                e.wait_ge(*L.pe(f"turned{r}", b))
                if c >= 2 and m == 0:
                    e.wait_ge(*L.pe(f"values{c - 2}", b))
                for o in range(2):
                    ins = e.activation(self.prob_t[c % 2][:, 0:c + 1, o, m, :], M.ps[4 + o][:, 0:(c + 1) * P].rearrange("p (j q) -> p j q", q=P), ACT.Copy)
                ins.then_inc(*L.act.mark(f"turned{r}"))
                if c >= 1 and m == A_H // 2 - 1:
                    self.act_mix(e, M, L, b, c - 1)
        self.act_mix(e, M, L, b, NC - 1)
        e.wait_ge(*L.pe("grouped", b))
        e.activation(M.sq[:, :], M.ps[0][:, :], ACT.Copy).then_inc(*L.act.mark("grouped"))

    def act_mix(self, e, M, L, b, c):
        e.wait_ge(*L.pe(f"values{c}", b))
        e.activation(self.mix[:, :, c * P:(c + 1) * P], M.ps[6][:, :].rearrange("p (m q) -> p m q", q=P), ACT.Copy).then_inc(*L.act.mark(f"mix{c}"))

    def dve(self, e, M, L, b):
        L.finished(e, b)

        def step(name, ins, wait=True):
            ins.then_inc(*L.dve.mark(name))
            if wait:
                e.wait_ge(*L.dve(name, b))

        norm_dve(e, M, L, b, "norm", M.x[:, b, :], M.h[:, :])
        step("sink", e.tensor_scalar(self.sink, M.w("a_sink"), 1.0 / self.SCALE, None, ALU.mult), False)
        step("gate_w", e.tensor_copy(self.kcw[:, 16:19], M.w("a_w_gate")), False)
        for u in range(5):
            t = self.t[u % 2]
            e.wait_ge(*L.pe(f"raw{u}", b))
            step(f"rope_a{u}", e.tensor_tensor(t, M.ps[2 * (u % 2)][:, :], M.k("rope_cos"), ALU.mult), False)
            step(f"rope_b{u}", e.tensor_tensor(self.t2, M.ps[2 * (u % 2) + 1][:, :], M.k("rope_sin"), ALU.mult))
            step(f"roped{u}", e.tensor_tensor((self.k, *self.q)[u], t, self.t2, ALU.add))
        e.wait_ge(*L.act("root", b))
        step("rms", e.reciprocal(self.rms, self.rms), False)
        for u in range(5):
            dst, g = (self.k, "a_gk") if u == 0 else (self.q[u - 1], "a_gq")
            e.wait_ge(*L.pe(f"rms{u}", b))
            step(f"normed{u}", e.scalar_tensor_tensor(dst, dst, M.w(g), M.ps[u % 2][:, :], ALU.mult, ALU.mult), u == 0)
            if u == 0:
                step("k_sum", e.tensor_reduce(self.kcw[:, 0:16], self.k.rearrange("p (n r) -> p n r", r=A_CR), AX, ALU.add))
                step("kcw", e.tensor_scalar(self.kcw[:, 0:16], self.kcw[:, 0:16], 1.0 / A_CR, None, ALU.mult))
        e.wait_ge(*L.pe("v_block", b))
        step("v_block", e.tensor_tensor(self.v_block.rearrange("p (m f) -> p m f", f=P), M.k("head_of_block").rearrange("p (m f) -> p m f", f=P),
                                        M.ps[6][:, 0:P].unsqueeze(1).broadcast_to([P, 4, P]), ALU.mult), False)
        e.wait_ge(*L.pe("block_scores", b))
        seen = M.k("blocks_seen").rearrange("p (c n) -> p c n", n=A_NB)
        gate = M.w("a_b_gate").rearrange("p (h n) -> p h n", n=3)[:, 0:4, :]
        for o, bank in enumerate((2, 7)):
            raw = M.ps[bank][:, :].rearrange("p (c m n) -> p c m n", m=4, n=32)
            comp = self.comp.rearrange("p (c m o) n -> p c m o n", m=4, o=2)[:, :, :, o, :]
            gates = self.g.rearrange("p (c m o) n -> p c m o n", m=4, o=2)[:, :, :, o, :]
            for c in range(NC):
                step(f"comp_raw{o}{c}", e.tensor_tensor(comp[:, c, :, 0:16], raw[:, c, :, 0:16], seen[:, c, :].unsqueeze(1).broadcast_to([P, 4, A_NB]), ALU.add), False)
                step(f"gate_in{o}{c}", e.tensor_tensor(gates[:, c, :, :], raw[:, c, :, 16:19], gate, ALU.add), False)
        step("gate_in", e.tensor_copy(self.comp.rearrange("p (c h) n -> p c h n", h=A_H)[:, :, :, 16],
                                      self.sink.unsqueeze(1).broadcast_to([P, NC, A_H])))
        wide = lambda a, n: a.unsqueeze(2).broadcast_to([P, NC * A_H, n])
        step("comp_max", e.tensor_reduce(self.cm, self.comp, AX, ALU.max))
        step("comp_c", e.tensor_tensor(self.comp, self.comp, wide(self.cm, 17), ALU.subtract), False)
        e.wait_ge(*L.act("gate_exp", b))
        step("gate_1", e.tensor_scalar(self.g, self.g, 1.0, None, ALU.add))
        step("gate_s", e.reciprocal(self.g, self.g))
        step("gate_sum", e.tensor_reduce(self.gs, self.g, AX, ALU.add))
        step("gate_clip", e.tensor_scalar(self.gs, self.gs, 1e-6, None, ALU.max))
        step("gate_inv", e.reciprocal(self.gs, self.gs))
        step("gates", e.tensor_tensor(self.g, self.g, wide(self.gs, 3), ALU.mult))
        e.wait_ge(*L.act("comp_exp", b))
        step("comp_sum", e.tensor_reduce(self.cd, self.comp, AX, ALU.add))
        step("comp_inv", e.reciprocal(self.cd, self.cd))
        step("comp_coef", e.tensor_tensor(self.cd, self.cd, self.g[:, :, 0], ALU.mult))
        step("comp_p", e.tensor_tensor(self.comp_p.rearrange("p (s n) -> p s n", n=A_NB), self.comp[:, :, 0:16], wide(self.cd, 16), ALU.mult), False)
        n = len(self.STEPS)
        for s in range(n + self.MIX):
            new, old = s < n, s >= self.MIX
            if new:
                c, m = self.STEPS[s]
                st, W, bw = self.stat[s % self.RING], (c + 1) * P, min(c + 1, 2) * P
                S, pr, bd = M.ps[2 * (s % 2):2 * (s % 2) + 2], self.prob[s % self.RING], self.band[s % self.RING]
            if old:
                r = s - self.MIX
                rc, rm = self.STEPS[r]
                rst, rW, rbw = self.stat[r % self.RING], (rc + 1) * P, min(rc + 1, 2) * P
                rpr, rbd = self.prob[r % self.RING], self.band[r % self.RING]

            def maximum(o):
                step(f"all{s}{'eo'[o]}", e.tensor_tensor_reduce(pr[o][:, 0:W], S[o][:, 0:W], M.k("causal")[:, T - W:T], 1.0, 3.0 * NEG,
                                                                ALU.add, ALU.max, st[:, 2 * o:2 * o + 1]), False)

            def window(o):
                h = 2 * m + o
                step(f"window{s}" if o else f"window{s}e", e.tensor_tensor_reduce(bd[:, o, 256 - bw:256], S[o][:, W - bw:W], M.k("band")[:, 256 - bw:256],
                                                                               1.0, self.sink[:, h:h + 1], ALU.add, ALU.max, st[:, 2 * o + 1:2 * o + 2]), False)

            def scaled(o):
                step(f"scaled{r}{'eo'[o]}", e.tensor_scalar(rpr[o][:, 0:rW], rpr[o][:, 0:rW], rst[:, 12 + 2 * o:13 + 2 * o], None, ALU.mult), False)

            if new:
                e.wait_ge(*L.pe(f"scores{s}", b))
                if s >= self.RING:
                    e.wait_ge(*L.pe(f"turned{s - self.RING}", b))
                step(f"window_sink{s}", e.tensor_copy(bd[:, :, 256], self.sink[:, 2 * m:2 * m + 2]), False)
                maximum(0)
            if old:
                e.wait_ge(*L.act(f"exp_window{r}o", b))
                step(f"inv_sum{r}", e.reciprocal(rst[:, 12:16], rst[:, 8:12]), not new)
            if new:
                maximum(1)
            if old:
                e.wait_ge(*L.dve(f"inv_sum{r}", b))
                step(f"coef{r}", e.tensor_tensor(rst[:, 12:16].rearrange("p (o n) -> p o n", n=2), rst[:, 12:16].rearrange("p (o n) -> p o n", n=2),
                                                 self.g[:, rc * A_H + 2 * rm:rc * A_H + 2 * rm + 2, 1:3], ALU.mult), not new)
            if new:
                window(0)
            if old:
                e.wait_ge(*L.dve(f"coef{r}", b))
                scaled(0)
            if new:
                window(1)
            if old:
                scaled(1)
            if new:
                e.wait_ge(*L.dve(f"window{s}", b))
                step(f"bias{s}", e.tensor_scalar(st[:, 4:8], st[:, 0:4], -self.SCALE, None, ALU.mult), False)
            if old:
                e.wait_ge(*L.dve(f"scaled{r}o", b))
                for o in range(2):
                    step(f"mixed{r}" if o else f"mixed{r}e", e.scalar_tensor_tensor(rpr[o][:, rW - rbw:rW], rbd[:, o, 256 - rbw:256], rst[:, 13 + 2 * o:14 + 2 * o],
                                                                                 rpr[o][:, rW - rbw:rW], ALU.mult, ALU.add), False)
        e.wait_ge(*L.pe("out", b))
        step("residual", e.tensor_tensor(M.x[:, b, :], M.x[:, b, :], M.ps[1][:, :], ALU.add), False)


class BlockProject(Layer):
    def __init__(self, M):
        self.rows = M.wide[:, 0:3, :].rearrange("p a t -> p (a t)").rearrange("p (c n) -> p c n", c=NC)

    def pe(self, e, M, L, b):
        L.finished(e, b)
        norm_pe(e, M, L, b, "norm", M.x[:, b, :], [])
        e.wait_ge(*L.dve("norm", b))
        for c in range(NC):
            e.matmul(M.ps[2 + c][:, 0:3 * C], M.h[:, c * P:(c + 1) * P], M.w("b_w"), start=True, stop=True).then_inc(*L.pe.mark(f"qkv{c}"))

    def pool(self, e, M, L, b):
        norm_pool(e, M, L, b, "norm")

    def act(self, e, M, L, b):
        L.finished(e, b)
        norm_act(e, M, L, b, "norm")
        e.wait_ge(*L.dve(f"rows{NC - 1}", b))
        e.dma_start(M.D["qkv"][bass.ts(b, T), :].rearrange("(c p) n -> p c n", p=P), self.rows).then_inc(*L.dma.mark("store"))

    def dve(self, e, M, L, b):
        L.finished(e, b)
        norm_dve(e, M, L, b, "norm", M.x[:, b, :], M.h[:, :])
        for c in range(NC):
            e.wait_ge(*L.pe(f"qkv{c}", b))
            e.tensor_tensor(self.rows[:, c, :], M.ps[2 + c][:, 0:3 * C], M.w("b_b"), ALU.add).then_inc(*L.dve.mark(f"rows{c}"))


class BlockAttend(Layer):
    turns = 1
    POOL_PRODUCTS = 2

    def __init__(self, M):
        self.qkv = M.tiles[:, :, :].rearrange("p a t -> p (a t)").rearrange("p (t n) -> p t n", t=GROUP)
        join = lambda lo, hi: M.wide[:, lo:hi, :].rearrange("p a t -> p (a t)")
        self.prod = [join(0, 4), join(4, 8), M.big[:, 0:2048], M.big[:, 2048:4096]]
        self.s = join(8, 16).rearrange("p (q k h) -> p q k h", q=GROUP, k=GROUP)
        self.out = join(16, 20).rearrange("p (h q d) -> p h q d", q=GROUP, d=DH)
        self.mx, self.den = (M.small[:, 256 * i:256 * (i + 1)].rearrange("p (q h) -> p q h", h=H) for i in range(2))

    def before(self, e, M, which, sem):
        if which == "sp":
            e.dma_start(self.qkv, M.D["qkv"].rearrange("(p t) n -> p t n", t=GROUP)).then_inc(sem, 16)
        if which in ("pool", "dve"):
            e.wait_ge(sem, 16)

    def on_pool(self, i):
        return i % 5 in (1, 3)

    def product(self, e, kind, i):
        q = i
        out = self.prod[i % 4]
        K, V = self.qkv[:, :, C:2 * C], self.qkv[:, :, 2 * C:3 * C]
        if kind == "score":
            return e.tensor_tensor(out.rearrange("p (k f) -> p k f", f=C), K, self.qkv[:, q, 0:C].unsqueeze(1).broadcast_to([P, GROUP, C]), ALU.mult)
        return e.tensor_tensor(out.rearrange("p (k h d) -> p k h d", h=H, d=DH), V.rearrange("p k (h d) -> p k h d", d=DH),
                               self.s[:, q, :, :].unsqueeze(3).broadcast_to([P, GROUP, H, DH]), ALU.mult)

    def pool(self, e, M, L, b):
        for kind in ("score", "value"):
            if kind == "value":
                e.wait_ge(*L.dve("prob", b))
            for i in range(GROUP):
                if self.on_pool(i):
                    if i >= 4:
                        e.wait_ge(*L.dve(f"{kind}_sum{i - 4}", b))
                    self.product(e, kind, i).then_inc(*L.pool.mark(f"{kind}{i}"))

    def dve(self, e, M, L, b):
        def step(name, ins):
            ins.then_inc(*L.dve.mark(name))
            e.wait_ge(*L.dve(name, b))

        def products(kind):
            for i in range(GROUP):
                if self.on_pool(i):
                    e.wait_ge(*L.pool(f"{kind}{i}", b))
                else:
                    step(f"{kind}{i}", self.product(e, kind, i))
                if kind == "score":
                    ins = e.tensor_reduce(self.s[:, i, :, :], self.prod[i % 4].rearrange("p (k h d) -> p k h d", h=H, d=DH), AX, ALU.add)
                else:
                    ins = e.tensor_reduce(self.out[:, :, i, :], self.prod[i % 4].rearrange("p (k h d) -> p h d k", h=H, d=DH), AX, ALU.add)
                ins.then_inc(*L.dve.mark(f"{kind}_sum{i}"))

        products("score")
        e.wait_ge(*L.dve(f"score_sum{GROUP - 1}", b))
        over_k = self.s.rearrange("p q k h -> p q h k")
        wide = lambda a: a.unsqueeze(2).broadcast_to([P, GROUP, GROUP, H])
        step("max", e.tensor_reduce(self.mx, over_k, AX, ALU.max))
        step("centred", e.tensor_tensor(self.s, self.s, wide(self.mx), ALU.subtract))
        e.wait_ge(*L.act("exp", b))
        step("sum", e.tensor_reduce(self.den, over_k, AX, ALU.add))
        step("inv", e.reciprocal(self.den, self.den))
        step("prob", e.tensor_tensor(self.s, self.s, wide(self.den), ALU.mult))
        products("value")

    def act(self, e, M, L, b):
        e.wait_ge(*L.dve("centred", b))
        flat = self.s.rearrange("p q k h -> p (q k h)")
        e.activation(flat, flat, ACT.Exp, scale=float(1.0 / np.sqrt(DH))).then_inc(*L.act.mark("exp"))

    def sp(self, e, M, L, b):
        e.wait_ge(*L.dve(f"value_sum{GROUP - 1}", b))
        rows = M.D["attended"].rearrange("(b h j) f -> b j h f", b=B, h=H)
        runs = T // GROUP
        for n in range(B):
            e.dma_start(rows[n], self.out[n * runs:(n + 1) * runs, :, :, :].rearrange("p h q d -> p h (q d)")).then_inc(*L.dma.mark(f"store{n}"))


class BlockMerge(Layer):
    def __init__(self, M):
        self.rows = M.tile(0)

    def act(self, e, M, L, b):
        L.finished(e, b)
        e.dma_start(self.rows.rearrange("p (c f) -> p c f", c=NC), M.D["attended"][bass.ts(b, T), :].rearrange("(c p) f -> p c f", p=P))\
            .then_inc(*L.dma.mark("load"))

    def pe(self, e, M, L, b):
        L.finished(e, b)
        e.wait_ge(*L.dma("load", b))
        for c in range(NC):
            mm = e.transpose(M.ps[0][:, c * P:(c + 1) * P], self.rows[:, c * P:(c + 1) * P], M.k("ident"))
        mm.then_inc(*L.pe.mark("turned"))

    def dve(self, e, M, L, b):
        e.wait_ge(*L.pe("turned", b))
        e.tensor_tensor(M.x[:, b, :], M.x[:, b, :], M.ps[0][:, :], ALU.add).then_inc(*L.dve.mark("residual"))


class Memory:
    def __init__(self, nc, ctx, const_cols, param_cols):
        def sb(name, shape, dt=F32):
            return ctx.enter_context(nc.sbuf_tensor(name, shape, dt))

        self.const_cols, self.param_cols = const_cols, param_cols
        self.consts = sb("consts", [P, max(b for a, b in const_cols.values())])
        self.params = sb("params", [P, max(b for a, b in param_cols.values())])
        self.x = sb("x", [P, B, T])
        self.h = sb("h", [P, T])
        self.norm_cols = sb("norm_cols", [P, 2 * NC])
        self.h2 = sb("h2", [P, T])
        self.xc, self.sq, self.sd, self.rs = (sb(n, [P, T]) for n in ("xc", "sq", "sd", "rs"))
        self.tiles = sb("tiles", [P, 12, T])
        self.wide = sb("wide", [P, 20, T])
        self.big = sb("big", [P, 9 * T])
        self.small = sb("small", [P, 640])
        self.expert_gate = sb("expert_gate", [P, E, F])
        self.expert_up = sb("expert_up", [P, E, F])
        self.expert_out = sb("expert_out", [P, E, NF, C])
        self.pos = sb("pos", [P, B * NC], I32)
        self.zeros = sb("zeros", [P, T])
        self.slot_index = sb("slot_index", [P, 2 * TOP * CHUNKS], I32)
        self.ps = [ctx.enter_context(nc.psum_tensor(f"bank{i}", [P, T], F32)) for i in range(8)]

    def k(self, name):
        a, b = self.const_cols[name]
        return self.consts[:, a:b]

    def w(self, name, rows=P):
        a, b = self.param_cols[name]
        return self.params[0:rows, a:b]

    def tile(self, i):
        return self.tiles[:, i, :]


KINDS = {1: [TokenAttention], 2: [Route, Experts], 3: [Flow], 4: [Route, Experts], 5: [TimeMix], 6: [Depth],
         7: [BlockProject, BlockAttend, BlockMerge], 8: [Depth]}
LAYERS = [1, 2, 3, 4, 5, 6, 7, 8]


def program(nc, D, const_cols, param_cols, plan=None):
    with ExitStack() as ctx:
        def sem(name):
            return ctx.enter_context(nc.semaphore(name))

        M = Memory(nc, ctx, const_cols, param_cols)
        M.D = D
        loaded, experts_loaded, stored = sem("loaded"), sem("experts_loaded"), sem("stored")
        zeroed, M.slots_cleared = sem("zeroed"), sem("slots_cleared")
        layers, prepared = [], {}
        for n in LAYERS:
            for i, cls in enumerate(KINDS[n]):
                name = f"l{n}_{i}"
                layers.append((cls(M), Stage(name, sem, plan, cls.turns, cls.lanes)))
                prepared[name] = sem(f"{name}_prepared")
        block = ctx.enter_context(nc.Block())

        def run(e, which):
            before = None
            for layer, L in layers:
                work, after = layer.parts()[which]
                if before is not None:
                    before.finished(e)
                counter = L.counters["dma" if which == "sp" else which]
                if counter.order is None or counter.order:
                    e.sem_inc(counter.sem, 1)
                layer.before(e, M, which, prepared[L.name])
                if work is not None:
                    if layer.needs_experts and which == "pe":
                        e.wait_ge(experts_loaded, 3 * 16)
                    if layer.turns == 1:
                        work(e, M, L, 0)
                    else:
                        with e.Fori(0, layer.turns) as b:
                            work(e, M, L, b)
                if after is not None:
                    after(e, M, L)
                before = L
            return before

        @block.tensor
        def _(pe):
            pe.wait_ge(loaded, 4 * 16)
            run(pe, "pe")

        @block.scalar
        def _(act):
            act.wait_ge(loaded, 4 * 16)
            run(act, "act")

        @block.vector
        def _(dve):
            dve.wait_ge(loaded, 4 * 16)
            run(dve, "dve")

        @block.gpsimd
        def _(pool):
            pool.memset(M.zeros[:, :], 0.0).then_inc(zeroed, 1)
            pool.wait_ge(loaded, 4 * 16)
            run(pool, "pool")

        @block.sync
        def _(sp):
            sp.dma_start(M.x[:, :, :], D["x"]).then_inc(loaded, 16)
            sp.dma_start(M.consts[:, :], D["consts"]).then_inc(loaded, 16)
            sp.dma_start(M.params[:, :], D["params"]).then_inc(loaded, 16)
            sp.dma_start(M.pos[:, :], D["pos"]).then_inc(loaded, 16)
            sp.wait_ge(zeroed, 1)
            sp.dma_start(D["slots"][0:E * HOLD, :].rearrange("(p n r) c -> p n (r c)", p=P, r=T // C), M.zeros[:, :].unsqueeze(1).broadcast_to([P, HOLD * E * C // P // T, T])).then_inc(M.slots_cleared, 16)
            sp.dma_start(M.expert_gate[:, :, :], D["wi_gate"]).then_inc(experts_loaded, 16)
            sp.dma_start(M.expert_up[:, :, :], D["wi_up"]).then_inc(experts_loaded, 16)
            sp.dma_start(M.expert_out[:, :, :, :], D["wo"]).then_inc(experts_loaded, 16)
            last = run(sp, "sp")
            last.finished(sp)
            sp.dma_start(D["out"], M.x[:, :, :]).then_inc(stored, 16)
            sp.wait_ge(stored, 16)
            sp.wait_ge(experts_loaded, 3 * 16)
        return {L.name: {k: c.seen for k, c in L.counters.items()} for _, L in layers}


def kernel(**inputs):
    import concourse.bacc as bacc
    from concourse.bass_utils import run_bass_kernel_spmd

    a = {k: np.asarray(v) for k, v in inputs.items()}

    def pack(named):
        cols, at = {}, 0
        for n, m in named.items():
            cols[n] = (at, at + m.shape[1])
            at += m.shape[1]
        return np.ascontiguousarray(np.concatenate(list(named.values()), axis=1)), cols

    consts, const_cols = pack(constants())
    params, param_cols = pack(parameters(a))
    lay = lambda m: np.ascontiguousarray(m)
    arrays = {
        "x": lay(a["L0_attn_a_h"].transpose(2, 0, 1)),
        "consts": consts,
        "params": params,
        "pos": lay(a["L1_ffn_position_ids"].reshape(B, NC, P).transpose(2, 0, 1).reshape(P, B * NC)),
        "wi_gate": lay(a["L0_ffn_wi_gate"].transpose(2, 0, 1)),
        "wi_up": lay(a["L0_ffn_wi_up"].transpose(2, 0, 1)),
        "wo": lay(a["L0_ffn_wo"].reshape(E, C, NF, P).transpose(3, 0, 2, 1)),
        "mask": lay(a["L1_ffn_attention_mask"].reshape(B, NC, P, T).transpose(2, 0, 1, 3)),
    }

    def declare(nc):
        D = {n: nc.dram_tensor(f"in_{n}", m.shape, mybir.dt.from_np(m.dtype), kind="ExternalInput").ap() for n, m in arrays.items()}
        D["out"] = nc.dram_tensor("out_x", (P, B, T), F32, kind="ExternalOutput").ap()
        D["slots"] = nc.dram_tensor("expert_slots", (E * HOLD + TOP * B * T, C), F32).ap()
        D["slots_out"] = nc.dram_tensor("expert_slots_out", (E * HOLD, C), F32).ap()
        D["qkv"] = nc.dram_tensor("qkv_tokens", (B * T, 3 * C), F32).ap()
        D["attended"] = nc.dram_tensor("attended_tokens", (B * T, C), F32).ap()
        return D

    draft = bacc.Bacc("TRN2", target_bir_lowering=False, num_devices=1)
    plan = program(draft, declare(draft), const_cols, param_cols)
    nc = bacc.Bacc("TRN2", target_bir_lowering=False, num_devices=1)
    assert program(nc, declare(nc), const_cols, param_cols, plan) == plan
    r = run_bass_kernel_spmd(nc, [{f"in_{n}": m for n, m in arrays.items()}], core_ids=[0])
    return lay(r.results[0]["out_x"].transpose(1, 2, 0))
```

```python
from contextlib import ExitStack

import numpy as np

import concourse.bass as bass
from concourse import mybir

ALU = mybir.AluOpType
ACT = mybir.ActivationFunctionType
AX = mybir.AxisListType.X
F32 = mybir.dt.float32
I32 = mybir.dt.int32

B, T, C = 4, 512, 128
P = 128
NC = T // P
A_H, A_D, A_CR = 8, 64, 32
A_NB = T // A_CR
A_WINDOW, A_QC, A_ROPE = 64, 32, 32
H, DH = 16, 8
F, E = 512, 8
NF = F // P
CAPACITY = int(B * T / E * 1.25)
SLOTS = T // 8
GROUP = 16
CHUNKS = B * T // P
TOP = 2
HOLD = TOP * CAPACITY
PIECES = HOLD // P
NEG = -1e30
PI_BELOW = 3.1415925

def split_two_pi():
    rest, parts = 2 * np.pi, []
    for bits in (2.0 ** -8, 2.0 ** -19):
        parts.append(float(np.floor(rest / bits) * bits))
        rest -= parts[-1]
    return parts + [float(np.float32(rest))]

TWO_PI = split_two_pi()

def constants():
    p = np.arange(P)
    f = lambda a: np.asarray(a, np.float32).reshape(P, -1)
    k = {}
    k["mean"] = f(np.full((P, P), 1.0 / C))
    k["ident"] = f(np.eye(P))
    k["ones"] = f(np.ones((P, T)))
    k["head2"] = f(np.where(p[:, None] // 64 == np.arange(2)[None, :], 1.0 / 64, 0.0))
    k["same8"] = f(p[:, None] // DH == p[None, :] // DH)
    k["feature"] = f(p[:, None] % DH == np.arange(DH)[None, :])
    k["upto"] = f(p[:, None] <= p[None, :])
    half = A_ROPE // 2
    inv = (np.float32(1.0) / np.float32(10000.0) ** (np.arange(half, dtype=np.float32) * np.float32(2.0) / np.float32(A_ROPE))).astype(np.float32)
    ang = np.arange(T, dtype=np.float32)[:, None] * inv[None, :]
    cos, sin = np.cos(ang), np.sin(ang)
    c64, s64 = np.ones((A_D, T), np.float32), np.zeros((A_D, T), np.float32)
    c64[:half], c64[half:2 * half] = cos.T, cos.T
    s64[:half], s64[half:2 * half] = -sin.T, sin.T
    k["rope_cos"], k["rope_sin"] = f(np.tile(c64, (2, 1))), f(np.tile(s64, (2, 1)))
    causal = np.zeros((P, T))
    causal[:, T - P:] = np.where(p[:, None] >= p[None, :], 0.0, NEG)
    k["causal"] = f(causal)
    d = (p[:, None] + P) - np.arange(2 * P)[None, :]
    k["band"] = f(np.where((d >= 0) & (d < A_WINDOW), 0.0, NEG))
    blk_end = (np.arange(A_NB) + 1) * A_CR - 1
    q = p[:, None] + P * np.arange(NC)[None, :]
    k["blocks_seen"] = f(np.where(blk_end[None, None, :] <= q[:, :, None], 0.0, NEG))
    rep = np.zeros((P, NC, A_H, A_NB))
    for c in range(NC):
        rep[p, c, :, (P * c + p) // A_CR] = 1.0 / A_CR
    k["block_mean"] = f(rep)
    hn = p // A_NB
    vc = np.zeros((P, A_H // 2, 2, A_D))
    for h in range(A_H):
        vc[hn == h, h // 2, h % 2, :] = 1.0
    k["head_of_block"] = f(vc)
    k["head"] = f(p[:, None] // DH == np.arange(H)[None, :])
    k["count_tok"] = f(P * np.arange(NC)[None, :] + p[:, None] + 1.0)
    k["inv_count_tok"] = f(1.0 / (P * np.arange(NC)[None, :] + p[:, None] + 1.0))
    k["expert_rank"] = f(np.tile(np.arange(E) - 99.0, (P, 1)))
    k["slot_before"] = f(np.tile((np.arange(E)[None, :] * HOLD + np.arange(TOP)[:, None] * CAPACITY - 1.0).reshape(-1), (P, 1)))
    k["spare_slot"] = f(E * HOLD + np.arange(TOP)[None, :, None] * B * T + np.arange(CHUNKS)[None, None, :] * P + p[:, None, None])
    u = np.arange(T + (NC - 1) * P)
    k["before"] = f(u[None, :] < p[:, None] + (NC - 1) * P)
    k["slot"] = f(np.tile(np.arange(SLOTS), (P, 1)))
    k["last_slot"] = f(np.tile(np.where(np.arange(SLOTS) == SLOTS - 1, NEG, 0.0), (P, 1)))
    hinv = 1.0 / np.float32(10000.0) ** (np.arange(0, DH, 2, dtype=np.float32) / np.float32(DH))
    k["mod_inv"] = f(hinv[(p % DH) % (DH // 2)])
    k["mod_sign"] = f(np.where(p % DH < DH // 2, -1.0, 1.0))
    pair = np.zeros((P, H // 2, H))
    for m in range(H // 2):
        pair[:, m, :] = np.arange(H)[None, :] == 2 * m + (p[:, None] // SLOTS)
    k["head_of_pair"] = f(pair)
    k["minus_half"] = f(np.full((P, NC), -0.5))
    k["eps6"] = f(np.full((P, 1), 1e-6))
    return k

def _swap(n, lo, hi):
    h = (hi - lo) // 2
    o = np.arange(n)
    o[lo:lo + h], o[lo + h:hi] = np.arange(lo + h, hi), np.arange(lo, lo + h)
    return o

def parameters(a):
    k = {}

    def col(v):
        return v.reshape(P, 1)

    def rows(m):
        return m.reshape(-1, P, m.shape[1]).transpose(1, 0, 2).reshape(P, -1)

    def tall(m):
        out = np.zeros((P, m.shape[1]), m.dtype)
        out[:m.shape[0]] = m
        return out

    rot = _swap(A_D, 0, A_ROPE)
    g = "L0_attn_a_"
    k["a_w_qc"] = a[g + "w_qc"]
    qup = a[g + "w_qup"]
    k["a_w_q"] = tall(qup)
    k["a_w_qr"] = tall(qup.reshape(A_QC, A_H, A_D)[:, :, rot].reshape(A_QC, -1))
    k["a_w_k"] = np.tile(a[g + "w_k"], (1, 2))
    k["a_w_kr"] = np.tile(a[g + "w_k"][:, rot], (1, 2))
    k["a_w_v"] = np.tile(a[g + "w_v"], (1, 2))
    k["a_gq"] = col(np.tile(a[g + "g_qnorm"], 2))
    k["a_gk"] = col(np.tile(a[g + "g_knorm"], 2))
    k["a_w_gate"] = np.tile(a[g + "w_gate"], (2, 1))
    k["a_b_gate"] = np.tile(a[g + "b_gate"], (P, A_H))
    k["a_sink"] = np.tile(a[g + "sink_logit"], (P, 1))
    wog = a[g + "w_out_group"]
    wide = np.zeros((4, P, P), wog.dtype)
    for pr in range(4):
        gg = pr // 2
        wide[pr, :, gg * 64:(gg + 1) * 64] = wog[gg, (pr % 2) * P:(pr % 2 + 1) * P]
    k["a_w_group"] = wide.transpose(1, 0, 2).reshape(P, -1)
    k["a_w_out"] = a[g + "w_out"]
    g = "L0_attn_b_"
    for n in ("Wq", "Wk", "Wv", "Wo", "W1"):
        k["f_" + n] = a[g + n]
    for n in ("bq", "bk", "bv", "bo", "b2", "ln1_g", "ln1_b", "ln2_g", "ln2_b"):
        k["f_" + n] = col(a[g + n])
    k["f_b1"] = a[g + "b1"].reshape(NF, P).T
    k["f_W2"] = rows(a[g + "W2"])
    k["e_gate"] = a["L0_ffn_gate_w"].T
    g = "L1_attn_a_"
    for n in ("Wk", "Wv", "Wr", "Wo"):
        k["r_" + n] = a[g + n].T
    for n in ("spatial_decay", "spatial_first", "mix_k", "mix_v", "mix_r"):
        k["r_" + n] = col(a[g + n])
    k["b_w"] = a["L1_attn_b_w_qkv"].T
    k["b_b"] = np.tile(a["L1_attn_b_b_qkv"], (P, 1))
    g = "L1_ffn_"
    rot = _swap(DH, 0, DH)
    k["m_router"] = a[g + "router_w"]
    k["m_router_b"] = np.tile(a[g + "router_b"], (P, 1))
    for n in ("wq", "wk"):
        k["m_" + n] = a[g + n]
        k["m_" + n + "r"] = a[g + n].reshape(C, H, DH)[:, :, rot].reshape(C, C)
    for n in ("wv", "wo", "w1"):
        k["m_" + n] = a[g + n]
    k["m_w2"] = rows(a[g + "w2"])
    k["m_ln1"], k["m_ln2"] = col(a[g + "ln1"]), col(a[g + "ln2"])
    return k

class Steps:

    def __init__(self, sem, order, turns):
        self.sem, self.order, self.turns, self.seen = sem, order, turns, []

    def mark(self, name):
        if self.seen and name == self.seen[0]:
            self.seen = []
        assert name not in self.seen, name
        self.seen.append(name)
        return self.sem, self.unit

    unit = 1
    entered = 1

    def __call__(self, name, turn):
        if self.order is None:
            return self.sem, 1
        return self.sem, turn * (len(self.order) * self.unit) + ((self.order.index(name) + 1) * self.unit + self.entered)

    def end(self, turns=None):
        n = 1 if self.order is None else len(self.order)
        return self.sem, (self.turns if turns is None else turns) * (n * self.unit) + self.entered

class DmaSteps(Steps):
    unit = 16

class LaneSteps(DmaSteps):
    entered = 0

class Stage:

    def __init__(self, name, sem, plan, turns=B, lanes=()):
        self.name = name
        self.counters = {}
        for lane in lanes:
            order = None if plan is None else plan[name][lane]
            self.counters[lane] = LaneSteps(sem(f"{name}_{lane}"), order, turns)
            self.lanes = self.counters
        for engine in ("pe", "act", "dve", "pool", "dma"):
            kind = DmaSteps if engine == "dma" else Steps
            order = None if plan is None else plan[name][engine]
            if order is None or order:
                self.counters[engine] = kind(sem(f"{name}_{engine}"), order, turns)
            else:
                self.counters[engine] = kind(None, [], turns)
        self.pe, self.act, self.dve, self.pool, self.dma = (self.counters[k] for k in ("pe", "act", "dve", "pool", "dma"))

    def finished(self, e, turns=None):
        for c in self.counters.values():
            if c.order is None or c.order:
                e.wait_ge(*c.end(turns))

class Layer:
    turns = B
    needs_experts = False
    lanes = ()
    prepares = False
    pe = act = dve = pool = sp = None

    def before(self, e, M, which, sem):
        pass

    def parts(self):
        return {"pe": self.pe, "act": self.act, "dve": self.dve, "pool": self.pool, "sp": self.sp}

class Norm(Layer):
    turns = 1
    gain = shift = None

    def source(self, M):
        return M.x

    def __init__(self, M):
        self.square = [M.sq, M.sd]
        self.cols = M.norm_cols

    def pe(self, e, M, L, b):
        for i in range(B + 2):
            if i < B:
                if i >= 2:
                    e.wait_ge(*L.dve(f"centred{i - 2}", 0))
                e.matmul(M.ps[i % 2][:, :], M.k("mean"), self.source(M)[:, i, :], start=True, stop=True).then_inc(*L.pe.mark(f"mean{i}"))
            if 1 <= i <= B:
                j = i - 1
                e.wait_ge(*L.act(f"square{j}", 0))
                if j >= 2:
                    e.wait_ge(*L.dve(f"var{j - 2}", 0))
                for c in range(NC):
                    mm = e.matmul(M.ps[2 + j % 2][:, c:c + 1], self.square[j % 2][:, c * P:(c + 1) * P], M.k("mean")[:, 0:1], start=True, stop=True)
                mm.then_inc(*L.pe.mark(f"var{j}"))
            if i >= 2:
                j = i - 2
                e.wait_ge(*L.pool(f"inv{j}", 0))
                if j >= 2:
                    e.wait_ge(*L.dve(f"norm{j - 2}", 0))
                for c in range(NC):
                    mm = e.transpose(M.ps[4 + j % 2][:, c * P:(c + 1) * P], self.inv(j)[:, c:c + 1].broadcast_to([P, P]), M.k("ident"))
                mm.then_inc(*L.pe.mark(f"inv{j}"))

    def var(self, i):
        return self.cols[:, NC * i:NC * (i + 1)]

    def inv(self, i):
        return self.cols[:, NC * (B + i):NC * (B + i + 1)]

    def act(self, e, M, L, b):
        for i in range(B):
            e.wait_ge(*L.dve(f"centred{i}", 0))
            if i >= 2:
                e.wait_ge(*L.pe(f"var{i - 2}", 0))
            e.activation(self.square[i % 2][:, :], M.hs[:, i, :], ACT.Square).then_inc(*L.act.mark(f"square{i}"))

    def pool(self, e, M, L, b):
        for i in range(B):
            e.wait_ge(*L.dve(f"var{i}", 0))
            e.tensor_tensor(self.inv(i), self.var(i), M.k("minus_half")[:, 0:NC], ALU.pow).then_inc(*L.pool.mark(f"inv{i}"))

    def dve(self, e, M, L, b):
        for i in range(B + 2):
            if i < B:
                e.wait_ge(*L.pe(f"mean{i}", 0))
                e.tensor_tensor(M.hs[:, i, :], self.source(M)[:, i, :], M.ps[i % 2][:, :], ALU.subtract).then_inc(*L.dve.mark(f"centred{i}"))
            if 1 <= i <= B:
                j = i - 1
                e.wait_ge(*L.pe(f"var{j}", 0))
                e.tensor_scalar(self.var(j), M.ps[2 + j % 2][:, 0:NC], 1e-5, None, ALU.add).then_inc(*L.dve.mark(f"var{j}"))
            if i >= 2:
                j = i - 2
                e.wait_ge(*L.pe(f"inv{j}", 0))
                if self.gain is None:
                    e.tensor_tensor(M.hs[:, j, :], M.hs[:, j, :], M.ps[4 + j % 2][:, :], ALU.mult).then_inc(*L.dve.mark(f"norm{j}"))
                else:
                    e.scalar_tensor_tensor(M.hs[:, j, :], M.hs[:, j, :], M.w(self.gain), M.ps[4 + j % 2][:, :], ALU.mult, ALU.mult)\
                        .then_inc(*L.dve.mark(f"norm{j}"))
                    e.wait_ge(*L.dve(f"norm{j}", 0))
                    self.shifted(e, M, j).then_inc(*L.dve.mark(f"shifted{j}"))

class Route(Layer):
    turns = 1

    def __init__(self, M):
        self.h_tok = M.wide[:, 0:B, :]
        self.lg = M.wide[:, 12, 0:CHUNKS * E]

    def pe(self, e, M, L, b):
        for i in range(CHUNKS):
            h = M.hs[:, i // NC, i % NC * P:(i % NC + 1) * P]
            mm = e.matmul(M.ps[0][:, i * E:(i + 1) * E], h, M.w("e_gate"), start=True, stop=True)
        mm.then_inc(*L.pe.mark("logits"))
        for i in range(CHUNKS):
            h = M.hs[:, i // NC, i % NC * P:(i % NC + 1) * P]
            mm = e.transpose(M.ps[4 + i // NC][:, i % NC * P:(i % NC + 1) * P], h, M.k("ident"))
            if i % NC == NC - 1:
                mm.then_inc(*L.pe.mark(f"turned{i // NC}"))

    def act(self, e, M, L, b):
        for i in range(B):
            e.wait_ge(*L.pe(f"turned{i}", 0))
            e.activation(self.h_tok[:, i, :], M.ps[4 + i][:, :], ACT.Copy).then_inc(*L.act.mark(f"h_tok{i}"))

    def dve(self, e, M, L, b):
        e.wait_ge(*L.pe("logits", 0))
        e.tensor_copy(self.lg, M.ps[0][:, 0:CHUNKS * E]).then_inc(*L.dve.mark("lg"))

class Experts(Layer):
    needs_experts = True
    turns = 1
    lanes = ("scatter", "load0", "load1", "store0", "store1") + tuple(f"fetch{b}" for b in range(B))

    def __init__(self, M):
        self.h_tok = M.wide[:, 0:B, :].rearrange("p b (c f) -> p (b c) f", f=C)
        self.fetched = M.wide[:, 4:12, :].rearrange("p (k b) (c f) -> p k (b c) f", k=TOP, f=C)
        self.combined = self.h_tok
        w = M.wide[:, 12:19, :].rearrange("p r t -> p (r t)")
        at = [0]

        def take(*dims):
            n = int(np.prod(dims))
            a = w[:, at[0]:at[0] + n]
            at[0] += n
            return a.rearrange("p (c k) -> p c k", k=dims[1]) if len(dims) == 2 else a

        self.lg = take(CHUNKS, E)
        self.eq, self.tmp = take(CHUNKS, E), take(CHUNKS, E)
        self.chosen, self.place, self.free = (take(CHUNKS, TOP * E) for _ in range(3))
        self.sums = [take(CHUNKS // 2 + CHUNKS, TOP * E) for _ in range(2)]
        self.m1, self.m2, self.pick, self.e2, self.w1, self.w2 = (take(CHUNKS) for _ in range(6))
        self.row, self.valid, self.weight, self.to, self.gather = (take(TOP * CHUNKS).rearrange("p (k c) -> p k c", k=TOP) for _ in range(5))
        self.scatter_i, self.gather_i = M.slot_index[:, 0:TOP * CHUNKS], M.slot_index[:, TOP * CHUNKS:2 * TOP * CHUNKS]
        big = M.big[:, 0:6 * HOLD].rearrange("p (i s) -> p i s", s=HOLD)
        self.rows_in, self.x_in, self.rows_out = ([big[:, 2 * i + j, :] for j in range(2)] for i in range(3))
        t = M.tiles.rearrange("p r t -> p (r t)")
        self.mid = [t[:, i * NF * HOLD:(i + 1) * NF * HOLD].rearrange("p (f s) -> p f s", f=NF) for i in range(2)]
        self.silu = [M.h, M.h2, M.xc]

    HALVES = [(0, HOLD // P // 2 * P + P), (HOLD // P // 2 * P + P, HOLD)]
    UNITS = [(f, h) for f in range(NF) for h in range(2)]
    N = len(UNITS)

    def sp(self, e, M, L, b):
        slots = M.D["slots"][0:E * HOLD, :].rearrange("(x p r) c -> x p (r c)", x=E, p=P)
        out = M.D["slots_out"].rearrange("(x p r) c -> x p (r c)", x=E, p=P)
        e.wait_ge(*L.counters["scatter"].end())

        def load(x):
            if x >= 2:
                e.wait_ge(*L.pe(f"x_in{x - 2}", 0))
            e.dma_start(self.rows_in[x % 2], slots[x, :, :]).then_inc(*L.counters[f"load{x % 2}"].mark(f"rows{x}"))

        load(0)
        load(1)
        for x in range(E):
            if x + 2 < E:
                load(x + 2)
            e.wait_ge(*L.dve(f"rows_out{x}_1", 0))
            e.dma_start(out[x, :, :], self.rows_out[x % 2]).then_inc(*L.counters[f"store{x % 2}"].mark(f"stored{x}"))

    def pool(self, e, M, L, b):
        e.wait_ge(M.slots_cleared, 16)
        e.wait_ge(*L.dve("scatter_i", 0))
        for i in range(TOP * CHUNKS):
            e.indirect_dma_start(M.D["slots"], bass.IndirectOffsetOnAxis(self.scatter_i[:, i:i + 1], 0), self.h_tok[:, i % CHUNKS, :], None)\
                .then_inc(*L.counters["scatter"].mark(f"scatter{i}"))
        e.wait_ge(*L.dve("gather_i", 0))
        e.wait_ge(*L.counters["store0"].end())
        e.wait_ge(*L.counters["store1"].end())
        for c in range(CHUNKS):
            for k in range(TOP):
                i = k * CHUNKS + c
                e.indirect_dma_start(self.fetched[:, k, c, :], None, M.D["slots_out"], bass.IndirectOffsetOnAxis(self.gather_i[:, i:i + 1], 0))\
                    .then_inc(*L.counters[f"fetch{c // NC}"].mark(f"fetch{i}"))

    def pe(self, e, M, L, b):
        e.wait_ge(*L.dve("chosen2", 0))
        chosen = self.chosen.rearrange("p c k -> p (c k)")
        n = CHUNKS * TOP * E
        e.matmul(M.ps[0][:, 0:n], M.k("upto"), chosen, start=True, stop=True)
        e.matmul(M.ps[1][:, 0:n], M.k("ones")[:, 0:P], chosen, start=True, stop=True).then_inc(*L.pe.mark("counted"))
        e.wait_ge(*L.dve("free", 0))

        def rows_to_columns(x):
            e.wait_ge(*L.counters[f"load{x % 2}"](f"rows{x}", 0))
            if x >= 1:
                e.wait_ge(*L.act(f"x_in{x - 1}_1", 0))
            for h, (lo, hi) in enumerate(self.HALVES):
                for s in range(lo, hi, P):
                    mm = e.transpose(M.ps[4 + h][:, s - lo:s - lo + P], self.rows_in[x % 2][:, s:s + P], M.k("ident"))
            mm.then_inc(*L.pe.mark(f"x_in{x}"))

        def down(x, i):
            h = 0 if i * P < self.HALVES[0][1] else 1
            lo = self.HALVES[h][0]
            e.wait_ge(*L.dve(f"mid{x}_{self.N - 1}", 0))
            if x >= 1:
                e.wait_ge(*L.dve(f"rows_out{x - 1}_{h}", 0))
            for f in range(NF):
                mm = e.matmul(M.ps[6 + h][:, i * P - lo:(i + 1) * P - lo], self.mid[x % 2][:, f, i * P:(i + 1) * P], M.expert_out[:, x, f, :],
                              start=(f == 0), stop=(f == NF - 1))
            mm.then_inc(*L.pe.mark(f"down{x}_{i}"))

        rows_to_columns(0)
        for x in range(E):
            for u, (f, h) in enumerate(self.UNITS):
                lo, hi = self.HALVES[h]
                g = x * self.N + u
                e.wait_ge(*L.act(f"x_in{x}_{h}", 0))
                if g >= 2:
                    e.wait_ge(*L.act(f"silu{g - 2}", 0))
                e.matmul(M.ps[g % 2][:, 0:hi - lo], M.expert_gate[:, x, f * P:(f + 1) * P], self.x_in[x % 2][:, lo:hi], start=True, stop=True)\
                    .then_inc(*L.pe.mark(f"gate{g}"))
                if g >= 2:
                    e.wait_ge(*L.dve(f"mid{(g - 2) // self.N}_{(g - 2) % self.N}", 0))
                e.matmul(M.ps[2 + g % 2][:, 0:hi - lo], M.expert_up[:, x, f * P:(f + 1) * P], self.x_in[x % 2][:, lo:hi], start=True, stop=True)\
                    .then_inc(*L.pe.mark(f"up{g}"))
                if x >= 1 and u >= 1 and u - 1 < PIECES:
                    down(x - 1, u - 1)
                if u == self.N - 2 and x + 1 < E:
                    rows_to_columns(x + 1)
        for i in range(PIECES):
            down(E - 1, i)
        for bb in range(B):
            e.wait_ge(*L.dve(f"combined{bb}", 0))
            for c in range(NC):
                mm = e.transpose(M.ps[bb][:, c * P:(c + 1) * P], self.combined[:, bb * NC + c, :], M.k("ident"))
            mm.then_inc(*L.pe.mark(f"back{bb}"))

    def act(self, e, M, L, b):
        e.wait_ge(*L.dve("gap", 0))
        e.activation(self.e2, self.w1, ACT.Exp).then_inc(*L.act.mark("e2"))

        def x_in(x):
            e.wait_ge(*L.pe(f"x_in{x}", 0))
            if x >= 2:
                e.wait_ge(*L.pe(f"up{(x - 1) * self.N - 1}", 0))
            for h, (lo, hi) in enumerate(self.HALVES):
                e.activation(self.x_in[x % 2][:, lo:hi], M.ps[4 + h][:, 0:hi - lo], ACT.Copy).then_inc(*L.act.mark(f"x_in{x}_{h}"))

        x_in(0)
        for x in range(E):
            for u, (f, h) in enumerate(self.UNITS):
                lo, hi = self.HALVES[h]
                g = x * self.N + u
                e.wait_ge(*L.pe(f"gate{g}", 0))
                if g >= 3:
                    e.wait_ge(*L.dve(f"mid{(g - 3) // self.N}_{(g - 3) % self.N}", 0))
                e.activation(self.silu[g % 3][:, 0:hi - lo], M.ps[g % 2][:, 0:hi - lo], ACT.Silu).then_inc(*L.act.mark(f"silu{g}"))
                if u == self.N - 2 and x + 1 < E:
                    x_in(x + 1)

    def dve(self, e, M, L, b):
        wide = lambda a: a.unsqueeze(2).broadcast_to([P, CHUNKS, E])
        rank = M.k("expert_rank").unsqueeze(1).broadcast_to([P, CHUNKS, E])

        def step(name, ins, wait=True):
            ins.then_inc(*L.dve.mark(name))
            if wait:
                e.wait_ge(*L.dve(name, 0))

        for i in range(2):
            step(f"pad{i}", e.memset(self.sums[i][:, 0:CHUNKS // 2, :], 0.0), False)
        for k, m in ((0, self.m1), (1, self.m2)):
            step(f"max{k}", e.tensor_reduce(m, self.lg, AX, ALU.max))
            step(f"top{k}", e.tensor_tensor(self.eq, self.lg, wide(m), ALU.is_equal))
            step(f"rank{k}", e.tensor_tensor(self.tmp, self.eq, rank, ALU.mult))
            step(f"first{k}", e.tensor_reduce(self.pick, self.tmp, AX, ALU.min))
            step(f"chosen{k + 1}", e.tensor_tensor(self.chosen[:, :, k * E:(k + 1) * E], rank, wide(self.pick), ALU.is_equal))
            if k == 0:
                step("rest", e.scalar_tensor_tensor(self.lg, self.chosen[:, :, 0:E], NEG, self.lg, ALU.mult, ALU.add))
        step("gap", e.tensor_tensor(self.w1, self.m2, self.m1, ALU.subtract), False)
        e.wait_ge(*L.pe("counted", 0))
        half = CHUNKS // 2
        total = M.ps[1][:, 0:CHUNKS * TOP * E].rearrange("p (c k) -> p c k", c=CHUNKS)
        step("total", e.tensor_copy(self.sums[0][:, half:, :], total))
        s, i = 1, 0
        while s < CHUNKS:
            a = self.sums[i]
            step(f"sum{s}", e.tensor_tensor(self.sums[1 - i][:, half:, :], a[:, half:, :], a[:, half - s:half + CHUNKS - s, :], ALU.add))
            s, i = 2 * s, 1 - i
        upto = M.ps[0][:, 0:CHUNKS * TOP * E].rearrange("p (c k) -> p c k", c=CHUNKS)
        step("others", e.tensor_tensor(self.place, self.sums[i][:, half:, :], total, ALU.subtract))
        step("place", e.tensor_tensor(self.place, self.place, upto, ALU.add))
        step("free", e.scalar_tensor_tensor(self.free, self.place, float(CAPACITY), self.chosen, ALU.is_le, ALU.mult), False)
        step("slot_at", e.tensor_tensor(self.place, self.place, M.k("slot_before").unsqueeze(1).broadcast_to([P, CHUNKS, TOP * E]), ALU.add))
        step("slot_of", e.tensor_tensor(self.place, self.place, self.free, ALU.mult))
        for k in range(TOP):
            step(f"row{k}", e.tensor_reduce(self.row[:, k, :], self.place[:, :, k * E:(k + 1) * E], AX, ALU.add), False)
            step(f"valid{k}", e.tensor_reduce(self.valid[:, k, :], self.free[:, :, k * E:(k + 1) * E], AX, ALU.add))
        spare = M.k("spare_slot").rearrange("p (k c) -> p k c", k=TOP)
        step("full", e.tensor_tensor(self.to, self.valid, spare, ALU.mult))
        step("spare", e.tensor_tensor(self.to, spare, self.to, ALU.subtract))
        step("to", e.tensor_tensor(self.to, self.to, self.row, ALU.add))
        step("scatter_i", e.tensor_copy(self.scatter_i, self.to.rearrange("p k c -> p (k c)")), False)
        step("gather_i", e.tensor_copy(self.gather_i, self.row.rearrange("p k c -> p (k c)")), False)
        e.wait_ge(*L.act("e2", 0))
        step("norm_sum", e.tensor_scalar(self.w2, self.e2, 1.0, None, ALU.add))
        step("w1", e.reciprocal(self.w1, self.w2))
        step("w2", e.tensor_tensor(self.w2, self.w1, self.e2, ALU.mult))
        for k, w in ((0, self.w1), (1, self.w2)):
            step(f"weight{k}", e.tensor_tensor(self.weight[:, k, :], self.valid[:, k, :], w, ALU.mult))

        def rows_out(x):
            for h, (lo, hi) in enumerate(self.HALVES):
                e.wait_ge(*L.pe(f"down{x}_{hi // P - 1}", 0))
                if x >= 2:
                    e.wait_ge(*L.counters[f"store{x % 2}"](f"stored{x - 2}", 0))
                e.tensor_copy(self.rows_out[x % 2][:, lo:hi], M.ps[6 + h][:, 0:hi - lo]).then_inc(*L.dve.mark(f"rows_out{x}_{h}"))

        for x in range(E):
            for u, (f, h) in enumerate(self.UNITS):
                lo, hi = self.HALVES[h]
                g = x * self.N + u
                e.wait_ge(*L.act(f"silu{g}", 0))
                e.wait_ge(*L.pe(f"up{g}", 0))
                if x >= 2:
                    e.wait_ge(*L.pe(f"down{x - 2}_{PIECES - 1}", 0))
                e.tensor_tensor(self.mid[x % 2][:, f, lo:hi], self.silu[g % 3][:, 0:hi - lo], M.ps[2 + g % 2][:, 0:hi - lo], ALU.mult)\
                    .then_inc(*L.dve.mark(f"mid{x}_{u}"))
                if u == PIECES + 1 and x >= 1:
                    rows_out(x - 1)
        rows_out(E - 1)

        def residual(bb):
            e.wait_ge(*L.pe(f"back{bb}", 0))
            e.tensor_tensor(M.x[:, bb, :], M.x[:, bb, :], M.ps[bb][:, :], ALU.add).then_inc(*L.dve.mark(f"residual{bb}"))

        for bb in range(B):
            e.wait_ge(*L.counters[f"fetch{bb}"].end())
            for c in range(bb * NC, (bb + 1) * NC):
                e.tensor_scalar(self.combined[:, c, :], self.fetched[:, 0, c, :], self.weight[:, 0, c:c + 1], None, ALU.mult)\
                    .then_inc(*L.dve.mark(f"first_result{c}"))
            for c in range(bb * NC, (bb + 1) * NC):
                e.wait_ge(*L.dve(f"first_result{c}", 0))
                ins = e.scalar_tensor_tensor(self.combined[:, c, :], self.fetched[:, 1, c, :], self.weight[:, 1, c:c + 1],
                                             self.combined[:, c, :], ALU.mult, ALU.add)
            ins.then_inc(*L.dve.mark(f"combined{bb}"))
            if bb:
                residual(bb - 1)
        residual(B - 1)

class Flow(Layer):
    prepares = True
    KEY, QUERY = (0, 1, 5), (2, 3, 7, 6)

    def __init__(self, M):
        t = M.tile
        self.q, self.k, self.v, self.qe, self.ke, self.ca, self.cb, self.da, self.db = (t(i) for i in range(9))
        self.spread = M.big[:, 0:DH * P].rearrange("p (d f) -> p d f", f=P)
        self.product, self.running, self.answer = ([M.wide[:, 3 * i + j, :] for j in range(3)] for i in range(3))
        self.inv_count = M.wide[:, 10, :]
        self.sink, self.src = M.wide[:, 18, :], M.wide[:, 19, :]
        self.cols = M.small[:, 0:128]
        self.sink_cols, self.src_cols, self.comp_cols = (M.small[:, 128 + 64 * i:192 + 64 * i] for i in range(3))
        self.rows = [M.tile(9), M.tile(10)]
        self.eps = 1e-6

    def before(self, e, M, which, sem):
        if which == "dve":
            e.tensor_tensor_scan(M.sq[:, :], M.k("ones"), M.k("ones"), 0.0, ALU.mult, ALU.add).then_inc(sem, 1)
            e.wait_ge(sem, 1)
            e.reciprocal(self.inv_count, M.sq[:, :]).then_inc(sem, 1)
            for d in range(DH):
                e.tensor_scalar(self.spread[:, d, :], M.k("same8"), M.k("feature")[:, d:d + 1], None, ALU.mult).then_inc(sem, 1)
        if which in ("dve", "pe"):
            e.wait_ge(sem, 2 + DH)

    def pe(self, e, M, L, b):
        L.finished(e, b)
        e.wait_ge(*L.dve("norm", b))
        for n, w in enumerate(("f_Wq", "f_Wk", "f_Wv")):
            e.matmul(M.ps[2 + n][:, :], M.w(w), M.h[:, :], start=True, stop=True).then_inc(*L.pe.mark(f"proj{n}"))

        def head_sums(tag, base):
            for n, src in enumerate((self.da, self.db)):
                e.wait_ge(*L.dve(f"{tag}{n}", b))
                for c in range(NC):
                    at = base + 64 * n + H * c
                    mm = e.matmul(M.ps[7][:, at:at + H], src[:, c * P:(c + 1) * P], M.k("head"), start=True, stop=True)
                mm.then_inc(*L.pe.mark(f"{tag}{n}"))

        def turn_back(bank, cols, name):
            for c in range(NC):
                mm = e.transpose(M.ps[bank][:, c * P:(c + 1) * P], cols[:, c * P:(c + 1) * P], M.k("ident"))
            mm.then_inc(*L.pe.mark(name))

        head_sums("flow", 0)
        e.wait_ge(*L.dve("inv_n", b))
        turn_back(5, self.rows[0], "in_back")
        turn_back(6, self.rows[1], "out_back")
        head_sums("cons", 128)
        e.wait_ge(*L.act("src", b))
        e.matmul(M.ps[7][:, 256:256 + H * NC], M.k("upto"), self.src_cols, start=True, stop=False, skip_group_check=True)
        for c in range(NC - 1):
            behind = NC - 1 - c
            mm = e.matmul(M.ps[7][:, 256 + H * (c + 1):256 + H * NC], M.k("ones")[:, 0:P],
                          self.src_cols[:, H * c:H * (c + 1)].unsqueeze(1).broadcast_to([P, behind, H]), start=False, stop=(behind == 1), skip_group_check=True)
        mm.then_inc(*L.pe.mark("cum_src"))
        e.wait_ge(*L.dve("comp", b))
        turn_back(5, self.rows[0], "comp_back")
        e.wait_ge(*L.act("sink", b))
        turn_back(6, self.rows[1], "sink_back")
        e.wait_ge(*L.dve("vs", b))
        def add(d):
            e.wait_ge(*L.dve(f"answer{d}", b))
            e.matmul(M.ps[4][:, :], M.k("ident"), self.answer[d % 3], start=(d == 0), stop=(d == DH - 1)).then_inc(*L.pe.mark(f"added{d}"))

        for d in range(DH):
            if d >= 3:
                e.wait_ge(*L.dve(f"product{d - 3}", b))
            e.matmul(M.ps[self.KEY[d % 3]][:, :], self.spread[:, d, :], self.k[:, :], start=True, stop=True).then_inc(*L.pe.mark(f"key{d}"))
            if d >= 4:
                e.wait_ge(*L.dve(f"answer{d - 4}", b))
            if d == 3:
                e.wait_ge(*L.act("sink_row", b))
            e.matmul(M.ps[self.QUERY[d % 4]][:, :], self.spread[:, d, :], self.q[:, :], start=True, stop=True).then_inc(*L.pe.mark(f"query{d}"))
            if d >= 3:
                add(d - 3)
        for d in range(DH - 3, DH):
            add(d)
        e.wait_ge(*L.dve("alloc", b))
        e.matmul(M.ps[2][:, :], M.w("f_Wo"), self.da[:, :], start=True, stop=True).then_inc(*L.pe.mark("out"))

    def act(self, e, M, L, b):
        L.finished(e, b)
        for n, (dst, bias, fn) in enumerate(((self.q, "f_bq", ACT.Sigmoid), (self.k, "f_bk", ACT.Sigmoid), (self.v, "f_bv", ACT.Identity))):
            e.wait_ge(*L.pe(f"proj{n}", b))
            e.activation(dst[:, :], M.ps[2 + n][:, :], fn, bias=M.w(bias)).then_inc(*L.act.mark(("q", "k", "v")[n]))
        e.wait_ge(*L.dve("src", b))
        e.activation(self.rows[1].rearrange("p (h d) -> p h d", d=DH), self.sink_cols.unsqueeze(2).broadcast_to([P, NC * H, DH]), ACT.Sigmoid)\
            .then_inc(*L.act.mark("sink"))
        e.activation(self.src_cols, self.src_cols, ACT.Exp).then_inc(*L.act.mark("src"))
        e.wait_ge(*L.pe("sink_back", b))
        e.activation(self.sink, M.ps[6][:, :], ACT.Copy).then_inc(*L.act.mark("sink_row"))

    def dve(self, e, M, L, b):
        L.finished(e, b)
        e.tensor_copy(M.h[:, :], M.hs[:, b, :]).then_inc(*L.dve.mark("norm"))
        q, k, v, qe, ke, ca, cb, da, db = (x[:, :] for x in (self.q, self.k, self.v, self.qe, self.ke, self.ca, self.cb, self.da, self.db))
        eps, ones = self.eps, M.k("ones")

        def step(name, ins, wait=True):
            ins.then_inc(*L.dve.mark(name))
            if wait:
                e.wait_ge(*L.dve(name, b))

        e.wait_ge(*L.act("q", b))
        step("qe", e.tensor_scalar(qe, q, eps, None, ALU.add), False)
        step("cum_q", e.tensor_tensor_scan(cb, ones, q, 0.0, ALU.mult, ALU.add), False)
        e.wait_ge(*L.act("k", b))
        step("ke", e.tensor_scalar(ke, k, eps, None, ALU.add), False)
        step("cum_k", e.tensor_tensor_scan(ca, ones, k, 0.0, ALU.mult, ALU.add))
        step("flow0", e.scalar_tensor_tensor(da, ca, eps, qe, ALU.add, ALU.mult), False)
        step("flow1", e.scalar_tensor_tensor(db, cb, eps, ke, ALU.add, ALU.mult), False)
        count = M.k("count_tok").unsqueeze(2).broadcast_to([P, NC, H])
        inv_count = M.k("inv_count_tok").unsqueeze(2).broadcast_to([P, NC, H])
        heads = lambda a: a.rearrange("p (c h) -> p c h", h=H)
        features = lambda a: a.rearrange("p (c h d) -> p c h d", h=H, d=DH)
        spread = lambda a: a.unsqueeze(3).broadcast_to([P, NC, H, DH])
        e.wait_ge(*L.pe("flow0", b))
        e.wait_ge(*L.pe("flow1", b))
        step("inv", e.reciprocal(self.cols, M.ps[7][:, 0:128]))
        for n, name in enumerate(("inv_in_n", "inv_n")):
            half = heads(self.cols[:, 64 * n:64 * (n + 1)])
            step(name, e.tensor_tensor(features(self.rows[n]), spread(half), spread(count), ALU.mult), False)
        e.wait_ge(*L.pe("in_back", b))
        step("q_in_n", e.tensor_tensor(ca, q, M.ps[5][:, :], ALU.mult), False)
        e.wait_ge(*L.pe("out_back", b))
        step("k_out_n", e.tensor_tensor(cb, k, M.ps[6][:, :], ALU.mult))
        step("cum_out", e.tensor_tensor_scan(self.sink, ones, cb, 0.0, ALU.mult, ALU.add), False)
        step("cum_in", e.tensor_tensor_scan(self.src, ones, ca, 0.0, ALU.mult, ALU.add))
        step("cons0", e.scalar_tensor_tensor(da, self.sink, eps, qe, ALU.add, ALU.mult), False)
        step("cons1", e.scalar_tensor_tensor(db, self.src, eps, ke, ALU.add, ALU.mult), False)
        step("qs", e.tensor_tensor(q, ca, self.inv_count, ALU.mult))
        e.wait_ge(*L.pe("cons0", b))
        e.wait_ge(*L.pe("cons1", b))
        step("sink", e.tensor_tensor(heads(self.sink_cols), heads(M.ps[7][:, 128:192]), inv_count, ALU.mult), False)
        step("src_n", e.tensor_tensor(heads(self.src_cols), heads(M.ps[7][:, 192:256]), inv_count, ALU.mult))
        step("src", e.tensor_scalar(self.src_cols, self.src_cols, -1.0, 1.0, ALU.max, ALU.min))
        e.wait_ge(*L.pe("cum_src", b))
        step("inv_src", e.reciprocal(self.comp_cols, M.ps[7][:, 256:320]))
        step("comp_n", e.tensor_tensor(self.comp_cols, self.comp_cols, self.src_cols, ALU.mult))
        step("comp", e.tensor_tensor(features(self.rows[0]), spread(heads(self.comp_cols)), spread(count), ALU.mult), False)
        e.wait_ge(*L.act("v", b))
        e.wait_ge(*L.pe("comp_back", b))
        step("vs", e.tensor_tensor(v, v, M.ps[5][:, :], ALU.mult), False)
        def key(d):
            e.wait_ge(*L.pe(f"key{d}", b))
            step(f"product{d}", e.tensor_tensor(self.product[d % 3], v, M.ps[self.KEY[d % 3]][:, :], ALU.mult), False)

        def run(d):
            e.wait_ge(*L.dve(f"product{d}", b))
            step(f"running{d}", e.tensor_tensor_scan(self.running[d % 3], ones, self.product[d % 3], 0.0, ALU.mult, ALU.add), False)

        def answer(d):
            e.wait_ge(*L.pe(f"query{d}", b))
            e.wait_ge(*L.dve(f"running{d}", b))
            if d >= 3:
                e.wait_ge(*L.pe(f"added{d - 3}", b))
            step(f"answer{d}", e.tensor_tensor(self.answer[d % 3], self.running[d % 3], M.ps[self.QUERY[d % 4]][:, :], ALU.mult), False)

        e.wait_ge(*L.dve("vs", b))
        for i in range(DH + 2):
            if i < DH:
                key(i)
            if i >= 2:
                answer(i - 2)
            if 1 <= i <= DH:
                run(i - 1)
        e.wait_ge(*L.pe(f"added{DH - 1}", b))
        e.wait_ge(*L.act("sink_row", b))
        step("alloc", e.tensor_tensor(da, self.sink, M.ps[4][:, :], ALU.mult), False)
        e.wait_ge(*L.pe("out", b))
        e.scalar_tensor_tensor(M.hs[:, b, :], M.ps[2][:, :], M.w("f_bo"), M.h[:, :], ALU.add, ALU.add).then_inc(*L.dve.mark("with_in"))

class FlowNorm(Norm):
    gain, shift = "f_ln1_g", "f_ln1_b"

    def source(self, M):
        return M.hs

    def shifted(self, e, M, i):
        return e.tensor_scalar(M.hs[:, i, :], M.hs[:, i, :], M.w(self.shift), None, ALU.add)

class FlowFeed(Layer):
    turns = 1

    def __init__(self, M):
        self.mid = [M.wide[:, NF * i:NF * (i + 1), :] for i in range(2)]

    def pe(self, e, M, L, b):
        def down(i):
            if i >= 2:
                e.wait_ge(*L.dve(f"with_ffn{i - 2}", 0))
            for f in range(NF):
                e.wait_ge(*L.act(f"gelu{i}_{f}", 0))
                mm = e.matmul(M.ps[4 + i % 2][:, :], M.w("f_W2")[:, f * P:(f + 1) * P], self.mid[i % 2][:, f, :], start=(f == 0), stop=(f == NF - 1))
            mm.then_inc(*L.pe.mark(f"down{i}"))

        for i in range(B):
            for f in range(NF):
                if i >= 1:
                    e.wait_ge(*L.act(f"gelu{i - 1}_{f}", 0))
                e.matmul(M.ps[f][:, :], M.w("f_W1")[:, f * P:(f + 1) * P], M.hs[:, i, :], start=True, stop=True).then_inc(*L.pe.mark(f"up{i}_{f}"))
            if i >= 1:
                down(i - 1)
        down(B - 1)

    def act(self, e, M, L, b):
        for i in range(B):
            if i >= 2:
                e.wait_ge(*L.pe(f"down{i - 2}", 0))
            for f in range(NF):
                e.wait_ge(*L.pe(f"up{i}_{f}", 0))
                e.activation(self.mid[i % 2][:, f, :], M.ps[f][:, :], ACT.Gelu, bias=M.w("f_b1")[:, f:f + 1]).then_inc(*L.act.mark(f"gelu{i}_{f}"))

    def dve(self, e, M, L, b):
        for i in range(B):
            e.wait_ge(*L.pe(f"down{i}", 0))
            e.scalar_tensor_tensor(M.hs[:, i, :], M.ps[4 + i % 2][:, :], M.w("f_b2"), M.hs[:, i, :], ALU.add, ALU.add)\
                .then_inc(*L.dve.mark(f"with_ffn{i}"))

class FlowOut(FlowNorm):
    gain, shift = "f_ln2_g", "f_ln2_b"

    def shifted(self, e, M, i):
        return e.scalar_tensor_tensor(M.x[:, i, :], M.hs[:, i, :], M.w(self.shift), M.x[:, i, :], ALU.add, ALU.add)

class TimeMix(Layer):

    def __init__(self, M):
        self.xx, self.xk, self.xv, self.xr, self.ek, self.eku, self.sr, self.v = (M.tile(i) for i in range(8))
        self.sa, self.sb, self.t, self.den, self.num = (M.wide[:, i, :] for i in range(5))
        self.one_less, self.cols = M.small[:, 0:3], M.small[:, 4:8]
        self.decay = M.tile(8)

    def pe(self, e, M, L, b):
        L.finished(e, b)
        for n, (w, s) in enumerate((("r_Wk", self.xk), ("r_Wv", self.xv), ("r_Wr", self.xr))):
            e.wait_ge(*L.dve(f"mixed{n}", b))
            e.matmul(M.ps[2 + n][:, :], M.w(w), s[:, :], start=True, stop=True).then_inc(*L.pe.mark(f"proj{n}"))
        e.wait_ge(*L.dve("gated", b))
        e.matmul(M.ps[5][:, :], M.w("r_Wo"), self.num, start=True, stop=True).then_inc(*L.pe.mark("out"))

    def act(self, e, M, L, b):
        L.finished(e, b)
        e.activation(self.cols[:, 0:1], M.w("r_spatial_decay"), ACT.Exp, scale=1.0 / T).then_inc(*L.act.mark("decay_col"))
        e.activation(self.cols[:, 1:2], M.w("r_spatial_first"), ACT.Copy, scale=1.0 / T).then_inc(*L.act.mark("first_col"))
        e.wait_ge(*L.act("first_col", b))
        e.wait_ge(*L.pe("proj0", b))
        e.activation(self.ek[:, :], M.ps[2][:, :], ACT.Exp).then_inc(*L.act.mark("ek"))
        e.activation(self.eku[:, :], M.ps[2][:, :], ACT.Exp, bias=self.cols[:, 1:2]).then_inc(*L.act.mark("eku"))
        e.wait_ge(*L.pe("proj2", b))
        e.activation(self.sr[:, :], M.ps[4][:, :], ACT.Sigmoid).then_inc(*L.act.mark("sr"))

    def dve(self, e, M, L, b):
        L.finished(e, b)
        e.tensor_copy(M.h[:, :], M.hs[:, b, :]).then_inc(*L.dve.mark("norm"))
        Q = C // 4
        e.wait_ge(*L.dve("norm", b))
        e.tensor_copy(self.xx[0:Q, 1:T], M.h[0:Q, 0:T - 1]).then_inc(*L.dve.mark("shift_a"))
        e.memset(self.xx[0:Q, 0:1], 0.0).then_inc(*L.dve.mark("shift_b"))
        e.tensor_copy(self.xx[Q:2 * Q, 0:T - 1], M.h[Q:2 * Q, 1:T]).then_inc(*L.dve.mark("shift_c"))
        e.memset(self.xx[Q:2 * Q, T - 1:T], 0.0).then_inc(*L.dve.mark("shift_d"))
        e.tensor_copy(self.xx[2 * Q:C, :], M.h[2 * Q:C, :]).then_inc(*L.dve.mark("shift_e"))
        mixes = [M.w(n) for n in ("r_mix_k", "r_mix_v", "r_mix_r")]
        for n, m in enumerate(mixes):
            e.tensor_scalar(self.one_less[:, n:n + 1], m, -1.0, 1.0, ALU.mult, ALU.add).then_inc(*L.dve.mark(f"less{n}"))
        e.wait_ge(*L.dve("less2", b))
        for n, (m, s) in enumerate(zip(mixes, (self.xk, self.xv, self.xr))):
            e.tensor_scalar(self.t, self.xx[:, :], self.one_less[:, n:n + 1], None, ALU.mult).then_inc(*L.dve.mark(f"other{n}"))
            e.wait_ge(*L.dve(f"other{n}", b))
            e.scalar_tensor_tensor(s[:, :], M.h[:, :], m, self.t, ALU.mult, ALU.add).then_inc(*L.dve.mark(f"mixed{n}"))
            e.wait_ge(*L.dve(f"mixed{n}", b))
        e.wait_ge(*L.act("decay_col", b))
        e.tensor_scalar(self.decay[:, :], M.k("ones"), self.cols[:, 0:1], None, ALU.mult).then_inc(*L.dve.mark("decay"))
        e.wait_ge(*L.dve("decay", b))
        e.wait_ge(*L.act("ek", b))
        e.wait_ge(*L.pe("proj1", b))
        e.tensor_tensor(self.t, self.ek[:, :], M.ps[3][:, :], ALU.mult).then_inc(*L.dve.mark("ekv"))
        e.wait_ge(*L.dve("ekv", b))
        e.tensor_tensor_scan(self.sa, self.decay[:, :], self.t, 0.0, ALU.mult, ALU.add).then_inc(*L.dve.mark("scan_a"))
        e.tensor_tensor_scan(self.sb, self.decay[:, :], self.ek[:, :], 0.0, ALU.mult, ALU.add).then_inc(*L.dve.mark("scan_b"))
        e.wait_ge(*L.act("eku", b))
        e.wait_ge(*L.dve("scan_b", b))
        e.tensor_tensor(self.num, self.eku[:, :], M.ps[3][:, :], ALU.mult).then_inc(*L.dve.mark("num0"))
        e.tensor_copy(self.den, self.eku[:, :]).then_inc(*L.dve.mark("den0"))
        e.wait_ge(*L.dve("den0", b))
        e.tensor_tensor(self.num[:, 1:T], self.num[:, 1:T], self.sa[:, 0:T - 1], ALU.add).then_inc(*L.dve.mark("num"))
        e.tensor_tensor(self.den[:, 1:T], self.den[:, 1:T], self.sb[:, 0:T - 1], ALU.add).then_inc(*L.dve.mark("den"))
        e.wait_ge(*L.dve("den", b))
        e.reciprocal(self.t, self.den).then_inc(*L.dve.mark("inv"))
        e.wait_ge(*L.dve("inv", b))
        e.tensor_tensor(self.num, self.num, self.t, ALU.mult).then_inc(*L.dve.mark("wkv"))
        e.wait_ge(*L.dve("wkv", b))
        e.wait_ge(*L.act("sr", b))
        e.tensor_tensor(self.num, self.num, self.sr[:, :], ALU.mult).then_inc(*L.dve.mark("gated"))
        e.wait_ge(*L.pe("out", b))
        e.tensor_tensor(M.x[:, b, :], M.x[:, b, :], M.ps[5][:, :], ALU.add).then_inc(*L.dve.mark("residual"))

class DepthPick(Layer):

    def __init__(self, M):
        t, s = M.tile, M.small
        self.h_tok = t(0)
        self.onehot = t(1)[:, 0:NC * SLOTS].rearrange("p (c s) -> p c s", s=SLOTS)
        self.row, self.rest = t(4), t(5)
        self.unread = [t(2), t(3), M.sq[:, :], M.sd[:, :], M.xc[:, :], M.h2[:, :]] + [M.wide[:, 5 + i, :] for i in range(6)]
        self.masks = M.wide[:, 0:4, :]
        self.seen = M.wide[:, 4, 0:NC * SLOTS].rearrange("p (c s) -> p c s", s=SLOTS)
        self.weight, self.rank, self.tie, self.reach, self.kept = (s[:, 4 * i:4 * i + 4] for i in range(5))
        self.posf = s[:, 32:36]
        n = B * SLOTS
        self.xs_all, self.ws_all, self.angle_all, self.mask_all = t(6)[:, 0:n], t(6)[:, n:2 * n], t(7)[:, 0:n], t(7)[0:SLOTS, n:2 * n]
        self.slot_rows = M.wide[0:SLOTS, 16:20, :]

    def slots(self, a, b):
        return a.rearrange("p (b s) -> p b s", b=B)[:, b, :]

    def pe(self, e, M, L, b):
        S = SLOTS
        L.finished(e, b)
        e.wait_ge(*L.dve("norm", b))
        ident = M.k("ident")
        for c in range(NC):
            mm = e.matmul(M.ps[2][:, c:c + 1], M.h[:, c * P:(c + 1) * P], M.w("m_router"), start=True, stop=True)
        mm.then_inc(*L.pe.mark("router"))
        for c in range(NC):
            mm = e.transpose(M.ps[3][:, c * P:(c + 1) * P], M.h[:, c * P:(c + 1) * P], ident)
        mm.then_inc(*L.pe.mark("h_tok"))
        e.wait_ge(*L.dve("weight", b))
        for c in range(NC):
            mm = e.transpose(M.ps[4][:, c * P:(c + 1) * P], self.weight[:, c:c + 1].broadcast_to([P, P]), ident)
        mm.then_inc(*L.pe.mark("weight_row"))
        e.wait_ge(*L.dve("onehot3", b))
        e.wait_ge(*L.dve("posf", b))
        e.wait_ge(*L.act("h_tok", b))
        for i, lhs in enumerate((lambda c: self.h_tok[:, c * P:(c + 1) * P], lambda c: self.posf[:, c:c + 1].broadcast_to([P, P]),
                                 lambda c: self.weight[:, c:c + 1].broadcast_to([P, P]))):
            for c in range(NC):
                mm = e.matmul(M.ps[5][:, i * S:(i + 1) * S], lhs(c), self.onehot[:, c, :], start=(c == 0), stop=(c == NC - 1))
        mm.then_inc(*L.pe.mark("gathered"))
        e.wait_ge(*L.dve("kept", b))
        for c in range(NC):
            e.transpose(M.ps[7][:, c * P:(c + 1) * P], self.kept[:, c:c + 1].broadcast_to([P, P]), ident)
        for c in range(NC):
            mm = e.transpose(M.ps[6][0:S, c * P:(c + 1) * P], self.onehot[:, c, :], ident)
        mm.then_inc(*L.pe.mark("slot_rows"))
        e.wait_ge(*L.dma("mask", b))
        for d in range(NC):
            for c in range(NC):
                mm = e.matmul(M.ps[2][:, d * S:(d + 1) * S], self.masks[:, c, d * P:(d + 1) * P], self.onehot[:, c, :],
                              start=(c == 0), stop=(c == NC - 1))
        mm.then_inc(*L.pe.mark("mask_rows"))
        e.wait_ge(*L.act("mask_rows", b))
        for d in range(NC):
            mm = e.matmul(M.ps[3][0:S, 0:S], self.seen[:, d, :], self.onehot[:, d, :], start=(d == 0), stop=(d == NC - 1))
        mm.then_inc(*L.pe.mark("mask"))

    def act(self, e, M, L, b):
        S = SLOTS
        L.finished(e, b)
        e.dma_start(self.masks, M.D["mask"][:, bass.ts(b, 1), :, :].rearrange("p b c t -> p (b c) t")).then_inc(*L.dma.mark("mask"))
        e.wait_ge(*L.pe("h_tok", b))
        e.activation(self.h_tok, M.ps[3][:, :], ACT.Copy).then_inc(*L.act.mark("h_tok"))
        e.wait_ge(*L.pe("weight_row", b))
        e.activation(self.row, M.ps[4][:, :], ACT.Copy).then_inc(*L.act.mark("weight_row"))
        e.wait_ge(*L.pe("slot_rows", b))
        e.activation(self.slot_rows[:, b, :], M.ps[6][0:S, :], ACT.Copy).then_inc(*L.act.mark("slot_rows"))
        e.wait_ge(*L.pe("mask_rows", b))
        e.activation(self.seen.rearrange("p c s -> p (c s)"), M.ps[2][:, 0:NC * S], ACT.Copy).then_inc(*L.act.mark("mask_rows"))

    def dve(self, e, M, L, b):
        S = SLOTS
        L.finished(e, b)

        def step(name, ins, wait=True):
            ins.then_inc(*L.dve.mark(name))
            if wait:
                e.wait_ge(*L.dve(name, b))

        e.tensor_copy(M.h[:, :], M.hs[:, b, :]).then_inc(*L.dve.mark("norm"))
        step("posf", e.tensor_copy(self.posf, M.pos[:, bass.ts(b, NC)]), False)
        e.wait_ge(*L.pe("router", b))
        step("weight", e.tensor_scalar(self.weight, M.ps[2][:, 0:NC], M.w("m_router_b"), None, ALU.add))
        e.wait_ge(*L.act("weight_row", b))

        def compare(kind, c, op, other, count):
            step(f"{kind}{c}", e.scalar_tensor_tensor(self.unread[("more", "tie", "reach").index(kind) * NC + c], self.row, self.weight[:, c:c + 1], other,
                                                      op, ALU.mult, accum_out=count[:, c:c + 1]), False)

        for c in range(NC):
            compare("more", c, ALU.is_gt, M.k("ones"), self.rank)
            compare("tie", c, ALU.is_equal, M.k("before")[:, (NC - 1 - c) * P:(NC - 1 - c) * P + T], self.tie)
        e.wait_ge(*L.dve(f"tie{NC - 1}", b))
        step("rank", e.tensor_tensor(self.rank, self.rank, self.tie, ALU.add))
        for c in range(NC):
            step(f"onehot{c}", e.tensor_scalar(self.onehot[:, c, :], M.k("slot"), self.rank[:, c:c + 1], None, ALU.is_equal), False)
        for c in range(NC):
            compare("reach", c, ALU.is_ge, M.k("ones"), self.reach)
        e.wait_ge(*L.dve(f"reach{NC - 1}", b))
        step("kept", e.tensor_scalar(self.kept, self.reach, SLOTS - 0.5, None, ALU.is_gt), False)
        e.wait_ge(*L.pe("gathered", b))
        step("xs", e.tensor_copy(self.slots(self.xs_all, b), M.ps[5][:, 0:S]), False)
        step("ws", e.tensor_copy(self.slots(self.ws_all, b), M.ps[5][:, 2 * S:3 * S]), False)
        step("angle", e.tensor_scalar(self.slots(self.angle_all, b), M.ps[5][:, S:2 * S], M.k("mod_inv"), None, ALU.mult), False)
        e.wait_ge(*L.pe("slot_rows", b))
        step("keep", e.tensor_tensor(self.rest, M.h[:, :], M.ps[7][:, :], ALU.mult))
        step("rest", e.tensor_tensor(M.x[:, b, :], self.rest, M.x[:, b, :], ALU.add), False)
        e.wait_ge(*L.pe("mask", b))
        step("mask", e.tensor_tensor(self.slots(self.mask_all, b), M.ps[3][0:S, 0:S], M.k("last_slot")[0:S, :], ALU.add), False)

class DepthBlock(DepthPick):
    turns = 1
    N = B * SLOTS
    PAIRS = B // 2

    def __init__(self, M):
        super().__init__(M)
        t, n = M.tile, self.N
        self.prob = M.big[:, 0:2 * 1024].rearrange("p (r h s) -> p r h s", r=2, s=SLOTS)
        self.prob_t = M.big[:, 2048:4096].rearrange("p (r m q) -> p r m q", r=2, q=P)
        self.key_head = M.wide[:, 0:8, :].rearrange("p (b r) (h s) -> p b (r h) s", b=B, s=SLOTS)
        self.v_pair = M.wide[:, 8:16, :].rearrange("p (b r) (m f) -> p b (r m) f", b=B, f=C)
        self.q, self.kk = t(8)[:, 0:n], t(8)[:, n:2 * n]
        self.cos, self.sin = t(9)[:, 0:n], t(9)[:, n:2 * n]
        self.hn = t(10).rearrange("p (b w s) -> p b w s", b=B, w=2)
        self.x1, self.y = t(11)[:, 0:n], t(11)[:, n:2 * n]
        self.sq, self.sd = t(0)[:, 0:n], t(0)[:, n:2 * n]
        self.a, self.b2 = t(1)[:, 0:n], t(1)[:, n:2 * n]
        self.c, self.d = t(2)[:, 0:n], t(2)[:, n:2 * n]
        self.mid = M.tiles[:, 3:5, :].rearrange("p r t -> p (r t)")
        self.rsd, self.o = t(5)[:, 0:n], t(5)[:, n:2 * n]
        self.mask2 = M.xc[:, 0:self.PAIRS * SLOTS].rearrange("p (r s) -> p r s", s=SLOTS)
        self.v = M.sq
        self.proc = M.h[0:SLOTS, :].rearrange("p (b f) -> p b f", f=C)
        self.mx, self.den = M.small[:, 64:96].rearrange("p (r h) -> p r h", h=H), M.small[:, 96:128].rearrange("p (r h) -> p r h", h=H)
        self.angles = M.h2[:, 0:n], M.h2[:, n:2 * n]

    def pe(self, e, M, L, b):
        S, N = SLOTS, self.N
        ident = M.k("ident")
        e.wait_ge(*L.act("sq1", 0))
        e.matmul(M.ps[4][:, 0:N], M.k("mean"), self.sq, start=True, stop=True).then_inc(*L.pe.mark("ms1"))
        e.wait_ge(*L.dve("hn_twice", 0))
        hn = self.hn[:, :, 0, :]
        for i, w in enumerate(("m_wq", "m_wqr", "m_wk", "m_wkr")):
            mm = e.matmul(M.ps[2 + i // 2][:, i % 2 * N:(i % 2 + 1) * N], M.w(w), hn, start=True, stop=True)
        mm.then_inc(*L.pe.mark("qk"))
        for bb in range(B):
            mm = e.matmul(M.ps[6][:, bb * C:(bb + 1) * C], self.hn[:, bb, :, :].rearrange("p w s -> p (w s)"), M.w("m_wv"), start=True, stop=True)
        mm.then_inc(*L.pe.mark("v"))
        for r in range(self.PAIRS):
            banks = (0, 1) if r == 0 else (4, 5)
            e.wait_ge(*L.dve(f"key_head{2 * r + 1}", 0))
            for turn in range(2):
                for w in range(2):
                    bb, i = 2 * r + w, (turn + w) % 2
                    mm = e.matmul(M.ps[banks[i]][w * S:(w + 1) * S, :], self.q[:, bb * S:(bb + 1) * S], self.key_head[:, bb, 8 * i:8 * i + 8, :],
                                  start=True, stop=True, tile_position=(0, w * S))
                mm.then_inc(*L.pe.mark(f"scores{r}_{turn}"))
                e.wait_ge(*L.pe(f"scores{r}_{turn}", 0))
        for r in range(self.PAIRS):
            e.wait_ge(*L.dve(f"prob{r}", 0))
            for m in range(H // 2):
                mm = e.transpose(M.ps[(2, 0)[r] + m // 4][:, m % 4 * P:(m % 4 + 1) * P], self.prob[:, r, 2 * m:2 * m + 2, :].rearrange("p h s -> p (h s)"), ident)
                if m % 4 == 3:
                    mm.then_inc(*L.pe.mark(f"prob_t{r}_{m // 4}"))
        for r in range(self.PAIRS):
            for w in range(2):
                bb = 2 * r + w
                e.wait_ge(*L.act(f"prob_t{r}_1", 0))
                e.wait_ge(*L.pool(f"v_pair{bb}", 0))
                for m in range(H // 2):
                    mm = e.matmul(M.ps[7][:, bb * S:(bb + 1) * S], self.v_pair[:, bb, m, :], self.prob_t[:, r, m, w * S:(w + 1) * S],
                                  start=(m == 0), stop=(m == H // 2 - 1))
        mm.then_inc(*L.pe.mark("attended"))
        e.wait_ge(*L.act("o", 0))
        e.matmul(M.ps[4][:, 0:N], M.w("m_wo"), self.o, start=True, stop=True).then_inc(*L.pe.mark("out"))
        e.wait_ge(*L.act("sq2", 0))
        e.matmul(M.ps[5][:, 0:N], M.k("mean"), self.sq, start=True, stop=True).then_inc(*L.pe.mark("ms2"))
        e.wait_ge(*L.dve("h2", 0))
        for f in range(NF):
            mm = e.matmul(M.ps[2 + f // 2][:, f % 2 * N:(f % 2 + 1) * N], M.w("m_w1")[:, f * P:(f + 1) * P], self.hn[:, :, 0, :], start=True, stop=True)
            if f % 2:
                mm.then_inc(*L.pe.mark(f"up{f // 2}"))
        for f in range(NF):
            if f % 2 == 0:
                e.wait_ge(*L.act(f"gelu{f // 2}", 0))
            mm = e.matmul(M.ps[7][:, 0:N], M.w("m_w2")[:, f * P:(f + 1) * P], self.mid[:, f * N:(f + 1) * N], start=(f == 0), stop=(f == NF - 1))
        mm.then_inc(*L.pe.mark("down"))
        e.wait_ge(*L.dve("proc", 0))
        for bb in range(B):
            mm = e.matmul(M.ps[6][0:S, bb * C:(bb + 1) * C], self.y[:, bb * S:(bb + 1) * S], ident, start=True, stop=True)
        mm.then_inc(*L.pe.mark("proc_tok"))
        e.wait_ge(*L.act("proc_tok", 0))
        for bb in range(B):
            e.matmul(M.ps[bb][:, :], self.proc[0:S - 1, bb, :], self.slot_rows[0:S - 1, bb, :], start=True, stop=True)\
                .then_inc(*L.pe.mark(f"scattered{bb}"))

    def pool(self, e, M, L, b):
        e.wait_ge(*L.act("v", 0))
        for bb in range(B):
            of_pair = M.k("head_of_pair").rearrange("p (m h) -> p m h", h=H)
            e.tensor_tensor(self.v_pair[:, bb, :, :].rearrange("p m (h d) -> p m h d", d=DH), of_pair.unsqueeze(3).broadcast_to([P, H // 2, H, DH]),
                            self.v[:, bb * C:(bb + 1) * C].rearrange("p (h d) -> p h d", d=DH).unsqueeze(1).broadcast_to([P, H // 2, H, DH]), ALU.mult).then_inc(*L.pool.mark(f"v_pair{bb}"))

    def act(self, e, M, L, b):
        S, N = SLOTS, self.N
        e.activation(self.sq, self.xs_all, ACT.Square).then_inc(*L.act.mark("sq1"))
        e.wait_ge(*L.pe("ms1", 0))
        e.activation(self.sd, M.ps[4][:, 0:N], ACT.Sqrt, bias=M.k("eps6")).then_inc(*L.act.mark("sd1"))
        for bb in range(B):
            e.activation(self.mask2[bb % 2 * S:(bb % 2 + 1) * S, bb // 2, :], self.slots(self.mask_all, bb), ACT.Copy).then_inc(*L.act.mark(f"mask{bb}"))
        e.wait_ge(*L.dve("reduced1", 0))
        e.activation(self.sin, self.angles[1], ACT.Sin).then_inc(*L.act.mark("sin"))
        e.activation(self.cos, self.angles[0], ACT.Sin).then_inc(*L.act.mark("cos"))
        e.wait_ge(*L.pe("v", 0))
        e.activation(self.v[:, :], M.ps[6][:, :], ACT.Copy).then_inc(*L.act.mark("v"))
        for r in range(self.PAIRS):
            e.wait_ge(*L.dve(f"centred{r}", 0))
            p = self.prob[:, r, :, :].rearrange("p h s -> p (h s)")
            e.activation(p, p, ACT.Exp).then_inc(*L.act.mark(f"exp{r}"))
        for r in range(self.PAIRS):
            for i in range(2):
                e.wait_ge(*L.pe(f"prob_t{r}_{i}", 0))
                e.activation(self.prob_t[:, r, 4 * i:4 * i + 4, :].rearrange("p m q -> p (m q)"), M.ps[(2, 0)[r] + i][:, :], ACT.Copy)\
                    .then_inc(*L.act.mark(f"prob_t{r}_{i}"))
        e.wait_ge(*L.pe("attended", 0))
        e.activation(self.o, M.ps[7][:, 0:N], ACT.Copy).then_inc(*L.act.mark("o"))
        e.wait_ge(*L.dve("x1", 0))
        e.activation(self.sq, self.x1, ACT.Square).then_inc(*L.act.mark("sq2"))
        e.wait_ge(*L.pe("ms2", 0))
        e.activation(self.sd, M.ps[5][:, 0:N], ACT.Sqrt, bias=M.k("eps6")).then_inc(*L.act.mark("sd2"))
        for i in range(2):
            e.wait_ge(*L.pe(f"up{i}", 0))
            e.activation(self.mid[:, 2 * i * N:2 * (i + 1) * N], M.ps[2 + i][:, :], ACT.Gelu_apprx_tanh).then_inc(*L.act.mark(f"gelu{i}"))
        e.wait_ge(*L.pe("proc_tok", 0))
        e.activation(self.proc.rearrange("p b f -> p (b f)"), M.ps[6][0:S, :], ACT.Copy).then_inc(*L.act.mark("proc_tok"))

    def dve(self, e, M, L, b):
        S, N = SLOTS, self.N

        def step(name, ins, wait=True):
            ins.then_inc(*L.dve.mark(name))
            if wait:
                e.wait_ge(*L.dve(name, 0))

        cases = ((self.angles[0], self.a, 0.25), (self.angles[1], self.b2, 0.0))

        def both(name, make):
            for i, (dst, tmp, quarter) in enumerate(cases):
                step(f"{name}{i}", make(dst, tmp, quarter), False)
            e.wait_ge(*L.dve(f"{name}1", 0))

        both("turns", lambda dst, tmp, quarter: e.tensor_scalar(tmp, self.angle_all, 1.0 / (2 * np.pi), quarter, ALU.mult, ALU.add))
        both("round_up", lambda dst, tmp, quarter: e.tensor_scalar(tmp, tmp, 12582912.0, None, ALU.add))
        both("round", lambda dst, tmp, quarter: e.tensor_scalar(tmp, tmp, 12582912.0, None, ALU.subtract))
        for j, part in enumerate(TWO_PI):
            both(f"part{j}_", lambda dst, tmp, quarter: e.scalar_tensor_tensor(dst, tmp, -part, dst if j else self.angle_all, ALU.mult, ALU.add))
        step("quarter", e.tensor_scalar(self.angles[0], self.angles[0], float(np.pi / 2), None, ALU.add))
        both("reduced", lambda dst, tmp, quarter: e.tensor_scalar(dst, dst, PI_BELOW, -PI_BELOW, ALU.min, ALU.max))
        e.wait_ge(*L.act("sd1", 0))
        step("rms1", e.reciprocal(self.rsd, self.sd))
        per_batch = lambda a: a.rearrange("p (b s) -> p b s", b=B)
        for w in range(2):
            step(("hn", "hn_twice")[w], e.scalar_tensor_tensor(self.hn[:, :, w, :], per_batch(self.xs_all), M.w("m_ln1"), per_batch(self.rsd), ALU.mult, ALU.mult), False)
        e.wait_ge(*L.act("cos", 0))
        step("signed", e.tensor_scalar(self.sin, self.sin, M.k("mod_sign"), None, ALU.mult))
        e.wait_ge(*L.pe("qk", 0))
        for i, (x, y) in enumerate(((self.a, self.b2), (self.c, self.d))):
            step(f"rope_a{i}", e.tensor_tensor(x, M.ps[2 + i][:, 0:N], self.cos, ALU.mult), False)
            step(f"rope_b{i}", e.tensor_tensor(y, M.ps[2 + i][:, N:2 * N], self.sin, ALU.mult), False)
        for i, (x, y, dst) in enumerate(((self.a, self.b2, self.q), (self.c, self.d, self.kk))):
            e.wait_ge(*L.dve("rope_b1", 0))
            step(f"rope{i}", e.tensor_tensor(dst, x, y, ALU.add), False)
        e.wait_ge(*L.dve("rope1", 0))
        for bb in range(B):
            step(f"key_head{bb}", e.tensor_tensor(self.key_head[:, bb, :, :], self.kk[:, bb * S:(bb + 1) * S].unsqueeze(1).broadcast_to([P, H, S]),
                                                  M.k("head").unsqueeze(2).broadcast_to([P, H, S]), ALU.mult), False)
        e.wait_ge(*L.act(f"mask{B - 1}", 0))
        wide = lambda a: a.unsqueeze(2).broadcast_to([P, H, S])
        for r in range(self.PAIRS):
            banks = (0, 1) if r == 0 else (4, 5)
            e.wait_ge(*L.pe(f"scores{r}_1", 0))
            for i in range(2):
                step(f"masked{r}_{i}", e.scalar_tensor_tensor(self.prob[:, r, 8 * i:8 * i + 8, :], M.ps[banks[i]][:, :].rearrange("p (h s) -> p h s", s=S),
                                                              float(1.0 / np.sqrt(DH)), self.mask2[:, r:r + 1, :].broadcast_to([P, 8, S]), ALU.mult, ALU.add), i == 1)
            step(f"max{r}", e.tensor_reduce(self.mx[:, r, :], self.prob[:, r, :, :], AX, ALU.max))
            step(f"centred{r}", e.tensor_tensor(self.prob[:, r, :, :], self.prob[:, r, :, :], wide(self.mx[:, r, :]), ALU.subtract), False)
        for r in range(self.PAIRS):
            e.wait_ge(*L.act(f"exp{r}", 0))
            step(f"sum{r}", e.tensor_reduce(self.den[:, r, :], self.prob[:, r, :, :], AX, ALU.add))
            step(f"inv_sum{r}", e.reciprocal(self.den[:, r, :], self.den[:, r, :]))
            step(f"prob{r}", e.tensor_tensor(self.prob[:, r, :, :], self.prob[:, r, :, :], wide(self.den[:, r, :]), ALU.mult), False)
        e.wait_ge(*L.pe("out", 0))
        step("x1", e.tensor_tensor(self.x1, self.xs_all, M.ps[4][:, 0:N], ALU.add))
        e.wait_ge(*L.act("sd2", 0))
        step("rms2", e.reciprocal(self.rsd, self.sd))
        step("h2", e.scalar_tensor_tensor(self.hn[:, :, 0, :], per_batch(self.x1), M.w("m_ln2"), per_batch(self.rsd), ALU.mult, ALU.mult), False)
        e.wait_ge(*L.pe("down", 0))
        step("x2", e.tensor_tensor(self.y, self.x1, M.ps[7][:, 0:N], ALU.add))
        step("proc", e.tensor_tensor(self.y, self.y, self.ws_all, ALU.mult), False)
        for bb in range(B):
            e.wait_ge(*L.pe(f"scattered{bb}", 0))
            step(f"residual{bb}", e.tensor_tensor(M.x[:, bb, :], M.x[:, bb, :], M.ps[bb][:, :], ALU.add), False)

class TokenAttention(Layer):
    prepares = True
    SCALE = 1.0 / 8.0
    RING = 4
    TURNED = (4, 5, 7)
    MIX, TURN = 2, 3

    def __init__(self, M):
        t, w, big, s = M.tile, M.wide, M.big, M.small
        self.q = [t(i) for i in range(4)]
        self.mix = M.tiles[:, 4:8, :]
        self.k, self.v_even, self.v_odd = t(8), t(9), t(10)
        tiles = [t(11), w[:, 16, :], w[:, 17, :], M.xc[:, :], M.h2[:, :], M.sd[:, :], M.sq[:, :], M.h[:, :]]
        self.prob = [tiles[2 * i:2 * i + 2] for i in range(4)]
        self.rms_wide = M.wide[:, 0:5, :].rearrange("p a t -> p (a t)")
        self.v_block, self.comp_t = w[:, 18, :], w[:, 19, :]
        self.prob_t = [w[:, 8 * i:8 * i + 8, :].rearrange("p a t -> p (a t)").rearrange("p (j o m q) -> p j o m q", j=4, o=2, m=4) for i in range(2)]
        self.band = [big[:, 520 * i:520 * i + 514].rearrange("p (o k) -> p o k", o=2) for i in range(4)]
        self.rms = M.small[:, 240:280]
        self.comp = big[:, 2560:3104].rearrange("p (s n) -> p s n", n=17)
        self.comp_p = big[:, 3104:3616]
        self.g = big[:, 3616:3712].rearrange("p (s n) -> p s n", n=3)
        self.t = [big[:, 5 * T:6 * T], big[:, 6 * T:7 * T]]
        self.t2, self.v_twice = big[:, 7 * T:8 * T], big[:, 8 * T:9 * T]
        self.kcw, self.k_sum = s[:, 280:344], s[:, 344:360]
        self.sink = s[:, 32:40]
        self.cm, self.cd, self.gs = s[:, 64:96], s[:, 96:128], s[:, 128:160]
        self.stat = [s[:, 160 + 16 * i:176 + 16 * i] for i in range(4)]

    def before(self, e, M, which, sem):
        if which == "pool":
            e.memset(self.v_even, 0.0).then_inc(sem, 1)
            e.memset(self.v_odd, 0.0).then_inc(sem, 1)
            e.memset(self.kcw, 0.0).then_inc(sem, 1)
        if which in ("pe", "act", "dve"):
            e.wait_ge(sem, 3)

    STEPS = [(c, m) for c in reversed(range(NC)) for m in range(A_H // 2)]
    FIRST = NC - 1

    def pe(self, e, M, L, b):
        L.finished(e, b)
        e.wait_ge(*L.dve("norm", b))
        e.matmul(M.ps[6][0:A_QC, :], M.w("a_w_qc"), M.h[:, :], start=True, stop=True).then_inc(*L.pe.mark("qc"))
        for c in range(NC):
            mm = e.matmul(M.ps[7][:, c * P:(c + 1) * P], M.h[:, c * P:(c + 1) * P], M.w("a_w_v"), start=True, stop=True)
        mm.then_inc(*L.pe.mark("v"))
        for u in range(5):
            if u == 1:
                e.wait_ge(*L.act("qc", b))
            if u >= 2:
                e.wait_ge(*L.dve(f"roped{u - 2}", b))
            for n, (wk, wq) in enumerate((("a_w_k", "a_w_q"), ("a_w_kr", "a_w_qr"))):
                if u == 0:
                    mm = e.matmul(M.ps[n][:, :], M.w(wk), M.h[:, :], start=True, stop=True)
                else:
                    mm = e.matmul(M.ps[2 * (u % 2) + n][:, :], M.w(wq, A_QC)[:, (u - 1) * P:u * P], self.qc_sb(M), start=True, stop=True)
            mm.then_inc(*L.pe.mark(f"raw{u}"))
            if u >= 1:
                self.pe_ms(e, M, L, b, u - 1)
        self.pe_ms(e, M, L, b, 4)
        e.wait_ge(*L.act("v_twice", b))
        for c in range(NC):
            mm = e.matmul(M.ps[6][:, 0:P], M.k("block_mean")[:, c * P:(c + 1) * P], self.v_twice[:, c * P:(c + 1) * P], start=(c == 0), stop=(c == NC - 1))
        mm.then_inc(*L.pe.mark("v_block"))
        for u in range(5):
            e.wait_ge(*L.act(f"rms_wide{0 if u == 0 else 1}", b))
            if u >= 2:
                e.wait_ge(*L.dve(f"normed{u - 2}", b))
            for c in range(NC):
                mm = e.transpose(M.ps[u % 2][:, c * P:(c + 1) * P], self.rms_wide[:, (u * NC + c) * P:(u * NC + c + 1) * P], M.k("ident"))
            mm.then_inc(*L.pe.mark(f"rms{u}"))
        e.wait_ge(*L.dve("kcw32", b))
        e.wait_ge(*L.dve("normed4", b))
        for c in range(NC):
            for m in range(A_H // 2):
                at = (c % 2 * 4 + m) * 64
                mm = e.matmul(M.ps[(2, 7)[c // 2]][:, at:at + 51], self.q[m][:, c * P:(c + 1) * P], self.kcw[:, 0:51], start=True, stop=True)
        mm.then_inc(*L.pe.mark("block_scores"))
        n = len(self.STEPS)
        for s in range(n + self.TURN):
            if s < n:
                c, m = self.STEPS[s]
                if s == 1:
                    e.wait_ge(*L.dve("gate_in", b))
                if s >= 2:
                    e.wait_ge(*L.dve(f"window{s - 2}", b))
                for o in range(2):
                    rows = slice(64 * o, 64 * o + 64)
                    mm = e.matmul(M.ps[2 * (s % 2) + o][:, 0:(c + 1) * P], self.q[m][rows, c * P:(c + 1) * P], self.k[rows, 0:(c + 1) * P],
                                  start=True, stop=True)
                mm.then_inc(*L.pe.mark(f"scores{s}"))
            if s == 3:
                e.wait_ge(*L.dve("comp_p", b))
                for c in range(NC):
                    mm = e.transpose(M.ps[7][:, c * P:(c + 1) * P], self.comp_p[:, c * P:(c + 1) * P], M.k("ident"))
                mm.then_inc(*L.pe.mark("comp_t"))
            if s >= self.TURN:
                r = s - self.TURN
                c, m = self.STEPS[r]
                if c != self.FIRST and m > 0:
                    self.pe_values(e, M, L, b, c + 1, m)
                e.wait_ge(*L.dve(f"mixed{r}", b))
                for o in range(2):
                    u = 2 * r + o
                    if u >= 3:
                        e.wait_ge(*L.act(f"turned{(u - 3) // 2}{'eo'[(u - 3) % 2]}", b))
                    if u == 2:
                        e.wait_ge(*L.act("comp_t", b))
                    for j in range(c + 1):
                        mm = e.transpose(M.ps[self.TURNED[u % 3]][:, j * P:(j + 1) * P], self.prob[r % self.RING][o][:, j * P:(j + 1) * P], M.k("ident"))
                    mm.then_inc(*L.pe.mark(f"turned{r}{'eo'[o]}"))
                if c != self.FIRST and m == 0:
                    self.pe_values(e, M, L, b, c + 1, m)
        for m in range(A_H // 2):
            self.pe_values(e, M, L, b, 0, m)
        e.wait_ge(*L.act("mix0", b))
        for m in range(4):
            mm = e.matmul(M.ps[0][:, :], M.w("a_w_group")[:, m * P:(m + 1) * P], self.mix[:, m, :], start=(m == 0), stop=(m == 3))
        mm.then_inc(*L.pe.mark("grouped"))
        e.wait_ge(*L.act("grouped", b))
        e.matmul(M.ps[1][:, :], M.w("a_w_out"), M.sq[:, :], start=True, stop=True).then_inc(*L.pe.mark("out"))

    def qc_sb(self, M):
        return M.h2[0:A_QC, :]

    def pe_ms(self, e, M, L, b, u):
        e.wait_ge(*L.act(f"square{u}", b))
        for c in range(NC):
            mm = e.matmul(M.ps[4][:, (u * NC + c) * 2:(u * NC + c) * 2 + 2], self.square(M, u)[:, c * P:(c + 1) * P], M.k("head2"), start=True, stop=True)
        mm.then_inc(*L.pe.mark(f"ms{u}"))

    def square(self, M, u):
        return (M.sq, M.sd)[u % 2][:, :]

    def pe_values(self, e, M, L, b, c, part):
        if part == 0:
            e.wait_ge(*L.act(f"turned{(self.FIRST - c + 1) * A_H // 2 - 1}o", b))
            if c == self.FIRST:
                e.wait_ge(*L.act("comp_t", b))
                e.wait_ge(*L.dve("v_block", b))
            else:
                e.wait_ge(*L.act(f"mix{c + 1}", b))
        products = [(j, o) for j in range(c + 1) for o in range(2)]
        n = len(products)
        for j, o in products[n * part // 4:n * (part + 1) // 4]:
            e.matmul(M.ps[6][:, :], (self.v_even, self.v_odd)[o][:, j * P:(j + 1) * P], self.prob_t[c % 2][:, j, o, :, :], start=(j == 0 and o == 0), stop=False,
                     skip_group_check=True)
        if part == 3:
            for m in range(4):
                mm = e.matmul(M.ps[6][:, m * P:(m + 1) * P], self.v_block[:, m * P:(m + 1) * P], self.comp_t[:, c * P:(c + 1) * P],
                              start=False, stop=(m == 3), skip_group_check=True)
            mm.then_inc(*L.pe.mark(f"values{c}"))

    def act(self, e, M, L, b):
        L.finished(e, b)
        e.wait_ge(*L.pe("qc", b))
        e.activation(self.qc_sb(M), M.ps[6][0:A_QC, :], ACT.Copy).then_inc(*L.act.mark("qc"))
        e.wait_ge(*L.pe("v", b))
        v = M.ps[7][:, :].rearrange("p (c d) -> p c d", d=P)
        for dst, lo in ((self.v_even, 0), (self.v_odd, A_D)):
            e.activation(dst.rearrange("p (c d) -> p c d", d=P)[:, :, lo:lo + A_D], v[:, :, lo:lo + A_D], ACT.Copy).then_inc(*L.act.mark(f"v{lo}"))
        e.activation(self.v_twice, M.ps[7][:, :], ACT.Copy).then_inc(*L.act.mark("v_twice"))
        for u in range(5):
            e.wait_ge(*L.dve(f"roped{u}", b))
            if u >= 2:
                e.wait_ge(*L.pe(f"ms{u - 2}", b))
            e.activation(self.square(M, u), (self.k, *self.q)[u], ACT.Square).then_inc(*L.act.mark(f"square{u}"))
        e.wait_ge(*L.pe("ms4", b))
        e.activation(self.rms, M.ps[4][:, 0:10 * NC], ACT.Sqrt, bias=M.k("eps6")).then_inc(*L.act.mark("root"))
        e.wait_ge(*L.dve("rms", b))
        for n, (lo, hi) in enumerate(((0, 1), (1, 5))):
            e.activation(self.rms_wide[:, lo * T:hi * T].rearrange("p (s d) -> p s d", d=A_D),
                         self.rms[:, lo * 8:hi * 8].unsqueeze(2).broadcast_to([P, 8 * (hi - lo), A_D]), ACT.Copy).then_inc(*L.act.mark(f"rms_wide{n}"))
        e.wait_ge(*L.dve("gate_in", b))
        e.activation(self.g, self.g, ACT.Exp, scale=-1.0).then_inc(*L.act.mark("gate_exp"))
        e.wait_ge(*L.dve("comp_c", b))
        e.activation(self.comp, self.comp, ACT.Exp, scale=self.SCALE).then_inc(*L.act.mark("comp_exp"))
        n = len(self.STEPS)
        for s in range(n + self.TURN):
            if s == self.TURN:
                e.wait_ge(*L.pe("comp_t", b))
                e.activation(self.comp_t, M.ps[7][:, :], ACT.Copy).then_inc(*L.act.mark("comp_t"))
            for o in range(2):
                if s < n:
                    c, m = self.STEPS[s]
                    st, W, bw = self.stat[s % self.RING], (c + 1) * P, min(c + 1, 2) * P
                    e.wait_ge(*L.dve(f"bias{s}", b))
                    pr, bd = self.prob[s % self.RING][o][:, 0:W], self.band[s % self.RING][:, o, 256 - bw:257]
                    e.activation(pr, pr, ACT.Exp, bias=st[:, 4 + 2 * o:5 + 2 * o], scale=self.SCALE, accum_out=st[:, 8 + 2 * o:9 + 2 * o])\
                        .then_inc(*L.act.mark(f"exp{s}{'eo'[o]}"))
                    e.activation(bd, bd, ACT.Exp, bias=st[:, 5 + 2 * o:6 + 2 * o], scale=self.SCALE, accum_out=st[:, 9 + 2 * o:10 + 2 * o])\
                        .then_inc(*L.act.mark(f"exp_window{s}{'eo'[o]}"))
                if s >= self.TURN:
                    r = s - self.TURN
                    c, m = self.STEPS[r]
                    e.wait_ge(*L.pe(f"turned{r}{'eo'[o]}", b))
                    if c + 2 <= self.FIRST and m == 0 and o == 0:
                        e.wait_ge(*L.pe(f"values{c + 2}", b))
                    e.activation(self.prob_t[c % 2][:, 0:c + 1, o, m, :], M.ps[self.TURNED[(2 * r + o) % 3]][:, 0:(c + 1) * P].rearrange("p (j q) -> p j q", q=P),
                                 ACT.Copy).then_inc(*L.act.mark(f"turned{r}{'eo'[o]}"))
                    if c != self.FIRST and m == A_H // 2 - 1 and o == 1:
                        self.act_mix(e, M, L, b, c + 1)
        self.act_mix(e, M, L, b, 0)
        e.wait_ge(*L.pe("grouped", b))
        e.activation(M.sq[:, :], M.ps[0][:, :], ACT.Copy).then_inc(*L.act.mark("grouped"))

    def act_mix(self, e, M, L, b, c):
        e.wait_ge(*L.pe(f"values{c}", b))
        e.activation(self.mix[:, :, c * P:(c + 1) * P], M.ps[6][:, :].rearrange("p (m q) -> p m q", q=P), ACT.Copy).then_inc(*L.act.mark(f"mix{c}"))

    def dve(self, e, M, L, b):
        L.finished(e, b)

        def step(name, ins, wait=True):
            ins.then_inc(*L.dve.mark(name))
            if wait:
                e.wait_ge(*L.dve(name, b))

        e.tensor_copy(M.h[:, :], M.hs[:, b, :]).then_inc(*L.dve.mark("norm"))
        step("sink", e.tensor_scalar(self.sink, M.w("a_sink"), 1.0 / self.SCALE, None, ALU.mult), False)
        halves = [(slice(64 * o, 64 * o + 64), 32 * o) for o in range(2)]
        for rows, at in halves:
            step(f"gate_w{at}", e.tensor_copy(self.kcw[rows, at + 16:at + 19], M.w("a_w_gate")[rows, :]), False)
        for u in range(5):
            t = self.t[u % 2]
            e.wait_ge(*L.pe(f"raw{u}", b))
            step(f"rope_a{u}", e.tensor_tensor(t, M.ps[2 * (u % 2)][:, :], M.k("rope_cos"), ALU.mult), False)
            step(f"rope_b{u}", e.tensor_tensor(self.t2, M.ps[2 * (u % 2) + 1][:, :], M.k("rope_sin"), ALU.mult))
            step(f"roped{u}", e.tensor_tensor((self.k, *self.q)[u], t, self.t2, ALU.add))
        e.wait_ge(*L.act("root", b))
        step("rms", e.reciprocal(self.rms, self.rms), False)
        for u in range(5):
            dst, g = (self.k, "a_gk") if u == 0 else (self.q[u - 1], "a_gq")
            e.wait_ge(*L.pe(f"rms{u}", b))
            step(f"normed{u}", e.scalar_tensor_tensor(dst, dst, M.w(g), M.ps[u % 2][:, :], ALU.mult, ALU.mult), u == 0)
            if u == 0:
                step("k_sum", e.tensor_reduce(self.k_sum, self.k.rearrange("p (n r) -> p n r", r=A_CR), AX, ALU.add))
                for rows, at in halves:
                    step(f"kcw{at}", e.tensor_scalar(self.kcw[rows, at:at + 16], self.k_sum[rows, :], 1.0 / A_CR, None, ALU.mult), False)
        e.wait_ge(*L.pe("v_block", b))
        step("v_block", e.tensor_tensor(self.v_block.rearrange("p (m f) -> p m f", f=P), M.k("head_of_block").rearrange("p (m f) -> p m f", f=P),
                                        M.ps[6][:, 0:P].unsqueeze(1).broadcast_to([P, 4, P]), ALU.mult), False)
        e.wait_ge(*L.pe("block_scores", b))
        seen = M.k("blocks_seen").rearrange("p (c n) -> p c n", n=A_NB)
        gate = M.w("a_b_gate").rearrange("p (h n) -> p h n", n=3)
        comp, gates = (a.rearrange("p (c h) n -> p c h n", h=A_H) for a in (self.comp, self.g))
        for c in range(NC):
            raw = M.ps[(2, 7)[c // 2]][:, c % 2 * 256:c % 2 * 256 + 256].rearrange("p (h n) -> p h n", n=32)
            step(f"comp_raw{c}", e.tensor_tensor(comp[:, c, :, 0:16], raw[:, :, 0:16], seen[:, c, :].unsqueeze(1).broadcast_to([P, A_H, A_NB]), ALU.add), False)
            step(f"gate_in{c}", e.tensor_tensor(gates[:, c, :, :], raw[:, :, 16:19], gate, ALU.add), False)
        step("gate_in", e.tensor_copy(self.comp.rearrange("p (c h) n -> p c h n", h=A_H)[:, :, :, 16],
                                      self.sink.unsqueeze(1).broadcast_to([P, NC, A_H])))
        wide = lambda a, n: a.unsqueeze(2).broadcast_to([P, NC * A_H, n])
        step("comp_max", e.tensor_reduce(self.cm, self.comp, AX, ALU.max))
        step("comp_c", e.tensor_tensor(self.comp, self.comp, wide(self.cm, 17), ALU.subtract), False)
        e.wait_ge(*L.act("gate_exp", b))
        step("gate_1", e.tensor_scalar(self.g, self.g, 1.0, None, ALU.add))
        step("gate_s", e.reciprocal(self.g, self.g))
        step("gate_sum", e.tensor_reduce(self.gs, self.g, AX, ALU.add))
        step("gate_clip", e.tensor_scalar(self.gs, self.gs, 1e-6, None, ALU.max))
        step("gate_inv", e.reciprocal(self.gs, self.gs))
        step("gates", e.tensor_tensor(self.g, self.g, wide(self.gs, 3), ALU.mult))
        e.wait_ge(*L.act("comp_exp", b))
        step("comp_sum", e.tensor_reduce(self.cd, self.comp, AX, ALU.add))
        step("comp_inv", e.reciprocal(self.cd, self.cd))
        step("comp_coef", e.tensor_tensor(self.cd, self.cd, self.g[:, :, 0], ALU.mult))
        step("comp_p", e.tensor_tensor(self.comp_p.rearrange("p (s n) -> p s n", n=A_NB), self.comp[:, :, 0:16], wide(self.cd, 16), ALU.mult), False)
        n = len(self.STEPS)
        for s in range(n + self.MIX):
            new, old = s < n, s >= self.MIX
            if new:
                c, m = self.STEPS[s]
                st, W, bw = self.stat[s % self.RING], (c + 1) * P, min(c + 1, 2) * P
                S, pr, bd = M.ps[2 * (s % 2):2 * (s % 2) + 2], self.prob[s % self.RING], self.band[s % self.RING]
            if old:
                r = s - self.MIX
                rc, rm = self.STEPS[r]
                rst, rW, rbw = self.stat[r % self.RING], (rc + 1) * P, min(rc + 1, 2) * P
                rpr, rbd = self.prob[r % self.RING], self.band[r % self.RING]

            def maximum(o):
                step(f"all{s}{'eo'[o]}", e.tensor_tensor_reduce(pr[o][:, 0:W], S[o][:, 0:W], M.k("causal")[:, T - W:T], 1.0, 3.0 * NEG,
                                                                ALU.add, ALU.max, st[:, 2 * o:2 * o + 1]), False)

            def window(o):
                h = 2 * m + o
                step(f"window{s}" if o else f"window{s}e", e.tensor_tensor_reduce(bd[:, o, 256 - bw:256], S[o][:, W - bw:W], M.k("band")[:, 256 - bw:256],
                                                                               1.0, self.sink[:, h:h + 1], ALU.add, ALU.max, st[:, 2 * o + 1:2 * o + 2]), False)

            def scaled(o):
                step(f"scaled{r}{'eo'[o]}", e.tensor_scalar(rpr[o][:, 0:rW], rpr[o][:, 0:rW], rst[:, 12 + 2 * o:13 + 2 * o], None, ALU.mult), False)

            if new:
                e.wait_ge(*L.pe(f"scores{s}", b))
                if s >= self.RING:
                    e.wait_ge(*L.pe(f"turned{s - self.RING}o", b))
                step(f"window_sink{s}", e.tensor_copy(bd[:, :, 256], self.sink[:, 2 * m:2 * m + 2]), False)
                maximum(0)
            if old:
                e.wait_ge(*L.act(f"exp_window{r}o", b))
                step(f"inv_sum{r}", e.reciprocal(rst[:, 12:16], rst[:, 8:12]), not new)
            if new:
                maximum(1)
            if old:
                e.wait_ge(*L.dve(f"inv_sum{r}", b))
                step(f"coef{r}", e.tensor_tensor(rst[:, 12:16].rearrange("p (o n) -> p o n", n=2), rst[:, 12:16].rearrange("p (o n) -> p o n", n=2),
                                                 self.g[:, rc * A_H + 2 * rm:rc * A_H + 2 * rm + 2, 1:3], ALU.mult), not new)
            if new:
                window(0)
            if old:
                e.wait_ge(*L.dve(f"coef{r}", b))
                scaled(0)
            if new:
                window(1)
            if old:
                scaled(1)
            if new:
                e.wait_ge(*L.dve(f"window{s}", b))
                step(f"bias{s}", e.tensor_scalar(st[:, 4:8], st[:, 0:4], -self.SCALE, None, ALU.mult), False)
            if old:
                e.wait_ge(*L.dve(f"scaled{r}o", b))
                for o in range(2):
                    step(f"mixed{r}" if o else f"mixed{r}e", e.scalar_tensor_tensor(rpr[o][:, rW - rbw:rW], rbd[:, o, 256 - rbw:256], rst[:, 13 + 2 * o:14 + 2 * o],
                                                                                 rpr[o][:, rW - rbw:rW], ALU.mult, ALU.add), False)
        e.wait_ge(*L.pe("out", b))
        step("residual", e.tensor_tensor(M.x[:, b, :], M.x[:, b, :], M.ps[1][:, :], ALU.add), False)

class BlockProject(Layer):
    turns = 1

    def __init__(self, M):
        self.rows = M.wide[:, 0:12, :].rearrange("p a t -> p (a t)").rearrange("p (c n) -> p c n", c=CHUNKS)

    def pe(self, e, M, L, b):
        for i in range(CHUNKS):
            if i >= 8:
                e.wait_ge(*L.dve(f"rows{i - 8}", 0))
            e.matmul(M.ps[i % 8][:, 0:3 * C], M.hs[:, i // NC, i % NC * P:(i % NC + 1) * P], M.w("b_w"), start=True, stop=True).then_inc(*L.pe.mark(f"qkv{i}"))

    def dve(self, e, M, L, b):
        for i in range(CHUNKS):
            e.wait_ge(*L.pe(f"qkv{i}", 0))
            e.tensor_tensor(self.rows[:, i, :], M.ps[i % 8][:, 0:3 * C], M.w("b_b"), ALU.add).then_inc(*L.dve.mark(f"rows{i}"))

    def sp(self, e, M, L, b):
        for i in range(B):
            e.wait_ge(*L.dve(f"rows{NC * i + NC - 1}", 0))
            e.dma_start(M.D["qkv"][i * T:(i + 1) * T, :].rearrange("(c p) n -> p c n", p=P), self.rows[:, NC * i:NC * (i + 1), :]).then_inc(*L.dma.mark(f"store{i}"))

class BlockAttend(Layer):
    prepares = True
    turns = 1

    def __init__(self, M):
        self.qkv = M.tiles[:, :, :].rearrange("p a t -> p (a t)").rearrange("p (t n) -> p t n", t=GROUP)
        join = lambda lo, hi: M.wide[:, lo:hi, :].rearrange("p a t -> p (a t)")
        self.prod = [join(0, 4), join(4, 8), M.big[:, 0:2048], M.big[:, 2048:4096]]
        self.s = join(8, 16).rearrange("p (q k h) -> p q k h", q=GROUP, k=GROUP)
        self.out = join(16, 20).rearrange("p (h q d) -> p h q d", q=GROUP, d=DH)
        self.mx, self.den = (M.small[:, 256 * i:256 * (i + 1)].rearrange("p (q h) -> p q h", h=H) for i in range(2))

    def before(self, e, M, which, sem):
        if which == "sp":
            e.dma_start(self.qkv, M.D["qkv"].rearrange("(p t) n -> p t n", t=GROUP)).then_inc(sem, 16)
        if which in ("pool", "dve"):
            e.wait_ge(sem, 16)

    def on_pool(self, i):
        return i % 8 in (1, 3, 4, 6, 7)

    def product(self, e, kind, i):
        q = i
        out = self.prod[i % 4]
        K, V = self.qkv[:, :, C:2 * C], self.qkv[:, :, 2 * C:3 * C]
        if kind == "score":
            return e.tensor_tensor(out.rearrange("p (k f) -> p k f", f=C), K, self.qkv[:, q, 0:C].unsqueeze(1).broadcast_to([P, GROUP, C]), ALU.mult)
        return e.tensor_tensor(out.rearrange("p (k h d) -> p k h d", h=H, d=DH), V.rearrange("p k (h d) -> p k h d", d=DH),
                               self.s[:, q, :, :].unsqueeze(3).broadcast_to([P, GROUP, H, DH]), ALU.mult)

    def pool(self, e, M, L, b):
        for kind in ("score", "value"):
            if kind == "value":
                e.wait_ge(*L.dve("prob", b))
            for i in range(GROUP):
                if self.on_pool(i):
                    if i >= 4:
                        e.wait_ge(*L.dve(f"{kind}_sum{i - 4}", b))
                    self.product(e, kind, i).then_inc(*L.pool.mark(f"{kind}{i}"))

    def dve(self, e, M, L, b):
        def step(name, ins):
            ins.then_inc(*L.dve.mark(name))
            e.wait_ge(*L.dve(name, b))

        def products(kind):
            for i in range(GROUP):
                if self.on_pool(i):
                    e.wait_ge(*L.pool(f"{kind}{i}", b))
                else:
                    step(f"{kind}{i}", self.product(e, kind, i))
                if kind == "score":
                    ins = e.tensor_reduce(self.s[:, i, :, :], self.prod[i % 4].rearrange("p (k h d) -> p k h d", h=H, d=DH), AX, ALU.add)
                else:
                    ins = e.tensor_reduce(self.out[:, :, i, :], self.prod[i % 4].rearrange("p (k h d) -> p h d k", h=H, d=DH), AX, ALU.add)
                ins.then_inc(*L.dve.mark(f"{kind}_sum{i}"))

        products("score")
        e.wait_ge(*L.dve(f"score_sum{GROUP - 1}", b))
        over_k = self.s.rearrange("p q k h -> p q h k")
        wide = lambda a: a.unsqueeze(2).broadcast_to([P, GROUP, GROUP, H])
        step("max", e.tensor_reduce(self.mx, over_k, AX, ALU.max))
        step("centred", e.tensor_tensor(self.s, self.s, wide(self.mx), ALU.subtract))
        e.wait_ge(*L.act("exp", b))
        step("sum", e.tensor_reduce(self.den, over_k, AX, ALU.add))
        step("inv", e.reciprocal(self.den, self.den))
        step("prob", e.tensor_tensor(self.s, self.s, wide(self.den), ALU.mult))
        products("value")

    def act(self, e, M, L, b):
        e.wait_ge(*L.dve("centred", b))
        flat = self.s.rearrange("p q k h -> p (q k h)")
        e.activation(flat, flat, ACT.Exp, scale=float(1.0 / np.sqrt(DH))).then_inc(*L.act.mark("exp"))

    def sp(self, e, M, L, b):
        e.wait_ge(*L.dve(f"value_sum{GROUP - 1}", b))
        rows = M.D["attended"].rearrange("(b h j) f -> b j h f", b=B, h=H)
        runs = T // GROUP
        for n in range(B):
            e.dma_start(rows[n], self.out[n * runs:(n + 1) * runs, :, :, :].rearrange("p h q d -> p h (q d)")).then_inc(*L.dma.mark(f"store{n}"))

class BlockMerge(Layer):
    turns = 1
    lanes = tuple(f"load{b}" for b in range(B))

    def __init__(self, M):
        self.rows = M.tiles[:, 0:B, :]

    def sp(self, e, M, L, b):
        for i in range(B):
            e.dma_start(self.rows[:, i, :].rearrange("p (c f) -> p c f", c=NC), M.D["attended"][i * T:(i + 1) * T, :].rearrange("(c p) f -> p c f", p=P))\
                .then_inc(*L.counters[f"load{i}"].mark(f"load{i}"))

    def pe(self, e, M, L, b):
        for i in range(B):
            e.wait_ge(*L.counters[f"load{i}"].end())
            for c in range(NC):
                mm = e.transpose(M.ps[i][:, c * P:(c + 1) * P], self.rows[:, i, c * P:(c + 1) * P], M.k("ident"))
            mm.then_inc(*L.pe.mark(f"turned{i}"))

    def dve(self, e, M, L, b):
        for i in range(B):
            e.wait_ge(*L.pe(f"turned{i}", 0))
            e.tensor_tensor(M.x[:, i, :], M.x[:, i, :], M.ps[i][:, :], ALU.add).then_inc(*L.dve.mark(f"residual{i}"))

class Memory:
    def __init__(self, nc, ctx, const_cols, param_cols):
        def sb(name, shape, dt=F32):
            return ctx.enter_context(nc.sbuf_tensor(name, shape, dt))

        self.const_cols, self.param_cols = const_cols, param_cols
        self.consts = sb("consts", [P, max(b for a, b in const_cols.values())])
        self.params = sb("params", [P, max(b for a, b in param_cols.values())])
        self.x = sb("x", [P, B, T])
        self.h = sb("h", [P, T])
        self.hs = sb("hs", [P, B, T])
        self.norm_cols = sb("norm_cols", [P, 2 * NC * B])
        self.h2 = sb("h2", [P, T])
        self.xc, self.sq, self.sd = (sb(n, [P, T]) for n in ("xc", "sq", "sd"))
        self.tiles = sb("tiles", [P, 12, T])
        self.wide = sb("wide", [P, 20, T])
        self.big = sb("big", [P, 9 * T])
        self.small = sb("small", [P, 640])
        self.expert_gate = sb("expert_gate", [P, E, F])
        self.expert_up = sb("expert_up", [P, E, F])
        self.expert_out = sb("expert_out", [P, E, NF, C])
        self.pos = sb("pos", [P, B * NC], I32)
        self.slot_index = sb("slot_index", [P, 2 * TOP * CHUNKS], I32)
        self.ps = [ctx.enter_context(nc.psum_tensor(f"bank{i}", [P, T], F32)) for i in range(8)]

    def k(self, name):
        a, b = self.const_cols[name]
        return self.consts[:, a:b]

    def w(self, name, rows=P):
        a, b = self.param_cols[name]
        return self.params[0:rows, a:b]

    def tile(self, i):
        return self.tiles[:, i, :]

KINDS = {1: [Norm, TokenAttention], 2: [Norm, Route, Experts], 3: [Norm, Flow, FlowNorm, FlowFeed, FlowOut], 4: [Norm, Route, Experts], 5: [Norm, TimeMix], 6: [Norm, DepthPick, DepthBlock],
         7: [Norm, BlockProject, BlockAttend, BlockMerge], 8: [Norm, DepthPick, DepthBlock]}
LAYERS = [1, 2, 3, 4, 5, 6, 7, 8]

def program(nc, D, const_cols, param_cols, plan=None):
    with ExitStack() as ctx:
        shared = []

        def sem(name):
            if plan is None and shared:
                return shared[0]
            shared.append(ctx.enter_context(nc.semaphore(name)))
            return shared[-1]

        M = Memory(nc, ctx, const_cols, param_cols)
        M.D = D
        loaded, experts_loaded, stored = sem("loaded"), sem("experts_loaded"), sem("stored")
        M.slots_cleared = sem("slots_cleared")
        layers, prepared = [], {}
        for n in LAYERS:
            for i, cls in enumerate(KINDS[n]):
                name = f"l{n}_{i}"
                layers.append((cls(M), Stage(name, sem, plan, cls.turns, cls.lanes)))
                prepared[name] = sem(f"{name}_prepared") if cls.prepares else None
        block = ctx.enter_context(nc.Block())

        def run(e, which):
            before = None
            for layer, L in layers:
                work = layer.parts()[which]
                if before is not None:
                    before.finished(e)
                counter = L.counters["dma" if which == "sp" else which]
                if counter.order is None or counter.order:
                    e.sem_inc(counter.sem, 1)
                layer.before(e, M, which, prepared[L.name])
                if work is not None:
                    if layer.needs_experts and which == "pe":
                        e.wait_ge(experts_loaded, 3 * 16)
                    if layer.turns == 1:
                        work(e, M, L, 0)
                    else:
                        with e.Fori(0, layer.turns) as b:
                            work(e, M, L, b)
                before = L
            return before

        @block.tensor
        def _(pe):
            pe.wait_ge(loaded, 4 * 16)
            run(pe, "pe")

        @block.scalar
        def _(act):
            act.wait_ge(loaded, 4 * 16)
            run(act, "act")

        @block.vector
        def _(dve):
            dve.wait_ge(loaded, 4 * 16)
            run(dve, "dve")

        @block.gpsimd
        def _(pool):
            pool.wait_ge(loaded, 4 * 16)
            run(pool, "pool")

        @block.sync
        def _(sp):
            sp.dma_start(M.x[:, :, :], D["x"]).then_inc(loaded, 16)
            sp.dma_start(M.consts[:, :], D["consts"]).then_inc(loaded, 16)
            sp.dma_start(M.params[:, :], D["params"]).then_inc(loaded, 16)
            sp.dma_start(M.pos[:, :], D["pos"]).then_inc(loaded, 16)
            zeros = M.k("causal")[:, 0:2 * P]
            sp.wait_ge(loaded, 4 * 16)
            sp.dma_start(D["slots"][0:E * HOLD, :].rearrange("(p n r) c -> p n (r c)", p=P, r=2), zeros.unsqueeze(1).broadcast_to([P, HOLD * E // P // 2, 2 * C])).then_inc(M.slots_cleared, 16)
            sp.dma_start(M.expert_gate[:, :, :], D["wi_gate"]).then_inc(experts_loaded, 16)
            sp.dma_start(M.expert_up[:, :, :], D["wi_up"]).then_inc(experts_loaded, 16)
            sp.dma_start(M.expert_out[:, :, :, :], D["wo"]).then_inc(experts_loaded, 16)
            last = run(sp, "sp")
            last.finished(sp)
            sp.dma_start(D["out"], M.x[:, :, :]).then_inc(stored, 16)
            sp.wait_ge(stored, 16)
            sp.wait_ge(experts_loaded, 3 * 16)
        return {L.name: {k: c.seen for k, c in L.counters.items()} for _, L in layers}

def kernel(**inputs):
    import concourse.bacc as bacc
    from concourse.bass_utils import run_bass_kernel_spmd

    a = {k: np.asarray(v) for k, v in inputs.items()}

    def pack(named):
        cols, at = {}, 0
        for n, m in named.items():
            cols[n] = (at, at + m.shape[1])
            at += m.shape[1]
        return np.ascontiguousarray(np.concatenate(list(named.values()), axis=1)), cols

    consts, const_cols = pack(constants())
    params, param_cols = pack(parameters(a))
    lay = lambda m: np.ascontiguousarray(m)
    arrays = {
        "x": lay(a["L0_attn_a_h"].transpose(2, 0, 1)),
        "consts": consts,
        "params": params,
        "pos": lay(a["L1_ffn_position_ids"].reshape(B, NC, P).transpose(2, 0, 1).reshape(P, B * NC)),
        "wi_gate": lay(a["L0_ffn_wi_gate"].transpose(2, 0, 1)),
        "wi_up": lay(a["L0_ffn_wi_up"].transpose(2, 0, 1)),
        "wo": lay(a["L0_ffn_wo"].reshape(E, C, NF, P).transpose(3, 0, 2, 1)),
        "mask": lay(a["L1_ffn_attention_mask"].reshape(B, NC, P, T).transpose(2, 0, 1, 3)),
    }

    def declare(nc):
        D = {n: nc.dram_tensor(f"in_{n}", m.shape, mybir.dt.from_np(m.dtype), kind="ExternalInput").ap() for n, m in arrays.items()}
        D["out"] = nc.dram_tensor("out_x", (P, B, T), F32, kind="ExternalOutput").ap()
        D["slots"] = nc.dram_tensor("expert_slots", (E * HOLD + TOP * B * T, C), F32).ap()
        D["slots_out"] = nc.dram_tensor("expert_slots_out", (E * HOLD, C), F32).ap()
        D["qkv"] = nc.dram_tensor("qkv_tokens", (B * T, 3 * C), F32).ap()
        D["attended"] = nc.dram_tensor("attended_tokens", (B * T, C), F32).ap()
        return D

    draft = bacc.Bacc("TRN2", target_bir_lowering=False, num_devices=1)
    plan = program(draft, declare(draft), const_cols, param_cols)
    nc = bacc.Bacc("TRN2", target_bir_lowering=False, num_devices=1)
    assert program(nc, declare(nc), const_cols, param_cols, plan) == plan
    r = run_bass_kernel_spmd(nc, [{f"in_{n}": m for n, m in arrays.items()}], core_ids=[0])
    return lay(r.results[0]["out_x"].transpose(1, 2, 0))
```
